# Optimizing a Trainium2 kernel written in Bass

```python
import numpy as np
import jax
import jax.numpy as jnp

def _softmax(x, axis=-1):
    return jax.nn.softmax(x, axis=axis)

def _gelu(x):
    return jax.nn.gelu(x, approximate=True)

def _silu(x):
    return jax.nn.silu(x)

def _sigmoid(x):
    return jax.nn.sigmoid(x)

def _layernorm(x, axis=-1, eps=1e-05):
    m = jnp.mean(x, axis=axis, keepdims=True)
    v = jnp.var(x, axis=axis, keepdims=True)
    return (x - m) / jnp.sqrt(v + eps)

def _scatter_add(tgt, idx, src, axis=0):
    return tgt.at[idx].add(src)

def _segment_sum(src, seg, n):
    return jax.ops.segment_sum(src, seg, n)
kernel_name = 'mk_adaln_d4_jaxref_r8_d2bd6e'

def setup_inputs(seed: int=0):
    np.random.seed(seed)
    _w = jnp.asarray

    def _L0_attn_setup():
        import jax, jax.numpy as jnp
        import numpy as np
        import math
        EMBED_DIM = 128
        NUM_HEADS = 8
        DEPTH = 12
        HEAD_DIM = EMBED_DIM // NUM_HEADS // 2
        LAMBDA_INIT = 0.8 - 0.6 * math.exp(-0.3 * DEPTH)
        EPS = 1e-08

        def _rotary(t):
            d = t.shape[-1]
            s = t.shape[1]
            inv_freq = 1.0 / 10000.0 ** (jnp.arange(0, d, 2, dtype=jnp.float32) / d)
            pos = jnp.arange(s, dtype=jnp.float32)
            freqs = pos[:, None] * inv_freq[None, :]
            freqs = jnp.repeat(freqs, 2, axis=-1)
            cos = jnp.cos(freqs)[None, :, None, :]
            sin = jnp.sin(freqs)[None, :, None, :]
            x = t.reshape(t.shape[:-1] + (d // 2, 2))
            x1, x2 = (x[..., 0], x[..., 1])
            rot = jnp.stack([-x2, x1], axis=-1).reshape(t.shape)
            return t * cos + rot * sin

        def _sdpa_over_heads(q, k, v):
            scores = jnp.einsum('bsnd,bsmd->bsnm', q, k) / HEAD_DIM ** 0.25
            aw = jax.nn.softmax(scores, axis=-1)
            return jnp.einsum('bsnm,bsme->bsne', aw, v)
        key = jax.random.key(seed)
        ks = jax.random.split(key, 10)
        E, H, D = (EMBED_DIM, NUM_HEADS, HEAD_DIM)
        scale = 1.0 / np.sqrt(E)
        return {'x': jax.random.normal(ks[0], (4, 512, E), jnp.float32), 'Wq': jax.random.normal(ks[1], (E, E), jnp.float32) * scale, 'Wk': jax.random.normal(ks[2], (E, E), jnp.float32) * scale, 'Wv': jax.random.normal(ks[3], (E, E), jnp.float32) * scale, 'Wo': jax.random.normal(ks[4], (E, E), jnp.float32) * scale, 'lambda_q1': jax.random.normal(ks[5], (D,), jnp.float32) * 0.1, 'lambda_k1': jax.random.normal(ks[6], (D,), jnp.float32) * 0.1, 'lambda_q2': jax.random.normal(ks[7], (D,), jnp.float32) * 0.1, 'lambda_k2': jax.random.normal(ks[8], (D,), jnp.float32) * 0.1, 'ln_w': 1.0 + 0.1 * jax.random.normal(ks[9], (2 * D,), jnp.float32), 'ln_b': jnp.zeros((2 * D,), jnp.float32)}
    _L0_attn_in = _L0_attn_setup()

    def _L0_ffn_setup():
        import math
        import jax, jax.numpy as jnp
        import numpy as np
        E = 8
        H = 128
        HP = 128
        SPARSITY = 8
        N_ROTATE = 64
        ROPE_BASE = 10000.0

        def _rope(x, pos):
            half = N_ROTATE // 2
            inv_freq = 1.0 / ROPE_BASE ** (jnp.arange(half, dtype=jnp.float32) * 2.0 / N_ROTATE)
            ang = pos.astype(jnp.float32)[..., None] * inv_freq
            sin, cos = (jnp.sin(ang), jnp.cos(ang))
            x1, x2 = (x[..., :half], x[..., half:])
            return jnp.concatenate([x1 * cos - x2 * sin, x2 * cos + x1 * sin], axis=-1)
        key = jax.random.key(seed)
        k1, k2, k3, k4 = jax.random.split(key, 4)
        B, T = (4, 1024)
        X = jax.random.normal(k1, (B, T, H), dtype=jnp.float32)
        Wr = jax.random.uniform(k2, (E, H), minval=-1 / math.sqrt(H), maxval=1 / math.sqrt(H), dtype=jnp.float32)
        bq = 1 / math.sqrt(3 * HP)
        Wqkv = jax.random.uniform(k3, (E, H, 3 * HP), minval=-bq, maxval=bq, dtype=jnp.float32)
        bo = 1 / math.sqrt(H * E)
        Wo = jax.random.uniform(k4, (E, HP, H), minval=-bo, maxval=bo, dtype=jnp.float32)
        return {'X': X, 'Wr': Wr, 'Wqkv': Wqkv, 'Wo': Wo}
    _L0_ffn_in = _L0_ffn_setup()
    _L0_c = _w((lambda *s: np.random.randn(*s).astype(np.float32) * 0.05)(8, 128))
    _L0_wmod = _w((lambda *s: np.random.randn(*s).astype(np.float32) * 0.05)(128, 6 * 128) * 128 ** (-0.5))

    def _L1_attn_setup():
        import jax, jax.numpy as jnp
        import numpy as np
        import math
        TOK_DIM = 64
        POS_DIM = 64
        D_MODEL = 128
        N_HEADS = 16
        HEAD_DIM = 64
        NUM_KV_HEADS = 4
        INNER = N_HEADS * HEAD_DIM
        KV_INNER = NUM_KV_HEADS * HEAD_DIM
        KV_REPEAT = N_HEADS // NUM_KV_HEADS
        B, T = (2, 256)
        key = jax.random.key(seed)
        ks = jax.random.split(key, 7)
        x = jax.random.normal(ks[0], (B, T, D_MODEL), dtype=jnp.float32)
        Wq = jax.random.normal(ks[1], (INNER, POS_DIM), dtype=jnp.float32) * 0.02
        Wk = jax.random.normal(ks[2], (KV_INNER, POS_DIM), dtype=jnp.float32) * 0.02
        Wv = jax.random.normal(ks[3], (KV_INNER, TOK_DIM), dtype=jnp.float32) * 0.02
        Wo = jax.random.normal(ks[4], (D_MODEL, INNER), dtype=jnp.float32) * 0.02
        q_phase_angle = jax.random.normal(ks[5], (N_HEADS,), dtype=jnp.float32) * 0.1
        alibi_log_slopes = jnp.full((N_HEADS,), math.log(math.log(10.0)), dtype=jnp.float32)
        return {'x': x, 'Wq': Wq, 'Wk': Wk, 'Wv': Wv, 'Wo': Wo, 'q_phase_angle': q_phase_angle, 'alibi_log_slopes': alibi_log_slopes}
    _L1_attn_in = _L1_attn_setup()

    def _L1_ffn_setup():
        import jax, jax.numpy as jnp
        import numpy as np
        B, S, H = (4, 256, 128)
        E = 8
        GS = 2
        NG = E // GS
        F = int(H * 4 * (2.0 / 3.0))
        key = jax.random.key(seed)
        ks = jax.random.split(key, 7)
        sc_h = 1.0 / np.sqrt(H)
        sc_f = 1.0 / np.sqrt(F)
        return {'x': jax.random.normal(ks[0], (B, S, H), dtype=jnp.float32), 'Wr': jax.random.normal(ks[1], (H, E), dtype=jnp.float32) * sc_h, 'br': jnp.zeros((E,), dtype=jnp.float32), 'W_up': jax.random.normal(ks[2], (NG, H, F), dtype=jnp.float32) * sc_h, 'b_up': jax.random.normal(ks[3], (NG, F), dtype=jnp.float32) * 0.01, 'W_down': jax.random.normal(ks[4], (E, F, H), dtype=jnp.float32) * sc_f, 'b_down': jax.random.normal(ks[5], (E, H), dtype=jnp.float32) * 0.01}
    _L1_ffn_in = _L1_ffn_setup()
    _L1_c = _w((lambda *s: np.random.randn(*s).astype(np.float32) * 0.05)(8, 128))
    _L1_wmod = _w((lambda *s: np.random.randn(*s).astype(np.float32) * 0.05)(128, 6 * 128) * 128 ** (-0.5))

    def _L2_attn_setup():
        import jax, jax.numpy as jnp
        import numpy as np
        B, S, D = (4, 256, 128)
        H = 16
        HS = D // H
        SCALE = HS ** 0.5
        key = jax.random.key(seed)
        ks = jax.random.split(key, 9)
        std = 1.0 / np.sqrt(D)

        def lin(kw, kb, fan_in, fan_out):
            w = jax.random.uniform(kw, (fan_in, fan_out), minval=-std, maxval=std, dtype=jnp.float32)
            b = jax.random.uniform(kb, (fan_out,), minval=-std, maxval=std, dtype=jnp.float32)
            return (w, b)
        Wq, bq = lin(ks[0], ks[1], D, D)
        Wk, bk = lin(ks[2], ks[3], D, D)
        Wv, bv = lin(ks[4], ks[5], D, D)
        Wm, bm = lin(ks[6], ks[7], D, D)
        x = jax.random.normal(ks[8], (B, S, D), dtype=jnp.float32)
        return {'x': x, 'Wq': Wq, 'bq': bq, 'Wk': Wk, 'bk': bk, 'Wv': Wv, 'bv': bv, 'Wm': Wm, 'bm': bm}
    _L2_attn_in = _L2_attn_setup()

    def _L2_ffn_setup():
        import jax, jax.numpy as jnp
        import numpy as np
        D = 128
        H = 512
        E = 8
        B = 2
        T = 256
        LN_EPS = 1e-05

        def _layer_norm(r, gamma, beta):
            mu = jnp.mean(r, axis=-1, keepdims=True)
            var = jnp.mean(jnp.square(r - mu), axis=-1, keepdims=True)
            return (r - mu) * jax.lax.rsqrt(var + LN_EPS) * gamma + beta
        key = jax.random.key(seed)
        ks = jax.random.split(key, 9)
        s_in = 1.0 / np.sqrt(D)
        s_hid = 1.0 / np.sqrt(H)
        x = jax.random.normal(ks[0], (B, T, D), dtype=jnp.float32)
        Wg = jax.random.uniform(ks[1], (D, E), jnp.float32, -s_in, s_in)
        bg = jax.random.uniform(ks[2], (E,), jnp.float32, -s_in, s_in)
        W1 = jax.random.uniform(ks[3], (E, D, H), jnp.float32, -s_in, s_in)
        b1 = jax.random.uniform(ks[4], (E, H), jnp.float32, -s_in, s_in)
        W2 = jax.random.uniform(ks[5], (E, H, D), jnp.float32, -s_hid, s_hid)
        b2 = jax.random.uniform(ks[6], (E, D), jnp.float32, -s_hid, s_hid)
        gamma = jnp.ones((D,), jnp.float32)
        beta = jnp.zeros((D,), jnp.float32)
        return {'x': x, 'Wg': Wg, 'bg': bg, 'W1': W1, 'b1': b1, 'W2': W2, 'b2': b2, 'gamma': gamma, 'beta': beta}
    _L2_ffn_in = _L2_ffn_setup()
    _L2_c = _w((lambda *s: np.random.randn(*s).astype(np.float32) * 0.05)(8, 128))
    _L2_wmod = _w((lambda *s: np.random.randn(*s).astype(np.float32) * 0.05)(128, 6 * 128) * 128 ** (-0.5))

    def _L3_attn_setup():
        import jax, jax.numpy as jnp
        import numpy as np
        B, S, D, H = (2, 256, 128, 16)
        HD = D // H
        key = jax.random.key(seed)
        k1, k2, k3 = jax.random.split(key, 3)
        x = jax.random.normal(k1, (B, S, D), dtype=jnp.float32)
        c_attn_kernel = 0.02 * jax.random.normal(k2, (3 * D, D), dtype=jnp.float32)
        c_attn_bias = jnp.zeros((3 * D,), dtype=jnp.float32)
        c_proj_kernel = 0.02 * jax.random.normal(k3, (D, D), dtype=jnp.float32)
        c_proj_bias = jnp.zeros((D,), dtype=jnp.float32)
        return {'hidden_states': x, 'c_attn_kernel': c_attn_kernel, 'c_attn_bias': c_attn_bias, 'c_proj_kernel': c_proj_kernel, 'c_proj_bias': c_proj_bias}
    _L3_attn_in = _L3_attn_setup()

    def _L3_ffn_setup():
        import jax, jax.numpy as jnp
        import numpy as np
        DIM = 128
        EXPERT_DIM = 64
        N_EXPERTS = 16
        TOPK = 2
        SHARED_HIDDEN = EXPERT_DIM * TOPK
        B, T = (4, 128)

        def _moe_forward(x, router_w, router_bias, up_proj, gate_proj, down_proj, sh_gate, sh_up, sh_down):
            Bb, Tt, D = x.shape
            flat = x.reshape(Bb * Tt, D)
            N = flat.shape[0]
            logits = flat @ router_w.T
            topk_scores, topk_idx = jax.lax.top_k(logits + router_bias, TOPK)
            topk_scores = jax.nn.softmax(topk_scores, axis=-1)
            combine = jnp.zeros((N, N_EXPERTS), flat.dtype)
            combine = combine.at[jnp.arange(N)[:, None], topk_idx].add(topk_scores)
            up_all = jnp.einsum('nd,kde->nke', flat, up_proj)
            gate_all = jnp.einsum('nd,kde->nke', flat, gate_proj)
            hidden = jax.nn.silu(gate_all) * up_all
            down_all = jnp.einsum('nke,ked->nkd', hidden, down_proj)
            out = jnp.einsum('nk,nkd->nd', combine, down_all)
            sh_hidden = jax.nn.silu(flat @ sh_gate.T) * (flat @ sh_up.T)
            out = out + sh_hidden @ sh_down.T
            return out.reshape(Bb, Tt, D)
        key = jax.random.key(seed)
        ks = jax.random.split(key, 9)
        std = 0.02
        return {'x': jax.random.normal(ks[0], (B, T, DIM), jnp.float32), 'router_w': jax.random.normal(ks[1], (N_EXPERTS, DIM), jnp.float32) * std, 'router_bias': jnp.zeros((N_EXPERTS,), jnp.float32), 'up_proj': jax.random.normal(ks[2], (N_EXPERTS, DIM, EXPERT_DIM), jnp.float32) * std, 'gate_proj': jax.random.normal(ks[3], (N_EXPERTS, DIM, EXPERT_DIM), jnp.float32) * std, 'down_proj': jax.random.normal(ks[4], (N_EXPERTS, EXPERT_DIM, DIM), jnp.float32) * std, 'sh_gate': jax.random.normal(ks[5], (SHARED_HIDDEN, DIM), jnp.float32) * std, 'sh_up': jax.random.normal(ks[6], (SHARED_HIDDEN, DIM), jnp.float32) * std, 'sh_down': jax.random.normal(ks[7], (DIM, SHARED_HIDDEN), jnp.float32) * std}
    _L3_ffn_in = _L3_ffn_setup()
    _L3_c = _w((lambda *s: np.random.randn(*s).astype(np.float32) * 0.05)(8, 128))
    _L3_wmod = _w((lambda *s: np.random.randn(*s).astype(np.float32) * 0.05)(128, 6 * 128) * 128 ** (-0.5))
    _d = {'L0_attn_x': _L0_attn_in['x'], 'L0_attn_Wq': _L0_attn_in['Wq'], 'L0_attn_Wk': _L0_attn_in['Wk'], 'L0_attn_Wv': _L0_attn_in['Wv'], 'L0_attn_Wo': _L0_attn_in['Wo'], 'L0_attn_lambda_q1': _L0_attn_in['lambda_q1'], 'L0_attn_lambda_k1': _L0_attn_in['lambda_k1'], 'L0_attn_lambda_q2': _L0_attn_in['lambda_q2'], 'L0_attn_lambda_k2': _L0_attn_in['lambda_k2'], 'L0_attn_ln_w': _L0_attn_in['ln_w'], 'L0_attn_ln_b': _L0_attn_in['ln_b'], 'L0_ffn_Wr': _L0_ffn_in['Wr'], 'L0_ffn_Wqkv': _L0_ffn_in['Wqkv'], 'L0_ffn_Wo': _L0_ffn_in['Wo'], 'L0_c': _L0_c, 'L0_wmod': _L0_wmod, 'L1_attn_Wq': _L1_attn_in['Wq'], 'L1_attn_Wk': _L1_attn_in['Wk'], 'L1_attn_Wv': _L1_attn_in['Wv'], 'L1_attn_Wo': _L1_attn_in['Wo'], 'L1_attn_q_phase_angle': _L1_attn_in['q_phase_angle'], 'L1_attn_alibi_log_slopes': _L1_attn_in['alibi_log_slopes'], 'L1_ffn_Wr': _L1_ffn_in['Wr'], 'L1_ffn_br': _L1_ffn_in['br'], 'L1_ffn_W_up': _L1_ffn_in['W_up'], 'L1_ffn_b_up': _L1_ffn_in['b_up'], 'L1_ffn_W_down': _L1_ffn_in['W_down'], 'L1_ffn_b_down': _L1_ffn_in['b_down'], 'L1_c': _L1_c, 'L1_wmod': _L1_wmod, 'L2_attn_Wq': _L2_attn_in['Wq'], 'L2_attn_bq': _L2_attn_in['bq'], 'L2_attn_Wk': _L2_attn_in['Wk'], 'L2_attn_bk': _L2_attn_in['bk'], 'L2_attn_Wv': _L2_attn_in['Wv'], 'L2_attn_bv': _L2_attn_in['bv'], 'L2_attn_Wm': _L2_attn_in['Wm'], 'L2_attn_bm': _L2_attn_in['bm'], 'L2_ffn_Wg': _L2_ffn_in['Wg'], 'L2_ffn_bg': _L2_ffn_in['bg'], 'L2_ffn_W1': _L2_ffn_in['W1'], 'L2_ffn_b1': _L2_ffn_in['b1'], 'L2_ffn_W2': _L2_ffn_in['W2'], 'L2_ffn_b2': _L2_ffn_in['b2'], 'L2_ffn_gamma': _L2_ffn_in['gamma'], 'L2_ffn_beta': _L2_ffn_in['beta'], 'L2_c': _L2_c, 'L2_wmod': _L2_wmod, 'L3_attn_c_attn_kernel': _L3_attn_in['c_attn_kernel'], 'L3_attn_c_attn_bias': _L3_attn_in['c_attn_bias'], 'L3_attn_c_proj_kernel': _L3_attn_in['c_proj_kernel'], 'L3_attn_c_proj_bias': _L3_attn_in['c_proj_bias'], 'L3_ffn_router_w': _L3_ffn_in['router_w'], 'L3_ffn_router_bias': _L3_ffn_in['router_bias'], 'L3_ffn_up_proj': _L3_ffn_in['up_proj'], 'L3_ffn_gate_proj': _L3_ffn_in['gate_proj'], 'L3_ffn_down_proj': _L3_ffn_in['down_proj'], 'L3_ffn_sh_gate': _L3_ffn_in['sh_gate'], 'L3_ffn_sh_up': _L3_ffn_in['sh_up'], 'L3_ffn_sh_down': _L3_ffn_in['sh_down'], 'L3_c': _L3_c, 'L3_wmod': _L3_wmod}
    _x0 = _d['L0_attn_x']
    _d['L0_attn_x'] = jax.random.normal(jax.random.fold_in(jax.random.key(seed), 1), (8, 512, 128), dtype=_x0.dtype)
    del _x0
    return _d

def reference(L0_attn_x, L0_attn_Wq, L0_attn_Wk, L0_attn_Wv, L0_attn_Wo, L0_attn_lambda_q1, L0_attn_lambda_k1, L0_attn_lambda_q2, L0_attn_lambda_k2, L0_attn_ln_w, L0_attn_ln_b, L0_ffn_Wr, L0_ffn_Wqkv, L0_ffn_Wo, L0_c, L0_wmod, L1_attn_Wq, L1_attn_Wk, L1_attn_Wv, L1_attn_Wo, L1_attn_q_phase_angle, L1_attn_alibi_log_slopes, L1_ffn_Wr, L1_ffn_br, L1_ffn_W_up, L1_ffn_b_up, L1_ffn_W_down, L1_ffn_b_down, L1_c, L1_wmod, L2_attn_Wq, L2_attn_bq, L2_attn_Wk, L2_attn_bk, L2_attn_Wv, L2_attn_bv, L2_attn_Wm, L2_attn_bm, L2_ffn_Wg, L2_ffn_bg, L2_ffn_W1, L2_ffn_b1, L2_ffn_W2, L2_ffn_b2, L2_ffn_gamma, L2_ffn_beta, L2_c, L2_wmod, L3_attn_c_attn_kernel, L3_attn_c_attn_bias, L3_attn_c_proj_kernel, L3_attn_c_proj_bias, L3_ffn_router_w, L3_ffn_router_bias, L3_ffn_up_proj, L3_ffn_gate_proj, L3_ffn_down_proj, L3_ffn_sh_gate, L3_ffn_sh_up, L3_ffn_sh_down, L3_c, L3_wmod):

    def _L0_attn_ref(x, Wq, Wk, Wv, Wo, lambda_q1, lambda_k1, lambda_q2, lambda_k2, ln_w, ln_b):
        import jax, jax.numpy as jnp
        import numpy as np
        import math
        EMBED_DIM = 128
        NUM_HEADS = 8
        DEPTH = 12
        HEAD_DIM = EMBED_DIM // NUM_HEADS // 2
        LAMBDA_INIT = 0.8 - 0.6 * math.exp(-0.3 * DEPTH)
        EPS = 1e-08

        def _rotary(t):
            d = t.shape[-1]
            s = t.shape[1]
            inv_freq = 1.0 / 10000.0 ** (jnp.arange(0, d, 2, dtype=jnp.float32) / d)
            pos = jnp.arange(s, dtype=jnp.float32)
            freqs = pos[:, None] * inv_freq[None, :]
            freqs = jnp.repeat(freqs, 2, axis=-1)
            cos = jnp.cos(freqs)[None, :, None, :]
            sin = jnp.sin(freqs)[None, :, None, :]
            x = t.reshape(t.shape[:-1] + (d // 2, 2))
            x1, x2 = (x[..., 0], x[..., 1])
            rot = jnp.stack([-x2, x1], axis=-1).reshape(t.shape)
            return t * cos + rot * sin

        def _sdpa_over_heads(q, k, v):
            scores = jnp.einsum('bsnd,bsmd->bsnm', q, k) / HEAD_DIM ** 0.25
            aw = jax.nn.softmax(scores, axis=-1)
            return jnp.einsum('bsnm,bsme->bsne', aw, v)
        b, s, E = x.shape
        H, D = (NUM_HEADS, HEAD_DIM)
        q = (x @ Wq).reshape(b, s, 2 * H, D)
        k = (x @ Wk).reshape(b, s, 2 * H, D)
        v = (x @ Wv).reshape(b, s, H, 2 * D)
        q = _rotary(q)
        k = _rotary(k)
        q = q.reshape(b, s, H, 2, D)
        k = k.reshape(b, s, H, 2, D)
        q1, q2 = (q[:, :, :, 0], q[:, :, :, 1])
        k1, k2 = (k[:, :, :, 0], k[:, :, :, 1])
        attn1 = _sdpa_over_heads(q1, k1, v)
        attn2 = _sdpa_over_heads(q2, k2, v)
        lam = jnp.exp(jnp.sum(lambda_q1 * lambda_k1)) - jnp.exp(jnp.sum(lambda_q2 * lambda_k2)) + LAMBDA_INIT
        a = attn1 - lam * attn2
        rms = jax.lax.rsqrt(jnp.mean(a * a, axis=-1, keepdims=True) + EPS)
        a = a * rms * ln_w + ln_b
        a = a * (1.0 - LAMBDA_INIT)
        return a.reshape(b, s, E) @ Wo

    def _L0_ffn_ref(X, Wr, Wqkv, Wo):
        import math
        import jax, jax.numpy as jnp
        import numpy as np
        E = 8
        H = 128
        HP = 128
        SPARSITY = 8
        N_ROTATE = 64
        ROPE_BASE = 10000.0

        def _rope(x, pos):
            half = N_ROTATE // 2
            inv_freq = 1.0 / ROPE_BASE ** (jnp.arange(half, dtype=jnp.float32) * 2.0 / N_ROTATE)
            ang = pos.astype(jnp.float32)[..., None] * inv_freq
            sin, cos = (jnp.sin(ang), jnp.cos(ang))
            x1, x2 = (x[..., :half], x[..., half:])
            return jnp.concatenate([x1 * cos - x2 * sin, x2 * cos + x1 * sin], axis=-1)
        B, T, _ = X.shape
        k = min(max(T // SPARSITY, 2), T)
        logits = jax.nn.sigmoid(jnp.einsum('bth,eh->bte', X, Wr))
        topk_vals, topk_I = jax.lax.top_k(logits.transpose(0, 2, 1), k)
        idx_flat = topk_I.reshape(B, E * k)
        Xg = jnp.take_along_axis(X, idx_flat[:, :, None], axis=1).reshape(B, E, k, H)
        QKV = jnp.einsum('beki,eij->bekj', Xg, Wqkv)
        Q, K, V = jnp.split(QKV, 3, axis=-1)
        Q = jnp.concatenate([_rope(Q[..., :N_ROTATE], topk_I), Q[..., N_ROTATE:]], axis=-1)
        K = jnp.concatenate([_rope(K[..., :N_ROTATE], topk_I), K[..., N_ROTATE:]], axis=-1)
        M = topk_I[..., :, None] >= topk_I[..., None, :]
        scores = jnp.einsum('bekd,bemd->bekm', Q, K) / math.sqrt(HP)
        scores = jnp.where(M, scores, -jnp.inf)
        A = jax.nn.softmax(scores, axis=-1)
        AV = jnp.einsum('bekm,bemd->bekd', A, V)
        AV = AV * topk_vals[..., None]
        Xpre = jnp.einsum('bekj,eji->beki', AV, Wo)
        out = jnp.zeros((B, T, H), dtype=X.dtype)
        out = out.at[jnp.arange(B)[:, None], idx_flat].add(Xpre.reshape(B, E * k, H))
        return out

    def _L1_attn_ref(x, Wq, Wk, Wv, Wo, q_phase_angle, alibi_log_slopes):
        import jax, jax.numpy as jnp
        import numpy as np
        import math
        TOK_DIM = 64
        POS_DIM = 64
        D_MODEL = 128
        N_HEADS = 16
        HEAD_DIM = 64
        NUM_KV_HEADS = 4
        INNER = N_HEADS * HEAD_DIM
        KV_INNER = NUM_KV_HEADS * HEAD_DIM
        KV_REPEAT = N_HEADS // NUM_KV_HEADS
        B, T = (2, 256)
        Bx, Tx, _ = x.shape
        x_tok = x[:, :, :TOK_DIM]
        x_pos = x[:, :, TOK_DIM:]
        q = x_pos @ Wq.T
        k = x_pos @ Wk.T
        v = x_tok @ Wv.T
        q = q.reshape(Bx, Tx, N_HEADS, HEAD_DIM).transpose(0, 2, 1, 3)
        k = k.reshape(Bx, Tx, NUM_KV_HEADS, HEAD_DIM).transpose(0, 2, 1, 3)
        v = v.reshape(Bx, Tx, NUM_KV_HEADS, HEAD_DIM).transpose(0, 2, 1, 3)
        c = jnp.cos(q_phase_angle)[None, :, None, None]
        s = jnp.sin(q_phase_angle)[None, :, None, None]
        qp = q.reshape(Bx, N_HEADS, Tx, HEAD_DIM // 2, 2)
        q0, q1 = (qp[..., 0], qp[..., 1])
        q = jnp.stack([q0 * c - q1 * s, q0 * s + q1 * c], axis=-1).reshape(Bx, N_HEADS, Tx, HEAD_DIM)
        k = jnp.repeat(k, KV_REPEAT, axis=1)
        v = jnp.repeat(v, KV_REPEAT, axis=1)
        att = jnp.einsum('bhqd,bhkd->bhqk', q, k) / math.sqrt(HEAD_DIM)
        pos = jnp.arange(Tx)
        rel = (pos[:, None] - pos[None, :]).astype(att.dtype)
        slopes = jnp.exp(alibi_log_slopes)
        att = att + slopes[None, :, None, None] * rel[None, None, :, :]
        causal = pos[None, :] <= pos[:, None]
        att = jnp.where(causal[None, None, :, :], att, -jnp.inf)
        att = jax.nn.softmax(att, axis=-1)
        out = jnp.einsum('bhqk,bhkd->bhqd', att, v)
        out = out.transpose(0, 2, 1, 3).reshape(Bx, Tx, INNER)
        return out @ Wo.T

    def _L1_ffn_ref(x, Wr, br, W_up, b_up, W_down, b_down):
        import jax, jax.numpy as jnp
        import numpy as np
        B, S, H = (4, 256, 128)
        E = 8
        GS = 2
        NG = E // GS
        F = int(H * 4 * (2.0 / 3.0))
        b, s, h = x.shape
        n_tok = b * s
        k = n_tok // E
        xf = x.reshape(n_tok, h)
        logits = xf @ Wr + br
        Sm = jax.nn.softmax(logits, axis=-1)
        G_t, idx_t = jax.lax.top_k(Sm.T, k)
        G = G_t.T
        idx = idx_t.T
        tokens = xf[idx]
        group = jnp.arange(E) // GS
        Wu = W_up[group]
        bu = b_up[group]
        mid = jax.nn.silu(jnp.einsum('keh,ehf->kef', tokens, Wu) + bu)
        out = jnp.einsum('kef,efh->keh', mid, W_down) + b_down
        y = jnp.zeros_like(xf).at[idx].add(G[..., None] * out)
        return y.reshape(b, s, h)

    def _L2_attn_ref(x, Wq, bq, Wk, bk, Wv, bv, Wm, bm):
        import jax, jax.numpy as jnp
        import numpy as np
        B, S, D = (4, 256, 128)
        H = 16
        HS = D // H
        SCALE = HS ** 0.5
        bs, seq, _ = x.shape

        def heads(w, b):
            return (x @ w + b).reshape(bs, seq, H, HS).transpose(0, 2, 1, 3)
        q = heads(Wq, bq)
        k = heads(Wk, bk)
        v = heads(Wv, bv)
        scores = jnp.einsum('bhqd,bhkd->bhqk', q, k) / SCALE
        causal_mask = jnp.arange(seq)[None, :] > jnp.arange(seq)[:, None]
        scores = jnp.where(causal_mask, jnp.float32(-1000000000000.0), scores)
        probs = jax.nn.softmax(scores, axis=-1)
        attn = jnp.einsum('bhqk,bhkd->bhqd', probs, v)
        attn = attn.transpose(0, 2, 1, 3).reshape(bs, seq, H * HS)
        return attn @ Wm + bm

    def _L2_ffn_ref(x, Wg, bg, W1, b1, W2, b2, gamma, beta):
        import jax, jax.numpy as jnp
        import numpy as np
        D = 128
        H = 512
        E = 8
        B = 2
        T = 256
        LN_EPS = 1e-05

        def _layer_norm(r, gamma, beta):
            mu = jnp.mean(r, axis=-1, keepdims=True)
            var = jnp.mean(jnp.square(r - mu), axis=-1, keepdims=True)
            return (r - mu) * jax.lax.rsqrt(var + LN_EPS) * gamma + beta
        logits = jnp.einsum('btd,de->bte', x, Wg) + bg
        top2_vals, top2_idx = jax.lax.top_k(logits, 2)
        scores = jax.nn.softmax(top2_vals, axis=-1)
        onehot = jax.nn.one_hot(top2_idx, E, dtype=x.dtype)
        combine = jnp.einsum('btk,btke->bte', scores, onehot)
        h = jnp.einsum('btd,edh->bteh', x, W1) + b1[None, None]
        h = jax.nn.gelu(h, approximate=False)
        y = jnp.einsum('bteh,ehd->bted', h, W2) + b2[None, None]
        out = jnp.einsum('bted,bte->btd', y, combine)
        return _layer_norm(x + out, gamma, beta)

    def _L3_attn_ref(hidden_states, c_attn_kernel, c_attn_bias, c_proj_kernel, c_proj_bias):
        import jax, jax.numpy as jnp
        import numpy as np
        B, S, D, H = (2, 256, 128, 16)
        HD = D // H
        b, s, d = hidden_states.shape
        qkv = hidden_states @ c_attn_kernel.T + c_attn_bias
        q, k, v = jnp.split(qkv, 3, axis=2)
        q = q.reshape(b, s, H, HD)
        k = k.reshape(b, s, H, HD)
        v = v.reshape(b, s, H, HD)
        causal = jnp.tril(jnp.ones((s, s), dtype=bool))
        neg = jnp.finfo(jnp.float32).min
        bias = jnp.where(causal, 0.0, neg).astype(jnp.float32)
        scale = 1.0 / jnp.sqrt(jnp.float32(HD))
        scores = jnp.einsum('bqhd,bkhd->bhqk', q * scale, k) + bias
        attn_weights = jax.nn.softmax(scores, axis=-1)
        attn_output = jnp.einsum('bhqk,bkhd->bqhd', attn_weights, v)
        attn_output = attn_output.reshape(b, s, d)
        out = attn_output @ c_proj_kernel.T + c_proj_bias
        return out

    def _L3_ffn_ref(x, router_w, router_bias, up_proj, gate_proj, down_proj, sh_gate, sh_up, sh_down):
        import jax, jax.numpy as jnp
        import numpy as np
        DIM = 128
        EXPERT_DIM = 64
        N_EXPERTS = 16
        TOPK = 2
        SHARED_HIDDEN = EXPERT_DIM * TOPK
        B, T = (4, 128)

        def _moe_forward(x, router_w, router_bias, up_proj, gate_proj, down_proj, sh_gate, sh_up, sh_down):
            Bb, Tt, D = x.shape
            flat = x.reshape(Bb * Tt, D)
            N = flat.shape[0]
            logits = flat @ router_w.T
            topk_scores, topk_idx = jax.lax.top_k(logits + router_bias, TOPK)
            topk_scores = jax.nn.softmax(topk_scores, axis=-1)
            combine = jnp.zeros((N, N_EXPERTS), flat.dtype)
            combine = combine.at[jnp.arange(N)[:, None], topk_idx].add(topk_scores)
            up_all = jnp.einsum('nd,kde->nke', flat, up_proj)
            gate_all = jnp.einsum('nd,kde->nke', flat, gate_proj)
            hidden = jax.nn.silu(gate_all) * up_all
            down_all = jnp.einsum('nke,ked->nkd', hidden, down_proj)
            out = jnp.einsum('nk,nkd->nd', combine, down_all)
            sh_hidden = jax.nn.silu(flat @ sh_gate.T) * (flat @ sh_up.T)
            out = out + sh_hidden @ sh_down.T
            return out.reshape(Bb, Tt, D)
        return _moe_forward(x, router_w, router_bias, up_proj, gate_proj, down_proj, sh_gate, sh_up, sh_down)
    x = L0_attn_x
    mod = (_silu(L0_c) @ L0_wmod).reshape(L0_c.shape[0], 6, 1, -1)
    sa, ca, ga, sb, cb, gb = (mod[:, 0], mod[:, 1], mod[:, 2], mod[:, 3], mod[:, 4], mod[:, 5])
    ga = (2 * (ga >= 0) - 1) * jnp.maximum(jnp.abs(ga), 0.25)
    gb = (2 * (gb >= 0) - 1) * jnp.maximum(jnp.abs(gb), 0.25)
    h = _layernorm(x, axis=-1) * (1 + ca) + sa
    x = x + ga * _L0_attn_ref(h, L0_attn_Wq, L0_attn_Wk, L0_attn_Wv, L0_attn_Wo, L0_attn_lambda_q1, L0_attn_lambda_k1, L0_attn_lambda_q2, L0_attn_lambda_k2, L0_attn_ln_w, L0_attn_ln_b)
    h = _layernorm(x, axis=-1) * (1 + cb) + sb
    x = x + gb * _L0_ffn_ref(h, L0_ffn_Wr, L0_ffn_Wqkv, L0_ffn_Wo)
    mod = (_silu(L1_c) @ L1_wmod).reshape(L1_c.shape[0], 6, 1, -1)
    sa, ca, ga, sb, cb, gb = (mod[:, 0], mod[:, 1], mod[:, 2], mod[:, 3], mod[:, 4], mod[:, 5])
    ga = (2 * (ga >= 0) - 1) * jnp.maximum(jnp.abs(ga), 0.25)
    gb = (2 * (gb >= 0) - 1) * jnp.maximum(jnp.abs(gb), 0.25)
    h = _layernorm(x, axis=-1) * (1 + ca) + sa
    x = x + ga * _L1_attn_ref(h, L1_attn_Wq, L1_attn_Wk, L1_attn_Wv, L1_attn_Wo, L1_attn_q_phase_angle, L1_attn_alibi_log_slopes)
    h = _layernorm(x, axis=-1) * (1 + cb) + sb
    x = x + gb * _L1_ffn_ref(h, L1_ffn_Wr, L1_ffn_br, L1_ffn_W_up, L1_ffn_b_up, L1_ffn_W_down, L1_ffn_b_down)
    mod = (_silu(L2_c) @ L2_wmod).reshape(L2_c.shape[0], 6, 1, -1)
    sa, ca, ga, sb, cb, gb = (mod[:, 0], mod[:, 1], mod[:, 2], mod[:, 3], mod[:, 4], mod[:, 5])
    ga = (2 * (ga >= 0) - 1) * jnp.maximum(jnp.abs(ga), 0.25)
    gb = (2 * (gb >= 0) - 1) * jnp.maximum(jnp.abs(gb), 0.25)
    h = _layernorm(x, axis=-1) * (1 + ca) + sa
    x = x + ga * _L2_attn_ref(h, L2_attn_Wq, L2_attn_bq, L2_attn_Wk, L2_attn_bk, L2_attn_Wv, L2_attn_bv, L2_attn_Wm, L2_attn_bm)
    h = _layernorm(x, axis=-1) * (1 + cb) + sb
    x = x + gb * _L2_ffn_ref(h, L2_ffn_Wg, L2_ffn_bg, L2_ffn_W1, L2_ffn_b1, L2_ffn_W2, L2_ffn_b2, L2_ffn_gamma, L2_ffn_beta)
    mod = (_silu(L3_c) @ L3_wmod).reshape(L3_c.shape[0], 6, 1, -1)
    sa, ca, ga, sb, cb, gb = (mod[:, 0], mod[:, 1], mod[:, 2], mod[:, 3], mod[:, 4], mod[:, 5])
    ga = (2 * (ga >= 0) - 1) * jnp.maximum(jnp.abs(ga), 0.25)
    gb = (2 * (gb >= 0) - 1) * jnp.maximum(jnp.abs(gb), 0.25)
    h = _layernorm(x, axis=-1) * (1 + ca) + sa
    x = x + ga * _L3_attn_ref(h, L3_attn_c_attn_kernel, L3_attn_c_attn_bias, L3_attn_c_proj_kernel, L3_attn_c_proj_bias)
    h = _layernorm(x, axis=-1) * (1 + cb) + sb
    x = x + gb * _L3_ffn_ref(h, L3_ffn_router_w, L3_ffn_router_bias, L3_ffn_up_proj, L3_ffn_gate_proj, L3_ffn_down_proj, L3_ffn_sh_gate, L3_ffn_sh_up, L3_ffn_sh_down)
    return x

_drawn_inputs = setup_inputs


def setup_inputs(seed=0):
    import zlib

    import numpy as np

    out = dict(_drawn_inputs(seed))
    spreads = {'L0_attn_ln_b': (0.0, 0.8),
     'L1_attn_alibi_log_slopes': (0.834032416343689, 0.6),
     'L1_ffn_br': (0.0, 0.8),
     'L2_ffn_gamma': (1.0, 0.2),
     'L2_ffn_beta': (0.0, 0.331),
     'L3_attn_c_attn_bias': (0.0, 0.8),
     'L3_attn_c_proj_bias': (0.0, 0.335),
     'L3_ffn_router_bias': (0.0, 0.8)}
    factors = {'L0_attn_lambda_q1': 8.0,
     'L0_attn_lambda_k1': 8.0,
     'L0_attn_lambda_q2': 8.0,
     'L0_attn_lambda_k2': 8.0,
     'L0_attn_ln_w': 7.85,
     'L0_ffn_Wr': 8.0,
     'L0_ffn_Wqkv': 8.0,
     'L0_ffn_Wo': 8.0,
     'L1_attn_Wq': 8.0,
     'L1_attn_Wk': 8.0,
     'L1_attn_q_phase_angle': 8.0,
     'L1_ffn_b_up': 8.0,
     'L1_ffn_b_down': 8.0,
     'L2_attn_Wq': 8.0,
     'L2_attn_bq': 8.0,
     'L2_attn_Wk': 8.0,
     'L2_attn_bk': 64.0,
     'L2_attn_Wv': 5.224,
     'L2_attn_bv': 6.501,
     'L2_attn_Wm': 4.375,
     'L2_attn_bm': 4.13,
     'L2_ffn_bg': 6.777,
     'L2_ffn_b1': 23.281,
     'L2_ffn_b2': 8.0,
     'L3_attn_c_attn_kernel': 8.0,
     'L3_attn_c_proj_kernel': 8.0,
     'L3_ffn_router_w': 8.0,
     'L3_ffn_up_proj': 8.0,
     'L3_ffn_gate_proj': 8.0,
     'L3_ffn_down_proj': 8.0,
     'L3_ffn_sh_gate': 8.0,
     'L3_ffn_sh_up': 8.0,
     'L3_ffn_sh_down': 8.0}
    for name, (base, spread) in spreads.items():
        noise = np.random.default_rng([zlib.crc32(name.encode()), seed]).standard_normal(out[name].shape)
        drawn = base * np.exp(spread * noise) if base else spread * noise
        out[name] = jnp.asarray(drawn.astype(out[name].dtype))
    for name, factor in factors.items():
        out[name] = (out[name] * factor).astype(out[name].dtype)
    return out
```

```python
from contextlib import ExitStack

import numpy as np

import concourse.bass as bass
from concourse import mybir

F32 = mybir.dt.float32
BF16 = mybir.dt.bfloat16
I32 = mybir.dt.int32
U32 = mybir.dt.uint32
ALU = mybir.AluOpType
ACT = mybir.ActivationFunctionType
AX = mybir.AxisListType

P = 128
NB = 8
T = 512
NI = T // P
NT = NB * NI
D = 128
LN_EPS = 1e-5
NEG = -1e30


def wait_alone(eng, sem, value):
    eng.wait_ge(sem, value)
    eng.sem_inc(State.passed[eng.engine], 1)


class Chain:

    def __init__(self, eng, sem, turn=0, per=0, before=0):
        self.eng, self.sem, self.base, self.per, self.n = eng, sem, turn * per + before, per, 0

    def then(self, ins):
        self.n += 1
        ins.then_inc(self.sem, 1)

    def wait(self, alone=False):
        if self.per and alone:
            wait_alone(self.eng, self.sem, self.base + self.n)
        else:
            self.eng.wait_ge(self.sem, self.base + self.n)

    def link(self, ins, alone=False):
        self.then(ins)
        self.wait(alone)

    def end(self):
        assert self.per in (0, self.n), f"{self.n} steps a turn"


def rsqrt(dve, c, out, v, t, scale, eps):
    rsqrt_guess(dve, c, out, v, scale, eps)
    for _ in range(4):
        rsqrt_newton(dve, c, out, v, t)


def rsqrt_guess(dve, c, out, v, scale, eps):
    c.link(dve.tensor_scalar(v, v, scale, eps, ALU.mult, ALU.add))
    c.link(dve.tensor_scalar(out.bitcast(I32), v.bitcast(I32), -0.5, float(0x5F3759DF), ALU.mult, ALU.add))


def rsqrt_newton(dve, c, out, v, t):
    c.link(dve.tensor_tensor(t, out, out, ALU.mult))
    c.link(dve.tensor_tensor(t, t, v, ALU.mult))
    c.link(dve.tensor_scalar(t, t, -0.5, 1.5, ALU.mult, ALU.add))
    c.link(dve.tensor_tensor(out, out, t, ALU.mult))


RSQRT_STEPS = 18


class State:
    passed = {}


    def sem(self, name):
        self.sems.append(self.nc.alloc_semaphore(name))
        return self.sems[-1]


def bcast(ap, axis, n):
    v = ap.unsqueeze(axis)
    return v.broadcast_to([n if k == axis else s for k, s in enumerate(v.shape)])


def setup_stage(S):
    nc = S.nc
    loaded = nc.alloc_semaphore("x_loaded")
    stats_ready = nc.alloc_semaphore("x_stats_chain")
    with nc.Block() as block:
        @block.sync
        def _(sp):
            for b in range(NB):
                sp.dma_start(S.x[:, b * NI:(b + 1) * NI], S.dram["x"][b].rearrange("(i p) f -> p i f", p=P)).then_inc(loaded, 16)
            sp.dma_start(S.ident[:], S.dram["ident"]).then_inc(loaded, 16)
            sp.dma_start(S.identb[:], S.dram["identb"]).then_inc(loaded, 16)

        @block.vector
        def _(dve):
            c = Chain(dve, stats_ready)
            dve.memset(S.ones[:], 1.0)
            dve.wait_ge(loaded, (NB + 2) * 16)
            for b in range(NB):
                for i in range(NI):
                    ins = dve.bn_stats(S.bn[:, b, i], S.x[:, b * NI + i])
                c.then(ins)
            c.wait()
            for t in range(NT):
                ins = dve.bn_aggr(S.mv[:, t], S.bn[:, t // NI, t % NI])
            c.then(ins)


def mod_stage(S, l):
    nc = S.nc
    n = f"L{l}_mod_"
    loaded, silu_done, modT_done, gates_done, diag_free, bc_done, bc_out = (
        S.sem(n + s) for s in ("loaded", "silu", "modT", "gates", "diag", "bcast", "bcast_out"))
    with ExitStack() as ctx:
        sb = lambda name, shape, dt=F32: ctx.enter_context(nc.sbuf_tensor(n + name, shape, dt))
        wmod = sb("w", [P, 6 * D])
        cT = sb("cT", [P, NB])
        sT = sb("sT", [P, NB])
        clip = sb("clip", [P, 2, 2, NB])
        diag = sb("diag", [P, 2, 4, D])
        ps = ctx.enter_context(nc.psum_tensor(n + "ps", [P, 6, NB], F32))
        pb = ctx.enter_context(nc.psum_tensor(n + "pb", [P, 2, 512], F32))
        block = ctx.enter_context(nc.Block())

        @block.sync
        def _(sp):
            sp.dma_start(wmod[:], S.dram[f"L{l}_wmod"]).then_inc(loaded, 16)
            sp.dma_start(cT[:], S.dram[f"L{l}_cT"]).then_inc(loaded, 16)

        @block.scalar
        def _(act):
            act.wait_ge(loaded, 32)
            act.activation(sT[:], cT[:], ACT.Silu).then_inc(silu_done, 1)
            for k in range(4):
                act.wait_ge(bc_done, k + 1)
                act.activation(S.gate[:, k // 2, 4 * (k % 2):4 * (k % 2) + 4], pb[:, k % 2, :].rearrange(
                    "p (b f) -> p b f", b=4), ACT.Copy).then_inc(bc_out, 1)

        @block.tensor
        def _(pe):
            pe.wait_ge(silu_done, 1)
            for k in range(6):
                ins = pe.matmul(ps[:, k], wmod[:, k * D:(k + 1) * D], sT[:], start=True, stop=True)
            ins.then_inc(modT_done, 1)
            for k in range(4):
                pe.wait_ge(diag_free, k + 1)
                if k >= 2:
                    pe.wait_ge(bc_out, k - 1)
                pe.matmul(pb[:, k % 2, :], S.ones[:], diag[:, k % 2].rearrange("p b f -> p (b f)"),
                          start=True, stop=True).then_inc(bc_done, 1)

        @block.vector
        def _(dve):
            c = Chain(dve, gates_done)
            dve.wait_ge(modT_done, 1)
            c.link(dve.tensor_copy(S.modT[:], ps[:]))
            scales = S.modT[:, 1::3]
            c.link(dve.tensor_scalar(scales, scales, 1.0, None, ALU.add))
            g = S.modT[:, 2::3]
            c.then(dve.tensor_scalar(clip[:, 0], g, 0.25, None, ALU.max))
            c.link(dve.tensor_scalar(clip[:, 1], g, -0.25, None, ALU.min))
            for k in range(2):
                gk = S.modT[:, 2 + 3 * k]
                c.then(dve.scalar_tensor_tensor(clip[:, 0, k], gk, 0.0, clip[:, 0, k], ALU.is_ge, ALU.mult))
                c.link(dve.scalar_tensor_tensor(clip[:, 1, k], gk, 0.0, clip[:, 1, k], ALU.is_lt, ALU.mult))
            c.link(dve.tensor_tensor(g, clip[:, 0], clip[:, 1], ALU.add))
            for k in range(4):
                if k >= 2:
                    dve.wait_ge(bc_done, k - 1)
                for j in range(4):
                    ins = dve.tensor_scalar(diag[:, k % 2, j], S.ident[:],
                                            S.modT[:, 2 + 3 * (k // 2), 4 * (k % 2) + j:4 * (k % 2) + j + 1],
                                            None, ALU.mult)
                ins.then_inc(diag_free, 1)


def rstd_step(S, dve, c):
    c.link(dve.tensor_copy(S.var[:], S.mv[:, :, 1]))
    rsqrt(dve, c, S.rstd[:], S.var[:], S.nwt[:], 1.0, LN_EPS)


def normalise(S, dve, b, z):
    for i in range(NI):
        t = b * NI + i
        ins = dve.tensor_scalar(z[:, i], S.x[:, bass.ds(t, 1)].squeeze(1), S.mv[:, bass.ds(t, 1), 0],
                                S.rstd[:, bass.ds(t, 1)], ALU.subtract, ALU.mult)
    return ins


def add_and_stats(S, dve, c, b, kind, result, was_read=None):
    xb = S.x[:, bass.ds(b * NI, NI)]
    g = bcast(S.gate[:, kind, bass.ds(b, 1)].squeeze(1), 1, NI)
    ins = dve.tensor_tensor(S.upd[:], result, g, ALU.mult)
    if was_read is None:
        c.link(ins)
    else:
        ins.then_inc(was_read, 1)
        dve.wait_ge(was_read, b + 1)
    c.link(dve.tensor_tensor(xb, xb, S.upd[:], ALU.add), alone=True)
    for i in range(NI):
        ins = dve.bn_stats(S.bn[:, 0, i], S.x[:, bass.ds(b * NI + i, 1)].squeeze(1))
    c.link(ins, alone=True)
    for i in range(NI):
        ins = dve.bn_aggr(S.mv4[:, i], S.bn[:, 0, i])
    c.link(ins, alone=True)
    c.then(dve.tensor_copy(S.mv[:, bass.ds(b * NI, NI)], S.mv4[:]))


ADD_STEPS = 5


def l0_attn_stage(S):
    nc = S.nc
    H, HD = 8, 8
    LAMBDA_INIT = 0.8 - 0.6 * float(np.exp(-0.3 * 12))
    n = "L0a_"
    sem = lambda s: S.sem(n + s)
    loaded, chain, z_ready, zT_done, hT_ready, qkv_done, qk_used, v_ready, rope_done, prod1, prod2 = map(
        sem, ("loaded", "dve", "z", "zT", "hT", "qkv", "qk_used", "v", "rope", "prod1", "prod2"))
    soft_ready, exp_done, pm_ready, red1, red2, a_ready, aT_done, aT_ready, o_done, added = map(
        sem, ("soft", "exp", "pm", "red1", "red2", "a", "aT", "aTs", "o", "added"))
    with ExitStack() as ctx:
        sb = lambda name, shape, dt=F32: ctx.enter_context(nc.sbuf_tensor(n + name, shape, dt))
        pt = lambda name, shape, dt=F32: ctx.enter_context(nc.psum_tensor(n + name, shape, dt))
        w = sb("w", [P, 6, D])
        rope = sb("rope", [P, NI, 2, D])
        lam4 = sb("lam4", [P, 4, HD])
        lnT = sb("lnT", [P, 2])
        lam = sb("lam", [P, 4])
        z = sb("z", [P, NI, D])
        hT = sb("hT", [P, T])
        vs = sb("v", [P, 2, NI, D])
        r1 = sb("r1", [P, NI, 2, D])
        r2 = sb("r2", [P, NI, 2, D])
        pr1 = sb("pr1", [P, NI, 2, 512])
        pr2 = sb("pr2", [P, NI, 1024])
        s = sb("s", [P, NI, 2, 8, 8])
        e = sb("e", [P, NI, 2, 8, 8])
        mx = sb("mx", [P, NI * 16])
        sm = sb("sm", [P, NI, 2, 8])
        pm = sb("pm", [P, NI, 8, 8])
        a = sb("a", [P, NI, D])
        a2 = sb("a2", [P, NI, D])
        ss = sb("ss", [P, 3, NI * 8])
        aT = sb("aT", [P, T])
        psT = pt("psT", [P, T])
        psQ = pt("psQ", [P, 2, 2, 2, D])
        psV = pt("psV", [P, NI, D])
        psA = pt("psA", [P, T])
        psO = pt("psO", [P, NI, D])
        block = ctx.enter_context(nc.Block())

        @block.sync
        def _(sp):
            sp.dma_start(w[:], S.dram["L0a_w"]).then_inc(loaded, 16)
            sp.dma_start(rope[:], S.dram["L0a_rope"]).then_inc(loaded, 16)
            sp.dma_start(lam4[:], S.dram["L0a_lam"].partition_broadcast(P)).then_inc(loaded, 16)
            for h in range(H):
                sp.dma_start(lnT[h * 16:(h + 1) * 16], S.dram["L0a_ln"]).then_inc(loaded, 16)

        def turns(eng, body):
            for t in range(3):
                body(t, t % 2, True, t > 0, True, t > 1)
            with eng.Fori(1, NB // 2 - 1) as two:
                for u in range(2):
                    body(two * 2 + (u + 1), 1 - u, True, True, True, True)
            body(NB - 1, 1, True, True, False, True)
            body(NB, 0, False, True, False, True)

        @block.tensor
        def _(pe):
            pe.wait_ge(loaded, (3 + H) * 16)

            def project(b, later):
                pe.wait_ge(z_ready, b + 1)
                if later:
                    pe.wait_ge(hT_ready, b)
                for i in range(NI):
                    ins = pe.transpose(psT[:, i * P:(i + 1) * P], z[:, i], S.ident[:])
                ins.then_inc(zT_done, 1)
                pe.wait_ge(hT_ready, b + 1)
                for i in range(NI):
                    if i == 0 and later:
                        pe.wait_ge(v_ready, b)
                    if i >= 2 or later:
                        pe.wait_ge(qk_used, NI * b + i - 1)
                    h = hT[:, i * P:(i + 1) * P]
                    pe.matmul(psQ[:, i % 2].rearrange("p a b f -> p (a b f)"), h,
                              w[:, 0:4].rearrange("p a f -> p (a f)"), start=True, stop=True)
                    pe.matmul(psV[:, i], h, w[:, 4], start=True, stop=True).then_inc(qkv_done, 1)

            project(0, False)

            def turn(t, par, front, back, ahead, end):
                if ahead:
                    project(t + 1, True)
                if back:
                    pe.wait_ge(a_ready, t)
                    for i in range(NI):
                        ins = pe.transpose(psA[:, i * P:(i + 1) * P], a[:, i], S.ident[:])
                    ins.then_inc(aT_done, 1)
                    pe.wait_ge(aT_ready, t)
                    for i in range(NI):
                        ins = pe.matmul(psO[:, i], aT[:, i * P:(i + 1) * P], w[:, 5], start=True, stop=True)
                    ins.then_inc(o_done, 1)

            turns(pe, turn)

        @block.scalar
        def _(act):
            act.wait_ge(chain, 2)
            act.activation(lam[:, 2:4], lam[:, 0:2], ACT.Exp).then_inc(exp_done, 1)

            def modulate(b):
                act.wait_ge(zT_done, b + 1)
                act.activation(hT[:], psT[:], ACT.Identity, bias=S.modT[:, 0, bass.ds(b, 1)],
                               scale=S.modT[:, 1, bass.ds(b, 1)]).then_inc(hT_ready, 1)

            def values(b, par, used):
                act.wait_ge(qkv_done, NI * (b + 1))
                if used:
                    act.wait_ge(prod2, NI * (b - 1))
                act.activation(vs[:, par], psV[:], ACT.Copy).then_inc(v_ready, 1)

            def turn(t, par, front, back, ahead, end):
                if ahead:
                    act.wait_ge(qkv_done, NI * (t + 1))
                    modulate(t + 1)
                if front:
                    act.wait_ge(soft_ready, t + 1)
                    act.activation(e[:], s[:], ACT.Exp, scale=float(HD) ** -0.25).then_inc(exp_done, 1)
                if ahead:
                    values(t + 1, 1 - par, back)
                if back:
                    act.wait_ge(aT_done, t)
                    act.activation(aT[:], psA[:], ACT.Identity, bias=lnT[:, 1:2], scale=lnT[:, 0:1]).then_inc(aT_ready, 1)

            modulate(0)
            values(0, 0, False)
            turns(act, turn)

        @block.gpsimd
        def _(pool):
            def turn(t, par, front, back, ahead, end):
                if front:
                    for i in range(NI):
                        pool.wait_ge(rope_done, NI * t + i + 1)
                        if back:
                            pool.wait_ge(red1, NI * (t - 1) + i + 1)
                        for g in range(2):
                            q = r1[:, i, 0].rearrange("p (n g d) -> p n g d", g=2, d=HD)[:, :, g]
                            k = r1[:, i, 1].rearrange("p (n g d) -> p n g d", g=2, d=HD)[:, :, g]
                            ins = pool.tensor_tensor(pr1[:, i, g].rearrange("p (n m d) -> p n m d", n=H, m=H),
                                                     bcast(q, 2, H), bcast(k, 1, H), ALU.mult)
                        ins.then_inc(prod1, 1)
                if back:
                    row = t - 1
                    pool.wait_ge(pm_ready, t)
                    pool.wait_ge(v_ready, t)
                    for i in range(NI):
                        if end:
                            pool.wait_ge(red2, NI * (row - 1) + i + 1)
                        v = vs[:, 1 - par, i].rearrange("p (m e) -> p e m", m=H)
                        pool.tensor_tensor(pr2[:, i].rearrange("p (n e m) -> p n e m", n=H, m=H),
                                           bcast(pm[:, i], 2, 2 * HD), bcast(v, 1, H), ALU.mult).then_inc(prod2, 1)

            turns(pool, turn)

        @block.vector
        def _(dve):
            dve.wait_ge(loaded, (3 + H) * 16)
            c = Chain(dve, chain)
            c.link(dve.tensor_tensor(lam4[:, 0:4:2], lam4[:, 0:4:2], lam4[:, 1:4:2], ALU.mult))
            c.link(dve.tensor_reduce(lam[:, 0:2], lam4[:, 0:4:2], AX.X, ALU.add))
            c.then(dve.tensor_scalar(lnT[:], lnT[:], 1.0 - LAMBDA_INIT, None, ALU.mult))
            dve.wait_ge(exp_done, 1)
            c.link(dve.tensor_tensor(lam[:, 0:1], lam[:, 3:4], lam[:, 2:3], ALU.subtract))
            c.link(dve.tensor_scalar(lam[:, 0:1], lam[:, 0:1], -LAMBDA_INIT, None, ALU.add))
            rstd_step(S, dve, c)
            n0 = c.n
            AHEAD, FRONT, BACK = NI, 1, 6 + RSQRT_STEPS
            sr = s[:].rearrange("p i g n m -> p (i g n) m")
            er = e[:].rearrange("p i g n m -> p (i g n) m")
            smr = sm[:].rearrange("p i g n -> p (i g n)")
            ar = a[:].rearrange("p i (n e) -> p (i n) e", e=16)

            def rotate(c, b):
                for i in range(NI):
                    dve.wait_ge(qkv_done, NI * b + i + 1)
                    c.then(dve.tensor_tensor(r1[:, i], psQ[:, i % 2, :, 0], bcast(rope[:, i, 0], 1, 2), ALU.mult))
                    ins = dve.tensor_tensor(r2[:, i], psQ[:, i % 2, :, 1], bcast(rope[:, i, 1], 1, 2), ALU.mult)
                    ins.then_inc(qk_used, 1)
                    dve.wait_ge(qk_used, NI * b + i + 1)
                    c.wait()
                    dve.tensor_tensor(r1[:, i], r1[:, i], r2[:, i], ALU.add).then_inc(rope_done, 1)

            def add(row):
                dve.wait_ge(o_done, row + 1)
                ac = Chain(dve, added, row, ADD_STEPS)
                add_and_stats(S, dve, ac, row, 0, psO[:])
                ac.end()

            normalise(S, dve, 0, z).then_inc(z_ready, 1)
            rotate(c, 0)
            n0 = c.n

            def turn(t, par, front, back, ahead, end):
                c = Chain(dve, chain, 0, front and back and ahead)
                c.base = n0 + (t if front else NB) * FRONT + (t if front else NB - 1) * AHEAD + (
                    (t - 1) * BACK if back else 0)
                row = t - 1
                if ahead:
                    dve.wait_ge(zT_done, t + 1)
                    normalise(S, dve, t + 1, z).then_inc(z_ready, 1)
                if back:
                    dve.wait_ge(exp_done, t + 1)
                    c.link(dve.tensor_reduce(smr, er, AX.X, ALU.add))
                    c.link(dve.reciprocal(smr, smr))
                    c.link(dve.tensor_scalar(sm[:, :, 1], sm[:, :, 1], lam[:, 0:1], None, ALU.mult))
                    c.link(dve.tensor_tensor(er, er, bcast(smr, 2, 8), ALU.mult))
                    dve.tensor_tensor(pm[:].rearrange("p i n m -> p i (n m)"),
                                      e[:, :, 0].rearrange("p i n m -> p i (n m)"),
                                      e[:, :, 1].rearrange("p i n m -> p i (n m)"), ALU.add).then_inc(pm_ready, 1)
                if end:
                    add(t - 2)
                if front:
                    for i in range(NI):
                        dve.wait_ge(prod1, NI * t + i + 1)
                        dve.tensor_reduce(s[:, i].rearrange("p g n m -> p (g n m)"), pr1[:, i].rearrange(
                            "p g (x d) -> p (g x) d", d=HD), AX.X, ALU.add).then_inc(red1, 1)
                    dve.wait_ge(red1, NI * (t + 1))
                    c.link(dve.tensor_reduce(mx[:], sr, AX.X, ALU.max))
                    dve.tensor_tensor(sr, sr, bcast(mx[:], 2, 8), ALU.subtract).then_inc(soft_ready, 1)
                if ahead:
                    rotate(c, t + 1)
                if back:
                    for i in range(NI):
                        dve.wait_ge(prod2, NI * row + i + 1)
                        dve.tensor_reduce(a[:, i], pr2[:, i].rearrange("p (x m) -> p x m", m=H),
                                          AX.X, ALU.add).then_inc(red2, 1)
                    dve.wait_ge(red2, NI * (row + 1))
                    c.link(dve.tensor_tensor(a2[:], a[:], a[:], ALU.mult))
                    c.link(dve.tensor_reduce(ss[:, 0], a2[:].rearrange("p i (n e) -> p (i n) e", e=16), AX.X, ALU.add))
                    rsqrt(dve, c, ss[:, 1], ss[:, 0], ss[:, 2], 1.0 / 16, 1e-8)
                    dve.tensor_tensor(ar, ar, bcast(ss[:, 1], 2, 16), ALU.mult).then_inc(a_ready, 1)
                assert c.n == FRONT * front + AHEAD * ahead + BACK * back, c.n

            turns(dve, turn)
            add(NB - 1)


def token_choice_stage(S):
    nc = S.nc
    n = "L0f_"
    E, R = 8, T // 8
    with ExitStack() as ctx:
        sb = lambda name, shape, dt=F32: ctx.enter_context(nc.sbuf_tensor(n + name, shape, dt))
        z = sb("z", [P, NT, D])
        gates = sb("gates", [P, NI, NB * E])
        rank = sb("rank", [P, NI, NB * E])
        w = dict(q=sb("wq", [P, E, D]), k=sb("wk", [P, E, D]), s=sb("wsw", [P, E, D]), v=sb("wv", [P, E, D]),
                 o=sb("wo", [P, E, D]))
        tables = sb("tables", [P, NI, 3, D], BF16)
        with ExitStack() as inner:
            token_choice_ranks(S, n, inner, z, gates, rank, w, tables, R)
        nc.all_engine_barrier()
        with ExitStack() as inner:
            token_choice_experts(S, n, inner, z, gates, rank, w, tables, R)


def token_choice_ranks(S, n, ctx, z, gates, rank, w, tables, R):
    nc = S.nc
    E = 8
    BE = NB * E
    small, loaded, chain, z_ready, zT_done, hT_ready, logits_done, gates_ready, pairs_done, top_chain, ranks_done = map(
        lambda s: S.sem(n + s), ("small", "loaded", "dve", "z", "zT", "hT", "logits", "gates", "pairs", "top", "ranks"))
    sb = lambda name, shape, dt=F32: ctx.enter_context(nc.sbuf_tensor(n + name, shape, dt))
    pt = lambda name, shape, dt=F32: ctx.enter_context(nc.psum_tensor(n + name, shape, dt))
    wr = sb("wr", [P, E])
    hT = sb("hT", [P, 2, T])
    work = sb("work", [BE, 2, T])
    top = sb("top", [BE, R // 8, 8])
    cum = sb("cum", [BE, 2, T])
    psT = pt("psT", [P, 2, T])
    psL = pt("psL", [P, 2, T])
    psP = pt("psP", [BE, T])
    psR = pt("psR", [P, NI, BE])
    with nc.Block() as block:
        @block.sync
        def _(sp):
            sp.dma_start(wr[:], S.dram[n + "wr"]).then_inc(small, 16)
            sp.dma_start(tables[:], S.dram[n + "tables"]).then_inc(loaded, 16)
            for k in "qksvo":
                sp.dma_start(w[k][:], S.dram[n + "w" + k]).then_inc(loaded, 16)
            sp.wait_ge(loaded, 6 * 16)

        @block.tensor
        def _(pe):
            pe.wait_ge(small, 16)

            def logits(b):
                pe.wait_ge(hT_ready, b + 1)
                if b >= 2:
                    pe.wait_ge(gates_ready, b - 1)
                for i in range(NI):
                    ins = pe.matmul(psL[:, b % 2, i * E:(i + 1) * E], hT[:, b % 2, i * P:(i + 1) * P], wr[:],
                                    start=True, stop=True)
                ins.then_inc(logits_done, 1)

            for b in range(NB):
                pe.wait_ge(z_ready, b + 1)
                if b >= 2:
                    pe.wait_ge(hT_ready, b - 1)
                for i in range(NI):
                    ins = pe.transpose(psT[:, b % 2, i * P:(i + 1) * P], z[:, b * NI + i], S.ident[:])
                ins.then_inc(zT_done, 1)
                if b > 0:
                    logits(b - 1)
            logits(NB - 1)
            pe.wait_ge(gates_ready, NB)
            for i in range(NI):
                ins = pe.transpose(psP[:, i * P:(i + 1) * P], gates[:, i], S.ident[:])
            ins.then_inc(pairs_done, 1)
            pe.wait_ge(ranks_done, 1)
            for i in range(NI):
                ins = pe.transpose(psR[:, i], cum[:, 0, i * P:(i + 1) * P], S.ident[0:BE, 0:BE])
            ins.then_inc(pairs_done, 1)

        @block.scalar
        def _(act):
            def take_gates(b):
                act.wait_ge(logits_done, b + 1)
                act.activation(gates[:, :, b * E:(b + 1) * E], psL[:, b % 2, 0:NI * E].rearrange("p (i e) -> p i e", i=NI),
                               ACT.Sigmoid).then_inc(gates_ready, 1)

            for b in range(NB):
                act.wait_ge(zT_done, b + 1)
                if b >= 2:
                    act.wait_ge(logits_done, b - 1)
                act.activation(hT[:, b % 2], psT[:, b % 2], ACT.Identity, bias=S.modT[:, 3, b:b + 1],
                               scale=S.modT[:, 4, b:b + 1]).then_inc(hT_ready, 1)
                if b >= 1:
                    take_gates(b - 1)
            take_gates(NB - 1)

        @block.vector
        def _(dve):
            c = Chain(dve, chain)
            rstd_step(S, dve, c)
            for b in range(NB):
                normalise(S, dve, b, z[:, b * NI:(b + 1) * NI]).then_inc(z_ready, 1)
            c = Chain(dve, top_chain)
            dve.wait_ge(pairs_done, 1)
            c.link(dve.tensor_copy(work[:, 0], psP[:]))
            for r in range(R // 8):
                c.link(dve.max(top[:, r], work[:, r % 2]))
                c.link(dve.match_replace(work[:, (r + 1) % 2], top[:, r], work[:, r % 2], -1.0))
            c.link(dve.tensor_scalar(work[:, 1], work[:, 0], -1.0, None, ALU.is_equal))
            c.link(dve.tensor_copy(cum[:, 0], work[:, 1]))
            a, s = 0, 1
            while s < T:
                c.then(dve.tensor_tensor(cum[:, 1 - a, s:], cum[:, a, s:], cum[:, a, :T - s], ALU.add))
                c.link(dve.tensor_copy(cum[:, 1 - a, :s], cum[:, a, :s]))
                a, s = 1 - a, 2 * s
            c.link(dve.tensor_tensor(cum[:, a], cum[:, a], work[:, 1], ALU.mult))
            dve.tensor_scalar(cum[:, 0], cum[:, a], -1.0, None, ALU.add).then_inc(ranks_done, 1)
            dve.wait_ge(pairs_done, 2)
            c.then(dve.tensor_copy(rank[:], psR[:]))


def token_choice_experts(S, n, ctx, z, gates, rank, w, tables, R):
    nc = S.nc
    E, NP, H2 = 8, 4, D // 2
    ER = E * R
    SCALE = float(D) ** -0.5
    (loaded, hot_ready, z_chain, z_parts, g_parts, x_done, x_ready, tab_done, tab_ready, q_done, rot_q, rot_k, high,
     sw_done, v_done, v_ready, hotT_done, hotT_ready, gg_done, gg_ready, gg_sum, rotated) = map(lambda s: S.sem(n + s), (
         "masks", "hot", "pool", "z_parts", "g_parts", "x", "xs", "tab", "tabs", "q", "rot_q", "rot_k", "high",
         "sw", "v", "vs", "hotT", "hotTs", "gg", "ggs", "gg_sum", "rotated"))
    chain, s_done, s_ready, exp_done, aT_done, aT_ready, av_done, av_ready, o_done, o_parts, y_done, added, op1, op2 = map(
        lambda s: S.sem(n + s), ("chain", "s", "ss", "exp_", "aT", "aTs", "av", "avs", "o", "os", "y", "added", "op1", "op2"))
    sb = lambda name, shape, dt=F32: ctx.enter_context(nc.sbuf_tensor(n + name, shape, dt))
    pt = lambda name, shape, dt=F32: ctx.enter_context(nc.psum_tensor(n + name, shape, dt))
    iota = sb("iota", [P, R])
    causal = sb("causal", [P, P])
    own = sb("own", [P, NP, 3, E])
    hot = sb("hot", [P, 2, NI, ER], BF16)
    zp = sb("zp", [P, 2, 3, NI, D], BF16)
    zr = sb("zr", [P, NI, D])
    gp = sb("gp", [P, 2, NI, 3, E], BF16)
    gr = sb("gr", [P, NI, E])
    xT = sb("xT", [P, ER])
    tab = sb("tab", [P, ER])
    tab_low = sb("tab_low", [H2, ER])
    rot = sb("rot", [H2, 2, 2, ER])
    qk = sb("qk", [P, 2, 2, ER])
    v = sb("v", [P, 2, NP, D])
    hotT = sb("hotT", [P, 2, NP, T], BF16)
    gg = sb("gg", [P, 2, NP])
    ggm = sb("ggm", [P, NP, 3 * E])
    s = sb("s", [P, NP, P])
    mx = sb("mx", [P, NP])
    sm = sb("sm", [P, NP])
    e = sb("e", [P, NP, P])
    aT = sb("aT", [P, NP, P])
    avT = sb("avT", [P, NP, P])
    o = sb("o", [P, NP, D])
    op = sb("op", [P, 3, NP, D], BF16)
    bx, bt, bq, bk, bh, bs, ba, by = (pt("bank_" + k, [P, T]) for k in ("x", "t", "q", "k", "h", "s", "a", "y"))
    LOOP0 = 2

    class Turn:
        def __init__(self, t, parity, steady):
            self.t, self.par, self.steady = t, parity, steady
            self.front, self.back, self.end = (steady or 0 <= t - lag < NB for lag in range(3))
            self.ahead = steady or t + 1 < NB
            self.later = steady or t > 0

    def turns(eng, body):
        for t in range(LOOP0):
            body(Turn(t, t % 2, False))
        with eng.Fori(LOOP0 // 2, NB // 2 - 1) as two:
            for u in range(2):
                body(Turn(two * 2 + u, u, True))
        for t in range(NB - 2, NB + 1):
            body(Turn(t, t % 2, False))

    with nc.Block() as block:
        @block.sync
        def _(sp):
            sp.dma_start(iota[:], S.dram[n + "iota"]).then_inc(loaded, 16)
            sp.dma_start(causal[:], S.dram[n + "causal"]).then_inc(loaded, 16)
            sp.dma_start(own[:], S.dram[n + "own"]).then_inc(loaded, 16)

        @block.gpsimd
        def _(pool):
            def parts(b, par, before):
                c = Chain(pool, z_chain, 0, 8 * before)
                c.base = b * 8
                zrow = z[:, bass.ds(b * NI, NI)]
                p3 = zp[:, par]
                g = gates[:, :, bass.ds(b * E, E)]
                g3 = gp[:, par]
                if before:
                    wait_alone(pool, gg_done, b - 1)
                c.link(pool.tensor_copy(p3[:, 0], zrow), alone=True)
                c.link(pool.tensor_tensor(zr[:], zrow, p3[:, 0], ALU.subtract), alone=True)
                c.link(pool.tensor_copy(p3[:, 1], zr[:]), alone=True)
                c.link(pool.tensor_tensor(zr[:], zr[:], p3[:, 1], ALU.subtract), alone=True)
                pool.tensor_copy(p3[:, 2], zr[:]).then_inc(z_parts, 1)
                c.link(pool.tensor_copy(g3[:, :, 0], g), alone=True)
                c.link(pool.tensor_tensor(gr[:], g, g3[:, :, 0], ALU.subtract), alone=True)
                c.link(pool.tensor_copy(g3[:, :, 1], gr[:]), alone=True)
                c.link(pool.tensor_tensor(gr[:], gr[:], g3[:, :, 1], ALU.subtract), alone=True)
                pool.tensor_copy(g3[:, :, 2], gr[:]).then_inc(g_parts, 1)
                assert c.n == 8

            parts(0, 0, False)
            parts(1, 1, False)
            with pool.Fori(1, NB // 2) as two:
                for par in range(2):
                    parts(two * 2 + par, par, True)

        @block.tensor
        def _(pe):
            def pair(e):
                return slice(e // 2 * P, e // 2 * P + P), slice(e % 2 * R, e % 2 * R + R)

            def turn(u):
                t, row = u.t, u.t - 1
                f, r = u.par, 1 - u.par
                if u.back:
                    pe.wait_ge(rot_k, row + 1)
                    pe.wait_ge(rot_q, row + 1)
                    pe.wait_ge(high, 2 * row + 2)
                    for p in range(NP):
                        ins = pe.matmul(bs[:, p * P:(p + 1) * P], qk[:, r, 0, p * P:(p + 1) * P],
                                        qk[:, r, 1, p * P:(p + 1) * P], start=True, stop=True)
                    ins.then_inc(s_done, 1)
                if u.front:
                    pe.wait_ge(z_parts, t + 1)
                    pe.wait_ge(hot_ready, t + 1)
                    if u.later:
                        pe.wait_ge(rot_k, t)
                    for i in range(NI):
                        for a in range(3):
                            ins = pe.matmul(bx[:], zp[:, f, a, i], hot[:, f, i], start=(i == a == 0), stop=(i == NI - 1 and a == 2))
                    ins.then_inc(x_done, 1)
                    if u.later:
                        pe.wait_ge(v_ready, t)
                    for i in range(NI):
                        for a in range(3):
                            ins = pe.matmul(bt[:], tables[:, i, a], hot[:, f, i], start=(i == a == 0), stop=(i == NI - 1 and a == 2))
                    ins.then_inc(tab_done, 1)
                if u.back:
                    pe.wait_ge(exp_done, row + 1)
                    for p in range(NP):
                        ins = pe.transpose(bs[:, p * P:(p + 1) * P], e[:, p], S.ident[:])
                    ins.then_inc(aT_done, 1)
                if u.front:
                    pe.wait_ge(x_ready, t + 1)
                    for a, (wt, bank) in enumerate((("q", bq), ("k", bk))):
                        for x in range(E):
                            ins = pe.matmul(bank[:, x * R:(x + 1) * R], w[wt][:, x], xT[:, x * R:(x + 1) * R],
                                            start=True, stop=True)
                    ins.then_inc(q_done, 1)
                    for x in range(E):
                        ins = pe.matmul(bx[:, x * R:(x + 1) * R], w["s"][:, x], xT[:, x * R:(x + 1) * R],
                                        start=True, stop=True)
                    ins.then_inc(sw_done, 1)
                if u.back:
                    pe.wait_ge(aT_ready, row + 1)
                    for p in range(NP):
                        ins = pe.matmul(ba[:, p * P:(p + 1) * P], v[:, r, p], aT[:, p], start=True, stop=True)
                    ins.then_inc(av_done, 1)
                if u.front:
                    pe.wait_ge(tab_ready, t + 1)
                    for x in range(E):
                        cols, rows = pair(x)
                        ins = pe.matmul(bt[rows, cols], xT[:, x * R:(x + 1) * R], w["v"][:, x], start=True, stop=True)
                    ins.then_inc(v_done, 1)
                if u.back:
                    pe.wait_ge(av_ready, row + 1)
                    for x in range(E):
                        cols, rows = pair(x)
                        ins = pe.matmul(ba[rows, cols], avT[:, x // 2, rows], w["o"][:, x], start=True, stop=True)
                    ins.then_inc(o_done, 1)
                if u.front:
                    for half in range(2):
                        if half == 0 and u.later:
                            pe.wait_ge(gg_ready, t)
                        if half == 1:
                            pe.wait_ge(hotT_ready, 2 * t + 1)
                        for p in range(2):
                            cols = slice((2 * half + p) * P, (2 * half + p + 1) * P)
                            for i in range(NI):
                                ins = pe.transpose(bh[:, p * 256 + i * 64:p * 256 + (i + 1) * 64].bitcast(BF16),
                                                   hot[:, f, i, cols], S.identb[:])
                        ins.then_inc(hotT_done, 1)
                    pe.wait_ge(hotT_ready, 2 * t + 2)
                    pe.wait_ge(g_parts, t + 1)
                    for p in range(NP):
                        for i in range(NI):
                            ins = pe.matmul(bh[:, p * 32:p * 32 + 3 * E], hot[:, f, i, p * P:(p + 1) * P],
                                            gp[:, f, i].rearrange("p a e -> p (a e)"), start=(i == 0), stop=(i == NI - 1))
                    ins.then_inc(gg_done, 1)
                if u.back:
                    pe.wait_ge(o_parts, row + 1)
                    if u.steady or row > 0:
                        pe.wait_ge(added, row * ADD_STEPS)
                    for i in range(NI):
                        for p in range(NP):
                            for a in range(3):
                                ins = pe.matmul(by[:, i * D:(i + 1) * D], hotT[:, r, p, i * P:(i + 1) * P], op[:, a, p],
                                                start=(p == a == 0), stop=(p == NP - 1 and a == 2))
                    ins.then_inc(y_done, 1)

            turns(pe, turn)

        @block.scalar
        def _(act):
            def turn(u):
                t, row = u.t, u.t - 1
                f, r = u.par, 1 - u.par
                if u.back:
                    act.wait_ge(s_ready, row + 1)
                    if u.steady or row > 0:
                        act.wait_ge(aT_done, row)
                    for p in range(NP):
                        ins = act.activation(e[:, p], s[:, p], ACT.Exp, bias=mx[:, p:p + 1], scale=SCALE,
                                             accum_out=sm[:, p:p + 1])
                    ins.then_inc(exp_done, 1)
                if u.front:
                    act.wait_ge(x_done, t + 1)
                    if u.later:
                        act.wait_ge(v_done, t)
                    act.activation(xT[:], bx[:], ACT.Identity, bias=S.modT[:, 3, bass.ds(t, 1)],
                                   scale=S.modT[:, 4, bass.ds(t, 1)]).then_inc(x_ready, 1)
                    act.wait_ge(tab_done, t + 1)
                    if u.later:
                        act.wait_ge(rot_k, t)
                    act.activation(tab_low[:], bt[H2:P], ACT.Copy)
                    act.activation(tab[:], bt[:], ACT.Copy).then_inc(tab_ready, 1)
                if u.back:
                    act.wait_ge(aT_done, row + 1)
                    if u.steady or row > 0:
                        act.wait_ge(av_done, row)
                    act.activation(aT[:], bs[:].rearrange("p (a k) -> p a k", a=NP), ACT.Copy).then_inc(aT_ready, 1)
                if u.front:
                    act.wait_ge(q_done, t + 1)
                    if u.later:
                        act.wait_ge(s_done, t - 1)
                    for a, bank in enumerate((bq, bk)):
                        act.activation(qk[H2:P, f, a], bank[H2:P], ACT.Copy).then_inc(high, 1)
                if u.back:
                    act.wait_ge(av_done, row + 1)
                    if u.steady or row > 0:
                        act.wait_ge(o_done, row)
                    act.activation(avT[:], ba[:].rearrange("p (a k) -> p a k", a=NP), ACT.Copy).then_inc(av_ready, 1)
                if u.front:
                    act.wait_ge(v_done, t + 1)
                    act.activation(v[:, f], bt[:].rearrange("p (a k) -> p a k", a=NP), ACT.Copy).then_inc(v_ready, 1)
                    for half in range(2):
                        act.wait_ge(hotT_done, 2 * t + half + 1)
                        if half == 0 and u.later:
                            act.wait_ge(y_done, t - 1)
                        act.activation(hotT[:, f, 2 * half:2 * half + 2], bh[:].bitcast(BF16).rearrange(
                            "p (a k) -> p a k", a=2), ACT.Copy).then_inc(hotT_ready, 1)

            turns(act, turn)

        @block.vector
        def _(dve):
            dve.wait_ge(loaded, 48)
            BACK = 7

            def one_hot(row, par, used):
                ranks = rank[:, :, bass.ds(row * E, E)]
                if used:
                    dve.wait_ge(gg_done, row - 1)
                for i in range(NI):
                    ins = dve.tensor_tensor(hot[:, par, i].rearrange("p (e j) -> p e j", e=E), bcast(ranks[:, i], 2, R),
                                            bcast(iota[:], 1, E), ALU.is_equal)
                ins.then_inc(hot_ready, 1)

            def add(row):
                dve.wait_ge(y_done, row + 1)
                ac = Chain(dve, added, row, ADD_STEPS)
                add_and_stats(S, dve, ac, row, 1, by[:].rearrange("p (i f) -> p i f", i=NI))

            def turn(u):
                t, row = u.t, u.t - 1
                f, r = u.par, 1 - u.par
                c = Chain(dve, chain, 0, u.steady)
                c.base = row * BACK
                if u.back:
                    dve.wait_ge(s_done, row + 1)
                    c.link(dve.tensor_tensor(s[:], bs[:].rearrange("p (a k) -> p a k", a=NP), bcast(causal[:], 1, NP), ALU.add))
                    c.link(dve.tensor_reduce(mx[:], s[:], AX.X, ALU.max))
                    dve.tensor_scalar(mx[:], mx[:], -SCALE, None, ALU.mult).then_inc(s_ready, 1)
                if u.end:
                    add(t - 2)
                if u.front:
                    dve.wait_ge(tab_ready, t + 1)
                    dve.wait_ge(q_done, t + 1)
                    dve.tensor_tensor(rot[:, 0, 0], bq[0:H2], tab[0:H2], ALU.mult)
                    dve.tensor_tensor(rot[:, 1, 0], bk[0:H2], tab[0:H2], ALU.mult)
                    dve.wait_ge(sw_done, t + 1)
                    dve.tensor_tensor(rot[:, 0, 1], bx[0:H2], tab_low[:], ALU.mult).then_inc(rotated, 1)
                    dve.tensor_tensor(rot[:, 1, 1], bx[H2:P], tab[H2:P], ALU.mult).then_inc(rotated, 1)
                    dve.wait_ge(rotated, 2 * t + 2)
                    if u.later:
                        dve.wait_ge(s_done, t - 1)
                    dve.tensor_tensor(qk[0:H2, f, 0], rot[:, 0, 0], rot[:, 0, 1], ALU.add).then_inc(rot_q, 1)
                    dve.tensor_tensor(qk[0:H2, f, 1], rot[:, 1, 0], rot[:, 1, 1], ALU.add).then_inc(rot_k, 1)
                if u.back:
                    dve.wait_ge(exp_done, row + 1)
                    c.link(dve.reciprocal(sm[:], sm[:]))
                    c.link(dve.tensor_tensor(sm[:], sm[:], gg[:, r], ALU.mult))
                    dve.wait_ge(o_done, row + 1)
                    for p in range(NP):
                        ins = dve.tensor_scalar(o[:, p], ba[:, p * P:(p + 1) * P], sm[:, p:p + 1], None, ALU.mult)
                    c.link(ins)
                    if u.steady or row > 0:
                        dve.wait_ge(y_done, row)
                    c.link(dve.tensor_copy(op[:, 0], o[:]))
                    c.link(dve.tensor_tensor(o[:], o[:], op[:, 0], ALU.subtract))
                    dve.tensor_copy(op[:, 1], o[:]).then_inc(op1, 1)
                    dve.wait_ge(op1, row + 1)
                    dve.tensor_tensor(o[:], o[:], op[:, 1], ALU.subtract).then_inc(op2, 1)
                    dve.wait_ge(op2, row + 1)
                    dve.tensor_copy(op[:, 2], o[:]).then_inc(o_parts, 1)
                if u.front:
                    dve.wait_ge(gg_done, t + 1)
                    dve.tensor_tensor(ggm[:], bh[:, 0:NP * 32].rearrange("p (a k) -> p a k", a=NP)[:, :, 0:3 * E],
                                      own[:].rearrange("p a b e -> p a (b e)"), ALU.mult).then_inc(gg_ready, 1)
                    dve.wait_ge(gg_ready, t + 1)
                    dve.tensor_reduce(gg[:, f], ggm[:], AX.X, ALU.add).then_inc(gg_sum, 1)
                if u.ahead:
                    one_hot(t + 1, r, u.later)
                assert not u.back or c.n == BACK, c.n

            one_hot(0, 0, False)
            turns(dve, turn)
            add(NB - 1)


def head_attn_stage(S, l):
    nc = S.nc
    H, HD = 16, 8
    K1, M0 = 96, 96
    K2 = M0 + 3
    GH = 4
    W = 10 * P
    COL_Q = {3: 0, 2: 512, 0: 896, 1: 1024}
    COL_K = {0: 0, 1: 512, 3: 896, 2: 1024}
    n = f"L{l}a_"
    sem = lambda s: S.sem(n + s)
    (loaded, cleared, chain, z_ready, zT_done, hT_ready, q_done, q_ready, k_done, k_ready, v_done, v_ready,
     parts_ready, parts_chain, parts_stored) = map(sem, (
         "loaded", "cleared", "dve", "z", "zT", "hT", "q", "qs", "k", "ks", "v", "vs",
         "parts", "parts_chain", "stored"))
    (sA, sB, maxA, maxB, m_ready, mT_done, mT_ready, m_stored, stA, stB, expA, expB, pv_done,
     raw_ready, rawT_done, norm_ready, nT_done, nT_ready, o_done, added) = map(sem, (
         "sA", "sB", "maxA", "maxB", "m", "mT", "mTs", "m_stored", "stA", "stB", "expA", "expB", "pv",
         "raw", "rawT", "norm", "nT", "nTs", "o", "added"))
    pool_cleared = sem("pool_cleared")
    stack_ready = [sem("stack0"), sem("stack1")]
    m_loaded = [sem("m_loaded0"), sem("m_loaded1")]
    scr = nc.dram_tensor(n + "parts_dram", (2, 2, 3, P, T), BF16, kind="Internal").ap()
    scrm = nc.dram_tensor(n + "maxima_dram", (2, 3 * 32, P), BF16, kind="Internal").ap()

    with ExitStack() as ctx:
        sb = lambda name, shape, dt=F32: ctx.enter_context(nc.sbuf_tensor(n + name, shape, dt))
        pt = lambda name, shape, dt=F32: ctx.enter_context(nc.psum_tensor(n + name, shape, dt))
        w = sb("w", [P, 4, D])
        qkb = sb("qkb", [P, 2])
        vob = sb("vob", [P, 2, D])
        mask = sb("mask", [P, T])
        maskT = sb("maskT", [P, P], BF16)
        z = sb("z", [P, NI, D])
        hT = sb("hT", [P, T])
        qk = sb("qk", [P, 2, T])
        rest = sb("rest", [P, 2, T])
        parts = sb("parts", [P, 2, 3, T], BF16)
        qst = sb("qst", [P, 2, H, T], BF16)
        kst = sb("kst", [P, 2, H, T], BF16)
        V = sb("V", [P, 2, NI, H, 32])
        mrow = sb("mrow", [P, H, NI])
        mrest = sb("mrest", [P, 32])
        mpart = sb("mpart", [P, 3, 32], BF16)
        mT = sb("mT", [3 * 32, P], BF16)
        PT = sb("PT", [P, 2, GH, W])
        raw = sb("raw", [P, T])
        rden = sb("rden", [P, NI, GH])
        norm = sb("norm", [P, 2, NI, H, HD])
        nT = sb("nT", [P, T])
        psS = pt("psS", [P, 3 * 512])
        psE = pt("psE", [P, 3 * 512])
        psO = pt("psO", [P, T])
        misc = pt("misc", [P, T])
        block = ctx.enter_context(nc.Block())
        SC = float(HD) ** -0.5

        USES = [(0, "m1", 2, (mT_ready, 2, 2)), (2, "v", 1, (v_ready, 1, 1)), (3, "raw3", 3, (norm_ready, 4, 4)),
                (4, "z", 0, (hT_ready, 1, 1)), (6, "q", 0, (q_ready, 1, 1)), (7, "raw0", 2, (norm_ready, 4, 1)),
                (8, "k", 0, (k_ready, 1, 1)), (9, "m0", 1, (mT_ready, 2, 1)), (10, "norm", 3, (nT_ready, 1, 1)),
                (11, "raw1", 2, (norm_ready, 4, 2)), (12, "out", 3, (added, 1, 1)),
                (15, "raw2", 2, (norm_ready, 4, 3))]
        LOOP0 = 3
        live = lambda t, lag: 0 <= t - lag < NB

        class Turn:

            def __init__(self, t, parity, steady):
                self.t, self.par, self.steady = t, parity, steady
                self.A, self.B, self.C, self.D = (steady or live(t, k) for k in range(4))

            def runs(self, back, lag):
                return self.steady or live(self.t - back, lag)

            def misc_copied_out(self, eng, k):
                for back in (0, 1):
                    for _, _, lag, (sem_, per, at) in reversed(USES[:k] if back == 0 else USES):
                        if self.runs(back, lag):
                            eng.wait_ge(sem_, (self.t - back - lag) * per + at)
                            return

        def turns(eng, body):
            for t in range(LOOP0):
                body(Turn(t, t % 2, False))
            last = LOOP0 + (NB - LOOP0) // 2 * 2
            with eng.Fori(LOOP0, last, 2) as t:
                for u in range(2):
                    body(Turn(t + u, (LOOP0 + u) % 2, True))
            for t in range(last, NB + 3):
                body(Turn(t, t % 2, False))

        @block.sync
        def _(sp):
            for dst, src in ((w, n + "w"), (qkb, n + "qkb"), (mask, "mask"), (maskT, "maskT")):
                sp.dma_start(dst[:], S.dram[src]).then_inc(loaded, 16)
            sp.dma_start(vob[:], S.dram[n + "vob"].partition_broadcast(P)).then_inc(loaded, 16)

            sp.wait_ge(pool_cleared, 1)

            def maxima_rows(row, par, half):
                wait_alone(sp, mT_ready, 2 * row + half + 1)
                wait_alone(sp, m_loaded[half], row * 16)
                sp.dma_start(scrm[half], mT[:]).then_inc(m_stored, 16)
                wait_alone(sp, m_stored, (2 * row + half + 1) * 16)
                sp.dma_start(qst[M0:K2, par, 8 * half:8 * half + 8, :].rearrange("c h t -> c (h t)"),
                             scrm[half].rearrange("(c x) p -> c (x p)", c=3)).then_inc(m_loaded[half], 16)

            def stack_rows(row, par, half):
                h = slice(8 * half, 8 * half + 8)
                src = scr[par].rearrange("a c (d h) t -> a c d h t", d=HD)
                for side, st in ((0, qst), (1, kst)):
                    r = 0
                    for c0, c1, rep in (((0, 1, 3), (1, 2, 2), (2, 3, 1)), ((0, 3, 1), (0, 2, 1), (0, 1, 1)))[side]:
                        for c in range(c0, c1):
                            for _ in range(rep):
                                sp.dma_start(st[r:r + HD, par, h, :], src[side, c, :, h, :]).then_inc(stack_ready[half], 16)
                                r += HD
                    assert r == 6 * HD

            def turn(u):
                t = u.t
                if u.C:
                    maxima_rows(t - 2, u.par, 1)
                if u.A:
                    wait_alone(sp, parts_ready, 2 * (t + 1))
                    if u.C:
                        for half in range(2):
                            wait_alone(sp, stack_ready[half], (t - 1) * 12 * 16)
                    for side in range(2):
                        sp.dma_start(scr[u.par, side].rearrange("c p t -> p c t"), parts[:, side]).then_inc(parts_stored, 16)
                    wait_alone(sp, parts_stored, 32 * (t + 1))
                    if u.C:
                        wait_alone(sp, stB, 16 * (t - 2) + 8)
                    stack_rows(t, u.par, 0)
                if u.B:
                    maxima_rows(t - 1, 1 - u.par, 0)
                if u.A:
                    if u.C:
                        wait_alone(sp, stB, 16 * (t - 2) + 16)
                    stack_rows(t, u.par, 1)

            turns(sp, turn)

        @block.tensor
        def _(pe):
            pe.wait_ge(loaded, 80)

            def max_scores(row, par, h):
                if h % 8 == 0:
                    pe.wait_ge(stack_ready[h // 8], (row + 1) * 12 * 16)
                for i in (3, 2, 0, 1):
                    if i == 3:
                        pe.wait_ge(maxA, 16 * row + h)
                    if i == 2:
                        pe.wait_ge(maxB, 16 * row + h)
                    ins = pe.matmul(psS[:, COL_Q[i]:COL_Q[i] + (i + 1) * P], qst[0:K1, par, h, i * P:(i + 1) * P],
                                    kst[0:K1, par, h, 0:(i + 1) * P], start=True, stop=True)
                    if i in (3, 1):
                        ins.then_inc(sA if i == 3 else sB, 1)

            def exp_scores(row, par, h):
                if h % 8 == 0:
                    pe.wait_ge(m_loaded[h // 8], (row + 1) * 16)
                for i in (0, 1, 3, 2):
                    if i == 0:
                        pe.wait_ge(expA, 16 * row + h)
                    if i == 1:
                        pe.wait_ge(expB, 16 * row + h)
                    c0 = COL_K[i]
                    pe.matmul(psE[:, c0:c0 + (4 - i) * P], kst[0:K2, par, h, i * P:(i + 1) * P],
                              qst[0:K2, par, h, i * P:T], start=True, stop=False, skip_group_check=True)
                    ins = pe.matmul(psE[:, c0:c0 + P], S.identb[:], maskT[:], start=False, stop=True,
                                    skip_group_check=True)
                    if i in (0, 2):
                        ins.then_inc(stA if i == 0 else stB, 1)

            def value_sums(row, par, g):
                pe.wait_ge(expB, 16 * row + 4 * g + 4)
                if g == 0:
                    pe.wait_ge(v_ready, row + 1)
                pe.wait_ge(raw_ready, 4 * row + g)
                for i in range(NI):
                    for j in range(GH):
                        ins = pe.matmul(psO[32 * j:32 * j + 32, i * P:T], V[:, par, i, GH * g + j],
                                        PT[:, g % 2, j, COL_K[i]:COL_K[i] + (4 - i) * P],
                                        start=(i == 0), stop=(i == NI - 1), skip_group_check=True)
                ins.then_inc(pv_done, 1)

            def turn(u):
                t = u.t
                if not u.steady and t == 1:
                    pe.wait_ge(cleared, 2)
                    pe.wait_ge(pool_cleared, 1)
                for s in range(16):
                    if u.B:
                        max_scores(t - 1, 1 - u.par, s)
                    if s == 1 and u.D:
                        value_sums(t - 3, 1 - u.par, 3)
                    if s % 4 == 1 and s > 1 and u.C:
                        value_sums(t - 2, u.par, s // 4 - 1)
                    if u.C:
                        exp_scores(t - 2, u.par, s)
                    for k, (slot, name, lag, _) in enumerate(USES):
                        if slot != s or not u.runs(0, lag):
                            continue
                        u.misc_copied_out(pe, k)
                        row = t - lag
                        if name in ("m0", "m1"):
                            pe.wait_ge(m_ready, 2 * row + int(name[1]) + 1)
                            pe.transpose(misc[0:96, 0:64].bitcast(BF16), mpart[:].rearrange("p c x -> p (c x)"),
                                         S.identb[:]).then_inc(mT_done, 1)
                        elif name == "v":
                            pe.wait_ge(hT_ready, row + 1)
                            for i in range(NI):
                                ins = pe.matmul(misc[:, i * P:(i + 1) * P], hT[:, i * P:(i + 1) * P], w[:, 2],
                                                start=True, stop=True)
                            ins.then_inc(v_done, 1)
                        elif name == "z":
                            pe.wait_ge(z_ready, row + 1)
                            for i in range(NI):
                                ins = pe.transpose(misc[:, i * P:(i + 1) * P], z[:, i], S.ident[:])
                            ins.then_inc(zT_done, 1)
                        elif name in ("q", "k"):
                            pe.wait_ge(hT_ready, row + 1)
                            pe.matmul(misc[:], w[:, "qk".index(name)], hT[:], start=True, stop=True).then_inc(
                                q_done if name == "q" else k_done, 1)
                        elif name[:3] == "raw":
                            pe.wait_ge(raw_ready, 4 * row + int(name[3]) + 1)
                            for i in range(NI):
                                ins = pe.transpose(misc[:, i * P:(i + 1) * P], raw[:, i * P:(i + 1) * P], S.ident[:])
                            ins.then_inc(rawT_done, 1)
                        elif name == "norm":
                            pe.wait_ge(norm_ready, 4 * row + 4)
                            for i in range(NI):
                                ins = pe.transpose(misc[:, i * P:(i + 1) * P],
                                                   norm[:, 1 - u.par, i].rearrange("p h d -> p (h d)"), S.ident[:])
                            ins.then_inc(nT_done, 1)
                        else:
                            pe.wait_ge(nT_ready, row + 1)
                            for i in range(NI):
                                ins = pe.matmul(misc[:, i * P:(i + 1) * P], nT[:, i * P:(i + 1) * P], w[:, 3],
                                                start=True, stop=True)
                            ins.then_inc(o_done, 1)

            turns(pe, turn)

        @block.scalar
        def _(act):
            act.wait_ge(loaded, 80)

            def turn(u):
                t = u.t
                for s in range(16):
                    if s == 2 and u.D:
                        act.wait_ge(pv_done, 4 * (t - 3) + 4)
                        act.wait_ge(rawT_done, 4 * (t - 3) + 3)
                        act.activation(raw[:], psO[:], ACT.Copy).then_inc(raw_ready, 1)
                    if s % 4 == 2 and s > 2 and u.C:
                        g = s // 4 - 1
                        act.wait_ge(pv_done, 4 * (t - 2) + g + 1)
                        act.wait_ge(rawT_done, 4 * (t - 2) + g)
                        act.activation(raw[:], psO[:], ACT.Copy).then_inc(raw_ready, 1)
                    if u.C:
                        row, g, j = t - 2, s // 4, s % 4
                        if j == 0 and (g >= 2 or u.D):
                            act.wait_ge(pv_done, 4 * row + g - 1)
                        act.wait_ge(stA, 16 * row + s + 1)
                        act.activation(PT[:, g % 2, j, 0:512], psE[:, 0:512], ACT.Exp).then_inc(expA, 1)
                        act.wait_ge(stB, 16 * row + s + 1)
                        act.activation(PT[:, g % 2, j, 512:W], psE[:, 512:W], ACT.Exp).then_inc(expB, 1)
                    if s in (0, 9) and (u.C if s == 0 else u.B):
                        row, half = (t - 2, 1) if s == 0 else (t - 1, 0)
                        act.wait_ge(mT_done, 2 * row + half + 1)
                        act.wait_ge(m_stored, (2 * row + half) * 16)
                        act.activation(mT[:], misc[0:96, 0:64].bitcast(BF16), ACT.Copy).then_inc(mT_ready, 1)
                    if s == 4 and u.A:
                        act.wait_ge(zT_done, t + 1)
                        if u.B:
                            act.wait_ge(k_done, t)
                            act.wait_ge(v_done, t)
                        act.activation(hT[:], misc[:], ACT.Identity, bias=S.modT[:, 0, bass.ds(t, 1)],
                                       scale=S.modT[:, 1, bass.ds(t, 1)]).then_inc(hT_ready, 1)
                    if s in (6, 8) and u.A:
                        side = s // 2 - 3
                        act.wait_ge((q_done, k_done)[side], t + 1)
                        act.wait_ge(parts_ready, 2 * t)
                        act.activation(qk[:, side], misc[:], ACT.Identity, bias=qkb[:, side:side + 1],
                                       scale=(SC, 1.0)[side]).then_inc((q_ready, k_ready)[side], 1)
                    if s == 10 and u.D:
                        row = t - 3
                        act.wait_ge(nT_done, row + 1)
                        act.wait_ge(o_done, row)
                        act.activation(nT[:], misc[:], ACT.Copy).then_inc(nT_ready, 1)

            turns(act, turn)

        @block.gpsimd
        def _(pool):
            for st in (qst, kst):
                pool.memset(st[32:64].bitcast(U32), 0)
                ins = pool.memset(st[64:M0].bitcast(U32), 0)
            ins.then_inc(pool_cleared, 1)
            pool.wait_ge(pool_cleared, 1)

            def turn(u):
                if not u.A:
                    return
                t = u.t
                c = Chain(pool, parts_chain, t, 6)
                for side in range(2):
                    f, r, p3 = qk[:, side], rest[:, side], parts[:, side]
                    if u.B and side == 0:
                        pool.wait_ge(parts_stored, 32 * t)
                    wait_alone(pool, (q_ready, k_ready)[side], t + 1)
                    c.link(pool.tensor_scalar(p3[:, 0], f, 1.0, 0.0, ALU.mult, ALU.add))
                    c.link(pool.tensor_tensor(r, f, p3[:, 0], ALU.subtract), alone=True)
                    c.link(pool.tensor_scalar(p3[:, 1], r, 1.0, 0.0, ALU.mult, ALU.add))
                    pool.tensor_tensor(p3[:, 2], r, p3[:, 1], ALU.subtract).then_inc(parts_ready, 1)
                c.end()
            turns(pool, turn)

        @block.vector
        def _(dve):
            dve.wait_ge(loaded, 80)
            c = Chain(dve, chain)
            c.then(dve.tensor_scalar(qkb[:, 0:1], qkb[:, 0:1], SC, None, ALU.mult))
            rstd_step(S, dve, c)
            n0 = c.n
            STEPS = {"A": 0, "B": 6, "C": 3, "D": 1 + ADD_STEPS}

            def chain_before(t):
                return sum(STEPS[x] for k in range(t) for x, lag in zip("ABCD", range(4)) if live(k, lag))

            def turn(u):
                t = u.t
                c = Chain(dve, chain, 0, u.steady)
                c.base = n0 + (chain_before(t) if not u.steady else
                               (t - LOOP0) * sum(STEPS.values()) + chain_before(LOOP0))

                def split_max(row, half):
                    dve.wait_ge(maxB, 16 * row + 8 * half + 8)
                    dve.wait_ge(maxA, 16 * row + 8 * half + 8)
                    if half or u.steady or t > 1:
                        dve.wait_ge(mT_done, 2 * row + half)
                    m = mrow[:, 8 * half:8 * half + 8].rearrange("p h i -> p (h i)")
                    c.link(dve.tensor_scalar(mpart[:, 0], m, -1.0, None, ALU.mult))
                    c.link(dve.scalar_tensor_tensor(mrest[:], m, -1.0, mpart[:, 0], ALU.mult, ALU.subtract))
                    c.link(dve.tensor_copy(mpart[:, 1], mrest[:]))
                    dve.tensor_tensor(mpart[:, 2], mrest[:], mpart[:, 1], ALU.subtract).then_inc(m_ready, 1)

                def divide(row, par, g):
                    dve.wait_ge(rawT_done, 4 * row + g + 1)
                    if g == 0 and (u.steady or t > 3):
                        dve.wait_ge(nT_done, row - 1)
                    tok = misc[:].rearrange("p (i j x) -> p i j x", i=NI, j=GH)
                    c.link(dve.reciprocal(rden[:], tok[:, :, :, HD]))
                    for i in range(NI):
                        ins = dve.tensor_tensor(norm[:, par, i, GH * g:GH * g + GH], tok[:, i, :, 0:HD],
                                                bcast(rden[:, i], 2, HD), ALU.mult)
                    ins.then_inc(norm_ready, 1)

                for s in range(16):
                    if u.B:
                        row = t - 1
                        for i in (3, 2, 0, 1):
                            if i == 3:
                                wait_alone(dve, sA, 16 * row + s + 1)
                            if i == 2:
                                wait_alone(dve, sB, 16 * row + s + 1)
                            ps = psS[:, COL_Q[i]:COL_Q[i] + (i + 1) * P]
                            ins = dve.tensor_tensor_reduce(ps, ps, mask[:, (3 - i) * P:T], 1.0, -3e38, ALU.add,
                                                           ALU.max, mrow[:, s, i:i + 1])
                            if i in (3, 1):
                                ins.then_inc(maxA if i == 3 else maxB, 1)
                        if s in (7, 15):
                            split_max(row, s // 8)
                    if s == 0 and u.A:
                        if u.B:
                            dve.wait_ge(zT_done, t)
                        normalise(S, dve, t, z).then_inc(z_ready, 1)
                    if s == 2 and u.B:
                        row = t - 1
                        dve.wait_ge(v_done, row + 1)
                        if u.D:
                            dve.wait_ge(pv_done, 4 * (t - 3) + 4)
                        c_v = V[:, 1 - u.par, :, :, 0:HD]
                        for i in range(NI):
                            ins = dve.tensor_tensor(c_v[:, i], misc[:, i * P:(i + 1) * P].rearrange(
                                "p (h d) -> p h d", h=H), vob[:, 0].rearrange("p (h d) -> p h d", h=H), ALU.add)
                        ins.then_inc(v_ready, 1)
                    if s == 3 and u.D:
                        divide(t - 3, 1 - u.par, 3)
                    if s in (7, 11, 15) and u.C:
                        divide(t - 2, u.par, s // 4 - 1)
                    if s == 12 and u.D:
                        row = t - 3
                        dve.wait_ge(o_done, row + 1)
                        dve.tensor_tensor(S.upd[:], misc[:].rearrange("p (i f) -> p i f", i=NI),
                                          bcast(vob[:, 1], 1, NI), ALU.add).then_inc(added, 1)
                        dve.wait_ge(added, row + 1)
                        add_and_stats(S, dve, c, row, 0, S.upd[:])
                assert c.n == sum(k for k, on in zip(STEPS.values(), (u.A, u.B, u.C, u.D)) if on)
                if not u.steady and t == 0:
                    dve.memset(V[:], 0.0).then_inc(cleared, 1)
                    dve.wait_ge(cleared, 1)
                    dve.memset(kst[M0:K2].bitcast(U32), 0x3F803F80)
                    dve.memset(V[:, :, :, :, HD:HD + 1], 1.0).then_inc(cleared, 1)

            turns(dve, turn)


def gqa_attn_stage(S):
    nc = S.nc
    H, HD, KV = 16, 64, 4
    PAIRS = H // 2
    W = 10 * P
    COL_Q = {3: 0, 2: 512, 0: 896, 1: 1024}
    COL_K = {0: 0, 1: 512, 3: 896, 2: 1024}
    SC = float(HD) ** -0.5
    n = "L1a_"
    sem = lambda s: S.sem(n + s)
    (loaded, cleared, setup, setup_act, chain, z_ready, zT_done, hT_ready, proj_done, v_ready, kA_ready,
     kB_ready, qA_ready, qD_ready, bias_ready, bias_chain, sA, sB, maxA, maxB, m_ready) = map(sem, (
         "loaded", "cleared", "setup", "setup_act", "dve", "z", "zT", "hT", "proj", "v", "kA",
         "kB", "qA", "qD", "bias", "bias_chain", "sA", "sB", "maxA", "maxB", "m"))
    (exp_done, rsum_ready, p_ready, tA, tB, ptA, ptB, pv_done, outT_ready, o_done) = map(sem, (
        "exp", "rsum", "p", "tA", "tB", "ptA", "ptB", "pv", "outT", "o"))
    with ExitStack() as ctx:
        sb = lambda name, shape, dt=F32: ctx.enter_context(nc.sbuf_tensor(n + name, shape, dt))
        pt = lambda name, shape, dt=F32: ctx.enter_context(nc.psum_tensor(n + name, shape, dt))
        wq = sb("wq", [P, H, HD // 2, 2])
        wr = sb("wr", [P, H, HD // 2, 2])
        wt = sb("wt", [P, H, HD // 2])
        wk = sb("wk", [P, KV, 2, HD])
        wv = sb("wv", [P, KV * HD])
        wo = sb("wo", [P, PAIRS, D])
        ang = sb("ang", [P, 2, H])
        turns_ = sb("angle_turns", [P, 2, H])
        slope = sb("slope", [P, H])
        cneg = sb("cneg", [P, T])
        mask = sb("mask", [P, P])
        z = sb("z", [P, NI, D])
        hT = sb("hT", [P, T])
        q = sb("q", [P, 2, PAIRS, T])
        k = sb("k", [P, 2, 2, KV, T])
        V = sb("V", [P, 2, NI, KV * HD])
        bias = sb("bias", [P, 2, T])
        Pm = sb("Pm", [P, 4, W])
        mrow = sb("mrow", [P, 4, NI])
        mneg = sb("mneg", [P, 4, NI])
        sums = sb("sums", [P, 4, NI])
        rsum = sb("rsum", [P, 4, NI])
        PT = sb("PT", [P, 4, W])
        outT = sb("outT", [P, PAIRS, T])
        psS = pt("psS", [P, 3 * 512])
        psT = pt("psT", [P, 3 * 512])
        psO = pt("psO", [P, T])
        misc = pt("misc", [P, T])
        block = ctx.enter_context(nc.Block())

        USES = [(3, "out", 0, 2, (chain, None, None)), (4, "z", 0, 0, (hT_ready, 1, 1)),
                (5, "v", 0, 0, (v_ready, 2, 1)), (5, "v", 1, 0, (v_ready, 2, 2))]
        USES += [(6 + g, "k", g, 0, (kB_ready, KV, g + 1)) for g in range(KV)]
        USES += [(s, "q", p, 0, ((qA_ready, qD_ready)[p % 2], PAIRS // 2, p // 2 + 1))
                 for p, s in enumerate((10, 11, 12, 12, 13, 13, 14, 15))]
        A_PROJ = 14
        LOOP0 = 2
        live = lambda t, lag: 0 <= t - lag < NB

        class Turn:

            def __init__(self, t, parity, steady):
                self.t, self.par, self.steady = t, parity, steady
                self.A, self.C, self.D = (steady or live(t, lag) for lag in range(3))

            def runs(self, back, lag):
                return self.steady or live(self.t - back, lag)

            def misc_copied_out(self, eng, at):
                for back in (0, 1):
                    for _, name, _, lag, (sem_, per, value) in reversed(USES[:at] if back == 0 else USES):
                        if self.runs(back, lag):
                            if name == "out":
                                eng.wait_ge(outs_read, self.t - back - lag + 1)
                            else:
                                eng.wait_ge(sem_, (self.t - back - lag) * per + value)
                                if name == "k":
                                    eng.wait_ge(kA_ready, (self.t - back - lag) * per + value)
                            return

        outs_read = sem("outs_read")

        def turns(eng, body):
            for t in range(LOOP0):
                body(Turn(t, t % 2, False))
            with eng.Fori(LOOP0 // 2, NB // 2) as pair:
                for u in range(2):
                    body(Turn(pair * 2 + u, u, True))
            for t in range(NB, NB + 2):
                body(Turn(t, t % 2, False))

        @block.sync
        def _(sp):
            for dst, src in ((wq, "wq"), (wk, "wk"), (wv, "wv"), (wo, "wo")):
                sp.dma_start(dst[:], S.dram[n + src]).then_inc(loaded, 16)
            sp.dma_start(cneg[:], S.dram["cneg"]).then_inc(loaded, 16)
            sp.dma_start(mask[:], S.dram["mask"][:, 3 * P:]).then_inc(loaded, 16)
            sp.dma_start(ang[:, 1], S.dram[n + "angle"].partition_broadcast(P)).then_inc(loaded, 16)
            sp.dma_start(slope[:], S.dram[n + "slopes"].partition_broadcast(P)).then_inc(loaded, 16)

        @block.tensor
        def _(pe):
            pe.wait_ge(loaded, 8 * 16)
            pe.wait_ge(setup, 12)
            pe.wait_ge(cleared, 1)

            def scores(t, row, par, h):
                g, pair, odd = h // 4, h // 2, h % 2
                if h % 2 == 0:
                    pe.wait_ge((qA_ready, qD_ready)[pair % 2], PAIRS // 2 * row + pair // 2 + 1)
                if h % 4 == 0:
                    pe.wait_ge(kA_ready, KV * row + g + 1)
                    pe.wait_ge(kB_ready, KV * row + g + 1)
                for i in (3, 2, 0, 1):
                    if i == 3:
                        pe.wait_ge(maxA, 16 * row + h)
                    if i == 2:
                        pe.wait_ge(maxB, 16 * row + h)
                    ins = pe.matmul(psS[:, COL_Q[i]:COL_Q[i] + (i + 1) * P], q[:, par, pair, i * P:(i + 1) * P],
                                    k[:, par, odd, g, 0:(i + 1) * P], start=True, stop=True)
                    if i in (3, 1):
                        ins.then_inc(sA if i == 3 else sB, 1)

            def transposes(G, h):
                pe.wait_ge(p_ready, G + 1)
                for part, tiles in enumerate(((0,), (1, 3, 2))):
                    pe.wait_ge((ptA, ptB)[part], G)
                    for kt in tiles:
                        for i in range(kt, NI):
                            c = COL_K[kt] + (i - kt) * P
                            ins = pe.transpose(psT[:, c:c + P], Pm[:, h % 4, COL_Q[i] + kt * P:COL_Q[i] + (kt + 1) * P],
                                               S.ident[:])
                    ins.then_inc((tA, tB)[part], 1)

            def values(pair_count, row, vpar, pair):
                pe.wait_ge(ptA, 2 * pair_count + 2)
                pe.wait_ge(ptB, 2 * pair_count + 2)
                if pair == 0:
                    pe.wait_ge(v_ready, 2 * row + 2)
                pe.wait_ge(outT_ready, pair_count)
                g = pair // 2
                for kt in range(NI):
                    for j in range(2):
                        ins = pe.matmul(psO[64 * j:64 * j + 64, kt * P:T], V[:, vpar, kt, g * HD:(g + 1) * HD],
                                        PT[:, (2 * pair + j) % 4, COL_K[kt]:COL_K[kt] + (4 - kt) * P],
                                        start=(kt == 0), stop=(kt == NI - 1), skip_group_check=True)
                ins.then_inc(pv_done, 1)

            def use(u, at):
                _, name, x, lag, _ = USES[at]
                if not u.runs(0, lag):
                    return
                u.misc_copied_out(pe, at)
                row = u.t - lag
                if name == "out":
                    pe.wait_ge(outT_ready, PAIRS * (row + 1))
                    for i in range(NI):
                        for p in range(PAIRS):
                            ins = pe.matmul(misc[:, i * P:(i + 1) * P], outT[:, p, i * P:(i + 1) * P], wo[:, p],
                                            start=(p == 0), stop=(p == PAIRS - 1))
                    ins.then_inc(o_done, 1)
                elif name == "z":
                    pe.wait_ge(z_ready, row + 1)
                    for i in range(NI):
                        ins = pe.transpose(misc[:, i * P:(i + 1) * P], z[:, i], S.ident[:])
                    ins.then_inc(zT_done, 1)
                else:
                    pe.wait_ge(hT_ready, row + 1)
                    if name == "v":
                        for i in range(2):
                            t_ = 2 * x + i
                            ins = pe.matmul(misc[:, i * 256:(i + 1) * 256], hT[:, t_ * P:(t_ + 1) * P], wv[:],
                                            start=True, stop=True)
                    elif name == "k":
                        ins = pe.matmul(misc[:], wk[:, x].rearrange("p a d -> p (a d)"), hT[:], start=True, stop=True)
                    else:
                        ins = pe.matmul(misc[:], wr[:, 2 * x:2 * x + 2].rearrange("p h a b -> p (h a b)"), hT[:],
                                        start=True, stop=True)
                    ins.then_inc(proj_done, 1)

            def turn(u):
                for s in range(H):
                    at = [k_ for k_, x in enumerate(USES) if x[0] == s]
                    G = 16 * (u.t - 1) + s
                    if u.C:
                        scores(u.t, u.t - 1, 1 - u.par, s)
                    if len(at) > 1:
                        use(u, at[0])
                    if (u.D if s < 2 else u.C):
                        transposes(G - 2, (s - 2) % H)
                    if s % 2 == 0 and (u.D if s < 4 else u.C):
                        pair = (s // 2 - 2) % PAIRS
                        row = u.t - (2 if s < 4 else 1)
                        values(PAIRS * (u.t - 1) + s // 2 - 2, row, u.par if s < 4 else 1 - u.par, pair)
                    if at:
                        use(u, at[-1])

            turns(pe, turn)

        @block.scalar
        def _(act):
            act.wait_ge(setup, 5)
            act.activation(ang[:], ang[:], ACT.Sin).then_inc(setup_act, 1)
            act.activation(slope[:], slope[:], ACT.Exp).then_inc(setup_act, 1)

            def turn(u):
                t = u.t
                row = t - 1
                for s in range(H):
                    G = 16 * row + s
                    if (u.D if s < 2 else u.C):
                        h = (s - 2) % H
                        act.wait_ge(tA, G - 1)
                        if u.D or s >= 6:
                            act.wait_ge(pv_done, PAIRS * row + s // 2 - 3)
                        act.activation(PT[:, h % 4, 0:512], psT[:, 0:512], ACT.Copy).then_inc(ptA, 1)
                    if u.C:
                        act.wait_ge(m_ready, G + 1)
                        for i in (3, 2, 0, 1):
                            part = Pm[:, s % 4, COL_Q[i]:COL_Q[i] + (i + 1) * P]
                            ins = act.activation(part, part, ACT.Exp, bias=mneg[:, s % 4, i:i + 1],
                                                 accum_out=sums[:, s % 4, i:i + 1])
                        ins.then_inc(exp_done, 1)
                    if not u.A:
                        continue
                    if s == 4:
                        act.wait_ge(zT_done, t + 1)
                        act.wait_ge(proj_done, A_PROJ * t)
                        act.activation(hT[:], misc[:], ACT.Identity, bias=S.modT[:, 0, bass.ds(t, 1)],
                                       scale=S.modT[:, 1, bass.ds(t, 1)]).then_inc(hT_ready, 1)
                    if 6 <= s < 10:
                        act.wait_ge(proj_done, A_PROJ * t + 2 + s - 5)
                        act.activation(k[0:64, u.par, 0, s - 6], misc[0:64], ACT.Copy).then_inc(kA_ready, 1)
                    for slot, name, p, _, _ in USES:
                        if slot == s and name == "q" and p % 2 == 0:
                            act.wait_ge(proj_done, A_PROJ * t + 2 + KV + p + 1)
                            act.activation(q[:, u.par, p], misc[:], ACT.Copy).then_inc(qA_ready, 1)

            turns(act, turn)

        @block.gpsimd
        def _(pool):
            pool.memset(k[64:128, :, 0], 0.0)
            pool.memset(k[0:64, :, 1], 0.0).then_inc(cleared, 1)
            pool.wait_ge(cleared, 1)
            pool.wait_ge(loaded, 8 * 16)
            pool.wait_ge(setup_act, 2)

            def turn(u):
                row = u.t - 1
                for s in range(H):
                    G = 16 * row + s
                    if u.C:
                        if u.D or s >= 2:
                            wait_alone(pool, maxB, G - 1)
                        pool.tensor_scalar(bias[:, s % 2], cneg[:], slope[:, s:s + 1], 0.0, ALU.mult,
                                           ALU.add).then_inc(bias_chain, 1)
                        pool.wait_ge(bias_chain, G + 1)
                        pool.tensor_tensor(bias[:, s % 2, 3 * P:], bias[:, s % 2, 3 * P:], mask[:],
                                           ALU.add).then_inc(bias_ready, 1)
                    if (u.D if s < 1 else u.C):
                        h = (s - 1) % H
                        wait_alone(pool, rsum_ready, G)
                        for i in range(NI):
                            part = Pm[:, h % 4, COL_Q[i]:COL_Q[i] + (i + 1) * P]
                            ins = pool.tensor_scalar(part, part, rsum[:, h % 4, i:i + 1], 1.0, ALU.mult, ALU.mult)
                        ins.then_inc(p_ready, 1)

            turns(pool, turn)

        @block.vector
        def _(dve):
            dve.wait_ge(loaded, 8 * 16)
            c = Chain(dve, setup)
            ROUND = 1.5 * 2.0 ** 23
            TWO_PI_HI = 6.28125
            TWO_PI_LO = 2 * np.pi - 6.28125
            PI = float(np.nextafter(np.float32(np.pi), np.float32(0)))
            c.link(dve.tensor_scalar(ang[:, 0], ang[:, 1], float(np.pi / 2), None, ALU.add))
            c.link(dve.tensor_scalar(turns_[:], ang[:], 1.0 / (2 * np.pi), ROUND, ALU.mult, ALU.add))
            c.link(dve.tensor_scalar(turns_[:], turns_[:], -ROUND, None, ALU.add))
            c.link(dve.scalar_tensor_tensor(ang[:], turns_[:], -TWO_PI_HI, ang[:], ALU.mult, ALU.add))
            c.link(dve.scalar_tensor_tensor(ang[:], turns_[:], -TWO_PI_LO, ang[:], ALU.mult, ALU.add))
            assert c.n == 5
            dve.wait_ge(setup_act, 1)
            c.link(dve.tensor_scalar(ang[:], ang[:], SC, None, ALU.mult))
            cos, sin = (bcast(ang[:, a], 2, HD // 2) for a in range(2))
            c.link(dve.tensor_tensor(wt[:], wq[:, :, :, 1], sin, ALU.mult))
            c.link(dve.tensor_tensor(wr[:, :, :, 0], wq[:, :, :, 0], cos, ALU.mult))
            c.link(dve.tensor_tensor(wr[:, :, :, 0], wr[:, :, :, 0], wt[:], ALU.subtract))
            c.link(dve.tensor_tensor(wt[:], wq[:, :, :, 0], sin, ALU.mult))
            c.link(dve.tensor_tensor(wr[:, :, :, 1], wq[:, :, :, 1], cos, ALU.mult))
            c.link(dve.tensor_tensor(wr[:, :, :, 1], wr[:, :, :, 1], wt[:], ALU.add))
            assert c.n == 12
            c = Chain(dve, chain)
            rstd_step(S, dve, c)
            n0 = c.n

            def turn(u):
                t = u.t
                row = t - 1
                c = Chain(dve, chain, 0, u.steady)
                for s in range(H):
                    G = 16 * row + s
                    if u.C:
                        dve.wait_ge(bias_ready, G + 1)
                        if u.D or s >= 4:
                            dve.wait_ge(tB, G - 3)
                        for i in (3, 2, 0, 1):
                            if i in (3, 2):
                                wait_alone(dve, sA if i == 3 else sB, G + 1)
                            ins = dve.tensor_tensor_reduce(
                                Pm[:, s % 4, COL_Q[i]:COL_Q[i] + (i + 1) * P], psS[:, COL_Q[i]:COL_Q[i] + (i + 1) * P],
                                bias[:, s % 2, (3 - i) * P:T], 1.0, -3e38, ALU.add, ALU.max, mrow[:, s % 4, i:i + 1])
                            if i in (3, 1):
                                ins.then_inc(maxA if i == 3 else maxB, 1)
                        dve.wait_ge(maxB, G + 1)
                        dve.wait_ge(maxA, G + 1)
                        dve.tensor_scalar(mneg[:, s % 4], mrow[:, s % 4], -1.0, None, ALU.mult).then_inc(m_ready, 1)
                    if (u.D if s < 1 else u.C):
                        h = (s - 1) % H
                        dve.wait_ge(exp_done, G)
                        dve.reciprocal(rsum[:, h % 4], sums[:, h % 4]).then_inc(rsum_ready, 1)
                    if (u.D if s < 2 else u.C):
                        h = (s - 2) % H
                        dve.wait_ge(tB, G - 1)
                        if u.D or s >= 6:
                            dve.wait_ge(pv_done, PAIRS * row + s // 2 - 3)
                        dve.tensor_copy(PT[:, h % 4, 512:W], psT[:, 512:W]).then_inc(ptB, 1)
                    if s % 2 == 0 and (u.D if s < 4 else u.C):
                        pair = (s // 2 - 2) % PAIRS
                        dve.wait_ge(pv_done, PAIRS * row + s // 2 - 1)
                        if s == 4 and u.D:
                            dve.wait_ge(o_done, row)
                        dve.tensor_copy(outT[:, pair], psO[:]).then_inc(outT_ready, 1)
                    if s == 3 and u.A:
                        if not (not u.steady and t == 0):
                            dve.wait_ge(zT_done, t)
                        normalise(S, dve, t, z).then_inc(z_ready, 1)
                    if s == 3 and u.D:
                        r = t - 2
                        c.base = n0 + r * (ADD_STEPS - 1)
                        dve.wait_ge(o_done, r + 1)
                        add_and_stats(S, dve, c, r, 0, misc[:].rearrange("p (i f) -> p i f", i=NI), outs_read)
                    if s == 5 and u.A:
                        for x in range(2):
                            dve.wait_ge(proj_done, A_PROJ * t + x + 1)
                            if u.D and x == 0:
                                dve.wait_ge(pv_done, PAIRS * (t - 1))
                            dve.tensor_copy(V[:, u.par, 2 * x:2 * x + 2].rearrange("p i f -> p (i f)"),
                                            misc[:]).then_inc(v_ready, 1)
                    if 6 <= s < 10 and u.A:
                        dve.wait_ge(proj_done, A_PROJ * t + 2 + s - 5)
                        dve.tensor_copy(k[64:128, u.par, 1, s - 6], misc[64:128]).then_inc(kB_ready, 1)
                    for slot, name, p, _, _ in USES:
                        if u.A and slot == s and name == "q" and p % 2:
                            dve.wait_ge(proj_done, A_PROJ * t + 2 + KV + p + 1)
                            dve.tensor_copy(q[:, u.par, p], misc[:]).then_inc(qD_ready, 1)

            turns(dve, turn)


def expert_choice_stage(S):
    nc = S.nc
    E, NG, K = 8, 4, NB * T // 8
    F = int(D * 4 * (2.0 / 3.0))
    NC = 3
    LAST = 96
    n = "L1f_"
    with ExitStack() as ctx:
        sb = lambda name, shape, dt=F32: ctx.enter_context(nc.sbuf_tensor(n + name, shape, dt))
        hT = sb("hT", [P, NB, T])
        prob = sb("prob", [P, E, NT])
        ws = sb("ws", [P, E, NT])
        wu = sb("wu", [P, NG, NC * P])
        wd = sb("wd", [P, NG, NC, 2 * D])
        bu = sb("bu", [P, NG, NC])
        with ExitStack() as inner:
            expert_choice_weights(S, n, inner, hT, prob, wu, wd, bu)
        S.nc.all_engine_barrier()
        with ExitStack() as inner:
            expert_choice_top(S, n, inner, prob, ws, K)
        S.nc.all_engine_barrier()
        with ExitStack() as inner:
            expert_choice_experts(S, n, inner, hT, ws, wu, wd, bu, LAST)


def expert_choice_weights(S, n, ctx, hT, prob, wu, wd, bu):
    nc = S.nc
    E = prob.shape[1]
    small, loaded, chain, z_ready, zT_done, hT_ready, logits_done, logits_read, shifted, exp_done = map(
        lambda s: S.sem(n + s), ("small", "loaded", "dve", "z", "zT", "hT", "logits", "logits_read", "shifted", "exp"))
    sb = lambda name, shape, dt=F32: ctx.enter_context(nc.sbuf_tensor(n + name, shape, dt))
    pt = lambda name, shape, dt=F32: ctx.enter_context(nc.psum_tensor(n + name, shape, dt))
    wr, br = sb("wr", [P, E]), sb("br", [P, E])
    z = sb("z", [P, 2, NI, D])
    mx, sm = sb("mx", [P, NT]), sb("sm", [P, NT])
    psT = pt("psT", [P, 2, T])
    psL = pt("psL", [P, 2, T])
    with nc.Block() as block:
        @block.sync
        def _(sp):
            sp.dma_start(wr[:], S.dram[n + "wr"]).then_inc(small, 16)
            sp.dma_start(br[:], S.dram[n + "br"].partition_broadcast(P)).then_inc(small, 16)
            sp.dma_start(bu[:], S.dram[n + "bu"]).then_inc(loaded, 16)
            for g in range(4):
                sp.dma_start(wu[:, g], S.dram[n + "wu"][:, g]).then_inc(loaded, 16)
                sp.dma_start(wd[:, g], S.dram[n + "wd"][:, g]).then_inc(loaded, 16)
            sp.wait_ge(loaded, 9 * 16)

        @block.tensor
        def _(pe):
            pe.wait_ge(small, 32)

            def transposes(row, par):
                pe.wait_ge(z_ready, row + 1)
                for i in range(NI):
                    ins = pe.transpose(psT[:, par, i * P:(i + 1) * P], z[:, par, i], S.ident[:])
                ins.then_inc(zT_done, 1)

            def logits(row, par):
                pe.wait_ge(hT_ready, row + 1)
                for i in range(NI):
                    ins = pe.matmul(psL[:, par, i * E:(i + 1) * E], hT[:, row, i * P:(i + 1) * P],
                                    wr[:], start=True, stop=True)
                ins.then_inc(logits_done, 1)

            for b in range(NB):
                if b >= 2:
                    pe.wait_ge(hT_ready, b - 1)
                transposes(b, b % 2)
                if b > 0:
                    if b > 2:
                        pe.wait_ge(logits_read, b - 2)
                    logits(b - 1, (b - 1) % 2)
            pe.wait_ge(logits_read, NB - 2)
            logits(NB - 1, (NB - 1) % 2)

        @block.scalar
        def _(act):
            for b in range(NB):
                act.wait_ge(zT_done, b + 1)
                act.activation(hT[:, b], psT[:, b % 2], ACT.Identity, bias=S.modT[:, 3, b:b + 1],
                               scale=S.modT[:, 4, b:b + 1]).then_inc(hT_ready, 1)
            act.wait_ge(shifted, 1)
            act.activation(prob[:], prob[:], ACT.Exp).then_inc(exp_done, 1)

        @block.vector
        def _(dve):
            c = Chain(dve, chain)
            rstd_step(S, dve, c)
            dve.wait_ge(small, 32)

            def take_logits(b):
                dve.wait_ge(logits_done, b + 1)
                dve.tensor_tensor(prob[:, :, b * NI:(b + 1) * NI], psL[:, b % 2, 0:NI * E].rearrange("p (i e) -> p e i", e=E),
                                  bcast(br[:], 2, NI), ALU.add).then_inc(logits_read, 1)

            for b in range(NB):
                if b >= 2:
                    dve.wait_ge(zT_done, b - 1)
                normalise(S, dve, b, z[:, b % 2]).then_inc(z_ready, 1)
                if b >= 2:
                    take_logits(b - 2)
            take_logits(NB - 2)
            take_logits(NB - 1)
            dve.wait_ge(logits_read, NB)
            by_token = prob[:].rearrange("p e t -> p t e")
            c.link(dve.tensor_reduce(mx[:], by_token, AX.X, ALU.max))
            dve.tensor_tensor(prob[:], prob[:], bcast(mx[:], 1, E), ALU.subtract).then_inc(shifted, 1)
            dve.wait_ge(exp_done, 1)
            c.link(dve.tensor_reduce(sm[:], by_token, AX.X, ALU.add))
            c.link(dve.reciprocal(sm[:], sm[:]))
            c.then(dve.tensor_tensor(prob[:], prob[:], bcast(sm[:], 1, E), ALU.mult))


def expert_choice_top(S, n, ctx, prob, ws, K):
    nc = S.nc
    E = prob.shape[1]
    loaded, chain, part_ready, total_done = map(lambda s: S.sem(n + s), ("tri_loaded", "top", "part", "total"))
    sb = lambda name, shape, dt=F32: ctx.enter_context(nc.sbuf_tensor(n + name, shape, dt))
    tri = sb("tri", [P, P])
    v, cand = sb("v", [P, E]), sb("cand", [P, E])
    hit = sb("hit", [P, E, NT])
    eq = sb("eq", [P, E, NT])
    pre = sb("pre", [P, 2, E, NT])
    cnt = sb("cnt", [P, E])
    need = sb("need", [P, E])
    ps = ctx.enter_context(nc.psum_tensor(n + "psN", [P, 512], F32))
    ps2 = ctx.enter_context(nc.psum_tensor(n + "psE", [P, 2, E, NT], F32))
    LEAST = 2.0 ** -126
    EXPONENT = [1.0] + [2.0 ** (1 << k) for k in reversed(range(7))]
    MANTISSA = [2.0 ** -k for k in range(1, 24)]
    ROUNDS = len(EXPONENT) + len(MANTISSA)
    with nc.Block() as block:
        @block.sync
        def _(sp):
            sp.dma_start(tri[:], S.dram[n + "tri"]).then_inc(loaded, 16)

        @block.tensor
        def _(pe):
            for k in range(ROUNDS + 1):
                pe.wait_ge(part_ready, k + 1)
                pe.matmul(ps[:, 0:E], S.ones[:], cnt[:], start=True, stop=True).then_inc(total_done, 1)
            pe.wait_ge(loaded, 16)
            flat = eq[:].rearrange("p e t -> p (e t)")
            pe.matmul(ps2[:, 0].rearrange("p e t -> p (e t)"), tri[:], flat, start=True, stop=True)
            pe.matmul(ps2[:, 1].rearrange("p e t -> p (e t)"), S.ones[:], flat, start=True, stop=True).then_inc(total_done, 1)

        @block.vector
        def _(dve):
            c = Chain(dve, chain)
            rounds = 0

            def count(op, than):
                nonlocal rounds
                c.link(dve.tensor_tensor(hit[:], prob[:], bcast(than, 2, NT), op))
                dve.tensor_reduce(cnt[:], hit[:], AX.X, ALU.add).then_inc(part_ready, 1)
                rounds += 1
                dve.wait_ge(total_done, rounds)

            dve.memset(v[:], 0.0)
            for k, m in enumerate(EXPONENT + MANTISSA):
                if k == 0:
                    c.link(dve.memset(cand[:], LEAST))
                elif k < len(EXPONENT):
                    c.link(dve.tensor_scalar(cand[:], v[:], m, None, ALU.mult))
                else:
                    if k == len(EXPONENT):
                        c.link(dve.tensor_copy(need[:], v[:]))
                    c.link(dve.scalar_tensor_tensor(cand[:], need[:], m, v[:], ALU.mult, ALU.add))
                count(ALU.is_ge, cand[:])
                c.link(dve.scalar_tensor_tensor(cand[:], ps[:, 0:E], K - 0.5, cand[:], ALU.is_ge, ALU.mult))
                c.link(dve.tensor_tensor(v[:], v[:], cand[:], ALU.max))
            c.then(dve.tensor_tensor(eq[:], prob[:], bcast(v[:], 2, NT), ALU.is_equal))
            count(ALU.is_gt, v[:])
            c.link(dve.tensor_scalar(need[:], ps[:, 0:E], -1.0, float(K), ALU.mult, ALU.add))
            dve.wait_ge(total_done, rounds + 1)
            c.link(dve.tensor_copy(pre[:, 0], ps2[:, 1]))
            a, s = 0, 1
            while s < NT:
                c.then(dve.tensor_tensor(pre[:, 1 - a, :, s:], pre[:, a, :, s:], pre[:, a, :, :NT - s], ALU.add))
                c.link(dve.tensor_copy(pre[:, 1 - a, :, :s], pre[:, a, :, :s]))
                a, s = 1 - a, 2 * s
            c.link(dve.tensor_tensor(pre[:, a], pre[:, a], ps2[:, 1], ALU.subtract))
            c.link(dve.tensor_tensor(pre[:, a], pre[:, a], ps2[:, 0], ALU.add))
            c.link(dve.tensor_tensor(pre[:, a], pre[:, a], bcast(need[:], 2, NT), ALU.is_le))
            c.link(dve.tensor_tensor(pre[:, a], pre[:, a], eq[:], ALU.mult))
            c.link(dve.tensor_tensor(hit[:], hit[:], pre[:, a], ALU.add))
            c.then(dve.tensor_tensor(ws[:], hit[:], prob[:], ALU.mult))


def expert_choice_experts(S, n, ctx, hT, ws, wu, wd, bu, LAST):
    nc = S.nc
    NG, NC = wd.shape[1], wd.shape[2]
    ones_ready, chain, up_done, mid_ready, down_done, used, chain2 = map(
        lambda s: S.sem(n + s), ("ones", "sum", "up", "mid", "down", "used", "added"))
    sb = lambda name, shape, dt=F32: ctx.enter_context(nc.sbuf_tensor(n + name, shape, dt))
    pt = lambda name, shape, dt=F32: ctx.enter_context(nc.psum_tensor(n + name, shape, dt))
    mid = sb("mid", [P, 2, NC, T])
    y = sb("y", [P, NI, D])
    psU = pt("psU", [P, NC, T])
    psO = pt("psO", [P, 2, NI, 2 * D])
    with nc.Block() as block:
        @block.gpsimd
        def _(pool):
            pool.memset(mid[LAST:P, :, NC - 1], 1.0).then_inc(ones_ready, 1)

        @block.tensor
        def _(pe):
            def up(row, g):
                s = row * NG + g
                for c in range(NC):
                    if not isinstance(s, int) or s > 0:
                        pe.wait_ge(mid_ready, NC * (s - 1) + c + 1)
                    m = P if c < NC - 1 else LAST
                    pe.matmul(psU[0:m, c], wu[:, g, c * P:c * P + m], hT[:, bass.ds(row, 1)].squeeze(1),
                              start=True, stop=True).then_inc(up_done, 1)

            def down(row, g):
                s = row * NG + g
                if not isinstance(s, int) or s >= 2:
                    pe.wait_ge(used, s - 1)
                pe.wait_ge(mid_ready, NC * s + NC)
                for i in range(NI):
                    for c in range(NC):
                        ins = pe.matmul(psO[:, g % 2, i], mid[:, g % 2, c, i * P:(i + 1) * P], wd[:, g, c],
                                        start=(c == 0), stop=(c == NC - 1))
                ins.then_inc(down_done, 1)

            pe.wait_ge(ones_ready, 1)
            up(0, 0)
            for g in range(NG):
                up((g + 1) // NG, (g + 1) % NG)
                down(0, g)
            with pe.Fori(1, NB - 1) as b:
                for g in range(NG - 1):
                    up(b, g + 1)
                    down(b, g)
                up(b + 1, 0)
                down(b, NG - 1)
            for g in range(NG):
                if g + 1 < NG:
                    up(NB - 1, g + 1)
                down(NB - 1, g)

        @block.scalar
        def _(act):
            def row(b):
                for g in range(NG):
                    s = b * NG + g
                    for c in range(NC):
                        act.wait_ge(up_done, NC * s + c + 1)
                        if c == 0 and (not isinstance(s, int) or s >= 2):
                            act.wait_ge(down_done, s - 1)
                        m = P if c < NC - 1 else LAST
                        act.activation(mid[0:m, g % 2, c], psU[0:m, c], ACT.Silu,
                                       bias=bu[0:m, g, c:c + 1]).then_inc(mid_ready, 1)
            row(0)
            with act.Fori(1, NB) as b:
                row(b)

        @block.vector
        def _(dve):
            with dve.Fori(0, NB) as b:
                c = Chain(dve, chain, b, NG)
                for g in range(NG):
                    dve.wait_ge(down_done, b * NG + g + 1)
                    for k in range(2):
                        for i in range(NI):
                            w = ws[:, 2 * g + k, bass.ds(b * NI + i, 1)]
                            out = psO[:, g % 2, i, k * D:(k + 1) * D]
                            if g == k == 0:
                                ins = dve.tensor_scalar(y[:, i], out, w, None, ALU.mult)
                            else:
                                ins = dve.scalar_tensor_tensor(y[:, i], out, w, y[:, i], ALU.mult, ALU.add)
                        if k == 0:
                            c.link(ins)
                        else:
                            ins.then_inc(used, 1)
                            dve.wait_ge(used, b * NG + g + 1)
                c.end()
                ac = Chain(dve, chain2, b, ADD_STEPS)
                add_and_stats(S, dve, ac, b, 1, y[:])
                ac.end()


def moe_stage(S, l):
    nc = S.nc
    gated = l == 3
    E = 16 if gated else 8
    NC = 9 if gated else 32
    PER = 1 if gated else 4
    SCALED = 8 if gated else 32
    NH = 3 if gated else 4
    NU = 2
    SLOT = dict(y=3, z=4, logits=5, c=8) if gated else dict(y=3, z=5, logits=7, c=15, c2=17)
    ROUTE = (5, 5, 6, 6, 7, 7) if gated else (7, 8, 9, 10, 11, 12)
    FINISH = () if gated else (3, 18, 19, 20, 21, 22, 23, 24, 25, 26, 27)
    n = f"L{l}f_"
    sem = lambda s: S.sem(n + s)
    (loaded, bias_loaded, chain, z_ready, zT_done, hT_ready, logits_done, logits_read, pair_ready, pair_exp,
     c_ready, cT_done, cT_ready, cb_done, up_done, g_ready, h_ready, down_done, yS_ready, yT_done, y_read,
     c2_done, c2_ready, hstep) = map(sem, (
         "loaded", "bias_loaded", "dve", "z", "zT", "hT", "logits", "logits_read", "pair", "pair_exp",
         "c", "cT", "cTs", "cb", "up", "g", "h", "down", "yS", "yT", "y_read", "c2", "c2s", "hstep"))

    def dist(k, bufs):
        return bufs if k >= bufs else k + NC - max(j for j in range(NC) if j % bufs == k % bufs)

    with ExitStack() as ctx:
        sb = lambda name, shape, dt=F32: ctx.enter_context(nc.sbuf_tensor(n + name, shape, dt))
        pt = lambda name, shape, dt=F32: ctx.enter_context(nc.psum_tensor(n + name, shape, dt))
        wu = sb("wu", [P, 2 if gated else 1, NC, P])
        wd = sb("wd", [P, NC, D])
        wr = sb("wr", [P, E])
        rb = sb("rb", [P, E])
        iota = sb("iota", [P, E])
        sel = sb("sel", [3 * E, SCALED // PER, P], BF16)
        z = sb("z", [P, NI, D])
        hT = sb("hT", [P, 2, T])
        logit = sb("logit", [P, NI, E])
        top = sb("top", [P, NI, 8])
        idx = sb("idx", [P, NI, 8], U32)
        idxf = sb("idxf", [P, NI, 2])
        pair = sb("pair", [P, NI, 2])
        den = sb("den", [P, NI])
        hot = sb("hot", [P, 2, NI, E])
        cw = sb("cw", [P, NI, E])
        crest = sb("crest", [P, NI, E])
        c3 = sb("c3", [P, NI, 3, E], BF16)
        c3T = sb("c3T", [3 * E, 2, T], BF16)
        g = sb("g", [P, 3, T])
        h = sb("h", [P, NH, T])
        yS = sb("yS", [P, T])
        psU = pt("psU", [P, NU, T])
        psG = pt("psG", [P, NU, T]) if gated else None
        psC = pt("psC", [P, 2, T])
        psY = pt("psY", [P, T])
        misc = pt("misc", [P, T])
        if not gated:
            b1 = sb("b1", [P, NC])
            b2 = sb("b2", [E, D])
            cT = sb("cT", [E, 2, T])
            lnp = sb("lnp", [P, 2, D])
            y = sb("y", [P, NI, D])
            ymv = sb("ymv", [P, NI, 2])
            yr = sb("yr", [P, 3, NI])
        block = ctx.enter_context(nc.Block())

        USES = [("y", 2, y_read), ("z", 0, hT_ready), ("logits", 0, logits_read), ("c", 0, cT_ready)]
        if not gated:
            USES.append(("c2", 0, c2_ready))
        LOOP0 = 2
        live = lambda t, lag: 0 <= t - lag < NB

        class Turn:

            def __init__(self, t, parity, steady):
                self.t, self.par, self.steady = t, parity, steady
                self.A, self.C, self.D = (steady or live(t, lag) for lag in range(3))

            def runs(self, back, lag):
                return self.steady or live(self.t - back, lag)

            def misc_copied_out(self, eng, at):
                for back in (0, 1):
                    for _, lag, sem_ in reversed(USES[:at] if back == 0 else USES):
                        if self.runs(back, lag):
                            eng.wait_ge(sem_, self.t - back - lag + 1)
                            return

        def turns(eng, body):
            for t in range(LOOP0):
                body(Turn(t, t % 2, False))
            with eng.Fori(LOOP0 // 2, NB // 2) as two:
                for u in range(2):
                    body(Turn(two * 2 + u, u, True))
            for t in range(NB, NB + 2):
                body(Turn(t, t % 2, False))

        @block.sync
        def _(sp):
            for dst, src in ((wr[:], n + "wr"), (rb[:], n + "rb"), (iota[:], n + "iota"), (sel[:], n + "sel")):
                s = S.dram[src]
                sp.dma_start(dst, s.partition_broadcast(P) if src == n + "rb" else s).then_inc(bias_loaded, 16)
            if not gated:
                sp.dma_start(b1[:], S.dram[n + "b1"]).then_inc(bias_loaded, 16)
                sp.dma_start(b2[:], S.dram[n + "b2"]).then_inc(bias_loaded, 16)
                sp.dma_start(lnp[:], S.dram[n + "lnp"].partition_broadcast(P)).then_inc(bias_loaded, 16)
            parts = 1 if gated else 8
            for p in range(parts):
                ks = slice(p * NC // parts, (p + 1) * NC // parts)
                sp.dma_start(wu[:, :, ks], S.dram[n + "wu"][:, :, ks]).then_inc(loaded, 16)
                sp.dma_start(wd[:, ks], S.dram[n + "wd"][:, ks]).then_inc(loaded, 16)
        SMALL = 4 * 16 if gated else 7 * 16
        LARGE = 2 * 16 if gated else 16 * 16

        @block.tensor
        def _(pe):
            pe.wait_ge(bias_loaded, SMALL)

            def weights_to_all(row, rpar, x):
                if x == 0:
                    pe.wait_ge(cT_ready, row + 1)
                last = PER * (x - 2) + PER
                if x >= 2:
                    pe.wait_ge(h_ready, NC * row + last)
                else:
                    pe.wait_ge(h_ready, NC * row)
                pe.matmul(psC[:, x % 2], sel[:, x], c3T[:, rpar], start=True, stop=True).then_inc(cb_done, 1)

            def up(row, rpar, k):
                d = dist(k, NU)
                sem_ = h_ready if gated else g_ready
                if not (isinstance(row, int) and NC * row + k - d + 1 < 0):
                    pe.wait_ge(sem_, NC * row + k - d + 1)
                if gated:
                    pe.matmul(psG[:, k % NU], wu[:, 0, k], hT[:, rpar], start=True, stop=True)
                pe.matmul(psU[:, k % NU], wu[:, 1 if gated else 0, k], hT[:, rpar], start=True, stop=True).then_inc(up_done, 1)

            def down(row, rpar, k):
                if k == 0:
                    pe.wait_ge(yS_ready, row)
                    if not gated:
                        pe.wait_ge(c2_ready, row + 1)
                        pe.matmul(psY[:], b2[:], cT[:, rpar], start=True, stop=False, skip_group_check=True)
                pe.wait_ge(h_ready, NC * row + k + 1)
                pe.matmul(psY[:], wd[:, k], h[:, k % NH], start=(gated and k == 0), stop=(k == NC - 1),
                          skip_group_check=True).then_inc(down_done, 1)

            def use(u, at):
                name, lag, _ = USES[at]
                if not u.runs(0, lag):
                    return
                u.misc_copied_out(pe, at)
                row = u.t - lag
                if name == "y":
                    pe.wait_ge(yS_ready, row + 1)
                    for i in range(NI):
                        ins = pe.transpose(misc[:, i * P:(i + 1) * P], yS[:, i * P:(i + 1) * P], S.ident[:])
                    ins.then_inc(yT_done, 1)
                elif name == "z":
                    pe.wait_ge(z_ready, row + 1)
                    for i in range(NI):
                        ins = pe.transpose(misc[:, i * P:(i + 1) * P], z[:, i], S.ident[:])
                    ins.then_inc(zT_done, 1)
                elif name == "logits":
                    pe.wait_ge(hT_ready, row + 1)
                    for i in range(NI):
                        ins = pe.matmul(misc[:, i * E:(i + 1) * E], hT[:, u.par, i * P:(i + 1) * P], wr[:],
                                        start=True, stop=True)
                    ins.then_inc(logits_done, 1)
                elif name == "c":
                    wait_alone(pe, c_ready, row + 1)
                    for i in range(NI):
                        ins = pe.transpose(misc[0:3 * E, i * 64:(i + 1) * 64].bitcast(BF16),
                                           c3[:, i].rearrange("p a e -> p (a e)"), S.identb[:])
                    ins.then_inc(cT_done, 1)
                else:
                    for i in range(NI):
                        ins = pe.transpose(misc[0:E, i * P:(i + 1) * P], cw[:, i], S.ident[:])
                    ins.then_inc(c2_done, 1)

            def turn(u):
                for k in range(NC):
                    if k < 2 and u.D:
                        down(u.t - 2, u.par, NC - 2 + k)
                    if u.C:
                        if k == 0 and not u.steady and u.t == 1:
                            pe.wait_ge(loaded, LARGE)
                        if k % PER == 0 and k < SCALED:
                            weights_to_all(u.t - 1, 1 - u.par, k // PER)
                        up(u.t - 1, 1 - u.par, k)
                        if k >= 2:
                            down(u.t - 1, 1 - u.par, k - 2)
                    for at, (name, _, _) in enumerate(USES):
                        if SLOT[name] == k:
                            use(u, at)

            turns(pe, turn)

        @block.scalar
        def _(act):
            def turn(u):
                t = u.t
                for k in range(NC):
                    if u.C:
                        G = NC * (t - 1) + k
                        act.wait_ge(up_done, G + 1)
                        if u.D or k >= 3:
                            act.wait_ge(h_ready, G - dist(k, 3) + 1)
                        if gated:
                            act.activation(g[:, k % 3], psG[:, k % NU], ACT.Silu).then_inc(g_ready, 1)
                        else:
                            act.activation(g[:, k % 3], psU[:, k % NU], ACT.Gelu, bias=b1[:, k:k + 1]).then_inc(g_ready, 1)
                    if k == 2 and u.D and gated:
                        act.wait_ge(down_done, NC * (t - 1))
                        act.wait_ge(yT_done, t - 2)
                        act.activation(yS[:], psY[:], ACT.Copy).then_inc(yS_ready, 1)
                    if not u.A:
                        continue
                    if k == SLOT["z"]:
                        act.wait_ge(zT_done, t + 1)
                        if u.D:
                            act.wait_ge(up_done, NC * (t - 1))
                            act.wait_ge(yS_ready, t - 1)
                        act.activation(hT[:, u.par], misc[:], ACT.Identity, bias=S.modT[:, 3, bass.ds(t, 1)],
                                       scale=S.modT[:, 4, bass.ds(t, 1)]).then_inc(hT_ready, 1)
                    if k == SLOT["logits"] + 1:
                        act.wait_ge(pair_ready, t + 1)
                        act.activation(pair[:, :, 1], pair[:, :, 1], ACT.Exp).then_inc(pair_exp, 1)
                    if k == SLOT["c"]:
                        act.wait_ge(cT_done, t + 1)
                        if u.D:
                            act.wait_ge(cb_done, SCALED // PER * (t - 1))
                        act.activation(c3T[:, u.par], misc[0:3 * E, 0:256].bitcast(BF16), ACT.Copy).then_inc(cT_ready, 1)
                    if not gated and k == SLOT["c2"]:
                        act.wait_ge(c2_done, t + 1)
                        if u.D:
                            act.wait_ge(down_done, NC * (t - 2) + 1)
                        act.activation(cT[:, u.par], misc[0:E], ACT.Copy).then_inc(c2_ready, 1)

            turns(act, turn)

        @block.vector
        def _(dve):
            dve.wait_ge(bias_loaded, SMALL)
            c = Chain(dve, chain)
            rstd_step(S, dve, c)
            n0 = c.n
            A_STEPS = 13
            D_STEPS = ADD_STEPS - 1 if gated else ADD_STEPS + RSQRT_STEPS + 6

            def finish(u, c, piece):
                row = u.t - 2
                if piece == 0:
                    dve.wait_ge(yT_done, row + 1)
                    dve.tensor_copy(y[:], misc[:].rearrange("p (i f) -> p i f", i=NI)).then_inc(y_read, 1)
                    wait_alone(dve, y_read, row + 1)
                elif piece == 1:
                    for i in range(NI):
                        ins = dve.bn_stats(S.bn[:, 1, i], y[:, i])
                    c.link(ins, alone=True)
                elif piece == 2:
                    for i in range(NI):
                        ins = dve.bn_aggr(ymv[:, i], S.bn[:, 1, i])
                    c.link(ins)
                    c.link(dve.tensor_copy(yr[:, 0], ymv[:, :, 1]))
                    rsqrt_guess(dve, c, yr[:, 1], yr[:, 0], 1.0, LN_EPS)
                elif piece <= 6:
                    rsqrt_newton(dve, c, yr[:, 1], yr[:, 0], yr[:, 2])
                elif piece == 7:
                    for i in range(NI):
                        ins = dve.tensor_scalar(y[:, i], y[:, i], ymv[:, i, 0:1], yr[:, 1, i:i + 1],
                                                ALU.subtract, ALU.mult)
                    c.link(ins)
                elif piece == 8:
                    c.link(dve.tensor_tensor(y[:], y[:], bcast(lnp[:, 0], 1, NI), ALU.mult))
                elif piece == 9:
                    c.link(dve.tensor_tensor(y[:], y[:], bcast(lnp[:, 1], 1, NI), ALU.add))
                else:
                    add_and_stats(S, dve, c, row, 1, y[:])

            def route(u, c, piece):
                t = u.t
                former = u.steady or t > 0
                if piece == 0:
                    dve.wait_ge(logits_done, t + 1)
                    if former:
                        dve.wait_ge(c_ready, t)
                    dve.tensor_tensor(logit[:], misc[:, 0:NI * E].rearrange("p (i e) -> p i e", i=NI),
                                      bcast(rb[:], 1, NI), ALU.add).then_inc(logits_read, 1)
                    wait_alone(dve, logits_read, t + 1)
                    for i in range(NI):
                        ins = dve.max(top[:, i], logit[:, i])
                    c.link(ins, alone=True)
                elif piece == 1:
                    for i in range(NI):
                        ins = dve.max_index(idx[:, i], top[:, i], logit[:, i])
                    c.link(ins)
                    dve.tensor_tensor(pair[:, :, 1], top[:, :, 1], top[:, :, 0], ALU.subtract).then_inc(pair_ready, 1)
                elif piece == 2:
                    c.link(dve.tensor_copy(idxf[:], idx[:, :, 0:2]))
                    for a in range(2):
                        ins = dve.tensor_tensor(hot[:, a], bcast(iota[:], 1, NI), bcast(idxf[:, :, a], 2, E),
                                                ALU.is_equal)
                    c.link(ins)
                elif piece == 3:
                    dve.wait_ge(pair_exp, t + 1)
                    c.link(dve.tensor_scalar(den[:], pair[:, :, 1], 1.0, None, ALU.add))
                    c.link(dve.reciprocal(pair[:, :, 0], den[:]))
                    c.link(dve.tensor_tensor(pair[:, :, 1], pair[:, :, 1], pair[:, :, 0], ALU.mult))
                elif piece == 4:
                    if former:
                        dve.wait_ge(cT_done if gated else c2_done, t)
                    for a in range(2):
                        ins = dve.tensor_tensor(hot[:, a], hot[:, a], bcast(pair[:, :, a], 2, E), ALU.mult)
                    c.link(ins)
                    c.link(dve.tensor_tensor(cw[:], hot[:, 0], hot[:, 1], ALU.add))
                    c.link(dve.tensor_copy(c3[:, :, 0], cw[:]))
                else:
                    c.link(dve.tensor_tensor(crest[:], cw[:], c3[:, :, 0], ALU.subtract))
                    c.link(dve.tensor_copy(c3[:, :, 1], crest[:]))
                    c.link(dve.tensor_tensor(crest[:], crest[:], c3[:, :, 1], ALU.subtract))
                    dve.tensor_copy(c3[:, :, 2], crest[:]).then_inc(c_ready, 1)

            def turn(u):
                t = u.t
                c = Chain(dve, chain, 0, u.steady)
                c.base = n0 + (t * A_STEPS if u.A else NB * A_STEPS) + ((t - 2) * D_STEPS if u.D else 0)
                steps = (A_STEPS if u.A else 0) + (D_STEPS if u.D else 0)

                for k in range(NC):
                    if u.C:
                        G = NC * (t - 1) + k
                        dve.wait_ge(g_ready, G + 1)
                        if u.D or k >= NH:
                            dve.wait_ge(down_done, G - dist(k, NH) + 1)
                        hk = h[:, k % NH]
                        if gated:
                            ins = dve.tensor_tensor(hk, g[:, k % 3], psU[:, k % NU], ALU.mult)
                            if k < SCALED:
                                ins.then_inc(hstep, 1)
                                dve.wait_ge(hstep, SCALED * (t - 1) + k + 1)
                        if k < SCALED:
                            if k % PER == 0:
                                dve.wait_ge(cb_done, SCALED // PER * (t - 1) + k // PER + 1)
                            ins = dve.tensor_tensor(hk, hk if gated else g[:, k % 3], psC[:, k // PER % 2], ALU.mult)
                        ins.then_inc(h_ready, 1)
                    if k == 0 and u.A:
                        if u.steady or t > 0:
                            dve.wait_ge(zT_done, t)
                        normalise(S, dve, t, z).then_inc(z_ready, 1)
                    if k == 2 and u.D and not gated:
                        dve.wait_ge(down_done, NC * (t - 1))
                        dve.wait_ge(yT_done, t - 2)
                        dve.tensor_tensor(yS[:], psY[:], hT[:, u.par], ALU.add).then_inc(yS_ready, 1)
                    if u.A:
                        for piece, slot in enumerate(ROUTE):
                            if k == slot:
                                route(u, c, piece)
                    if u.D:
                        if gated and k == SLOT["y"]:
                            dve.wait_ge(yT_done, t - 1)
                            add_and_stats(S, dve, c, t - 2, 1, misc[:].rearrange("p (i f) -> p i f", i=NI), y_read)
                        for piece, slot in enumerate(FINISH):
                            if k == slot:
                                finish(u, c, piece)
                assert c.n == steps, (c.n, steps)

            turns(dve, turn)


def store_stage(S):
    nc = S.nc
    stored = nc.alloc_semaphore("stored")
    with nc.Block() as block:
        @block.sync
        def _(sp):
            for b in range(NB):
                sp.dma_start(S.dram["out"][b].rearrange("(i p) f -> p i f", p=P), S.x[:, b * NI:(b + 1) * NI]).then_inc(stored, 16)
            sp.wait_ge(stored, NB * 16)


def run_stage(S, stage, *args):
    nc = S.nc
    S.sems = []
    stage(S, *args)
    nc.clear_and_free_semaphores(S.sems)
    nc.all_engine_barrier()


def program(nc, dram, stages):
    S = State()
    S.nc, S.dram = nc, dram
    for eng in (nc.vector, nc.gpsimd, nc.tensor, nc.sync):
        State.passed[eng.engine] = nc.alloc_semaphore(f"waits_passed_{eng.engine.name}")
    al = nc.alloc_sbuf_tensor
    S.x = al("x", [P, NT, D], F32)
    S.ident = al("ident", [P, P], F32)
    S.identb = al("identb", [P, P], BF16)
    S.ones = al("ones", [P, P], F32)
    S.bn = al("bn", [P, NB, NI, 6], F32)
    S.mv = al("mv", [P, NT, 2], F32)
    S.mv4 = al("mv4", [P, NI, 2], F32)
    S.var = al("var", [P, NT], F32)
    S.rstd = al("rstd", [P, NT], F32)
    S.nwt = al("nwt", [P, NT], F32)
    S.modT = al("modT", [P, 6, NB], F32)
    S.gate = al("gate", [P, 2, NB, D], F32)
    S.upd = al("upd", [P, NI, D], F32)
    setup_stage(S)
    parts = [l0_attn_stage, token_choice_stage, gqa_attn_stage, expert_choice_stage, lambda S: head_attn_stage(S, 2),
             lambda S: moe_stage(S, 2), lambda S: head_attn_stage(S, 3), lambda S: moe_stage(S, 3)]
    for k, part in enumerate(parts):
        if k in stages:
            if k % 2 == 0 or k == stages[0]:
                run_stage(S, mod_stage, k // 2)
            run_stage(S, part)
    store_stage(S)


def swap_pairs(w):
    return w.reshape(w.shape[0], -1, 2)[:, :, ::-1].reshape(w.shape)


def layouts(i):
    bf16 = np.dtype("bfloat16")
    f32 = np.float32
    out = {"x": i["L0_attn_x"], "ident": np.eye(P, dtype=f32), "identb": np.eye(P, dtype=bf16)}
    for l in range(4):
        out[f"L{l}_wmod"] = i[f"L{l}_wmod"]
        out[f"L{l}_cT"] = i[f"L{l}_c"].T
    q, k, v, o = (i["L0_attn_W" + c] for c in "qkvo")
    out["L0a_w"] = np.stack([q, swap_pairs(q), k, swap_pairs(k), v, o], 1)
    inv = (1.0 / 10000.0 ** (np.arange(0, 8, 2, dtype=f32) / f32(8))).astype(f32)
    fr = np.repeat(np.arange(T, dtype=f32)[:, None] * inv[None], 2, 1)
    sign = np.tile(np.array([-1, 1], f32), 4)
    cs = np.stack([np.tile(np.cos(fr), (1, 16)), np.tile(np.sin(fr) * sign, (1, 16))], 1)
    out["L0a_rope"] = cs.reshape(NI, P, 2, D).transpose(1, 0, 2, 3)
    out["L0a_lam"] = np.stack([i["L0_attn_lambda_" + c] for c in ("q1", "k1", "q2", "k2")])
    out["L0a_ln"] = np.stack([i["L0_attn_ln_w"], i["L0_attn_ln_b"]], 1)
    in_pos = lambda w: np.concatenate([np.zeros_like(w), w], 0)
    out["L1a_wq"] = in_pos(i["L1_attn_Wq"].T).reshape(P, 16, 32, 2)
    out["L1a_wk"] = np.repeat(in_pos(i["L1_attn_Wk"].T).reshape(P, 4, 1, 64), 2, 2)
    out["L1a_wv"] = np.concatenate([i["L1_attn_Wv"].T, np.zeros((64, 256), f32)], 0)
    out["L1a_wo"] = i["L1_attn_Wo"].T.reshape(8, P, D).transpose(1, 0, 2)
    out["L1a_angle"] = i["L1_attn_q_phase_angle"]
    out["L1a_slopes"] = i["L1_attn_alibi_log_slopes"]
    out["cneg"] = np.tile(-np.arange(T, dtype=f32), (P, 1))
    def part_rows(E, sets, experts):
        s = np.zeros((3, E, sets, P), bf16)
        for x in range(sets):
            for j in range(experts):
                s[:, x * experts + j, x, j * P // experts:(j + 1) * P // experts] = 1
        return s.reshape(3 * E, sets, P)
    out["iota"] = np.tile(np.arange(16, dtype=f32), (P, 1))
    out["L2f_iota"] = out["iota"][:, :8]
    out["L3f_iota"] = out.pop("iota")
    out["L2f_wu"] = i["L2_ffn_W1"].transpose(1, 0, 2).reshape(P, 1, 32, P)
    out["L2f_wd"] = i["L2_ffn_W2"].reshape(32, P, D).transpose(1, 0, 2)
    out["L2f_wr"] = i["L2_ffn_Wg"]
    out["L2f_rb"] = i["L2_ffn_bg"]
    out["L2f_sel"] = part_rows(8, 8, 1)
    out["L2f_b1"] = i["L2_ffn_b1"].reshape(32, P).T
    out["L2f_b2"] = i["L2_ffn_b2"]
    out["L2f_lnp"] = np.stack([i["L2_ffn_gamma"], i["L2_ffn_beta"]])
    two = lambda w: w.transpose(1, 0, 2).reshape(P, 8, P)
    gate = np.concatenate([two(i["L3_ffn_gate_proj"]), i["L3_ffn_sh_gate"].T[:, None]], 1)
    up = np.concatenate([two(i["L3_ffn_up_proj"]), i["L3_ffn_sh_up"].T[:, None]], 1)
    out["L3f_wu"] = np.stack([gate, up], 1)
    out["L3f_wd"] = np.concatenate([i["L3_ffn_down_proj"].reshape(8, P, D).transpose(1, 0, 2),
                                    i["L3_ffn_sh_down"].T[:, None]], 1)
    out["L3f_wr"] = i["L3_ffn_router_w"].T
    out["L3f_rb"] = i["L3_ffn_router_bias"]
    out["L3f_sel"] = part_rows(16, 8, 2)
    out["L0f_wr"] = i["L0_ffn_Wr"].T
    q, k, v = np.split(i["L0_ffn_Wqkv"].transpose(1, 0, 2), 3, axis=2)
    half_swapped = lambda w: np.concatenate([w[..., 32:64], w[..., :32]], -1)
    out["L0f_wq"], out["L0f_wk"], out["L0f_wv"] = q, k, v
    out["L0f_ws"] = np.concatenate([half_swapped(q), half_swapped(k)], -1)
    out["L0f_wo"] = i["L0_ffn_Wo"].transpose(1, 0, 2)
    inv = (1.0 / f32(10000.0) ** (np.arange(32, dtype=f32) * f32(2.0) / f32(64))).astype(f32)
    ang = np.arange(T, dtype=f32)[:, None] * inv
    sin, cos = np.sin(ang), np.cos(ang)
    rest = np.concatenate([cos, cos, -sin, sin], 1)
    parts = []
    for _ in range(3):
        parts.append(rest.astype(bf16))
        rest = rest - parts[-1].astype(f32)
    out["L0f_tables"] = np.stack(parts, 1).reshape(NI, P, 3, P).transpose(1, 0, 2, 3)
    out["L0f_iota"] = np.tile(np.arange(64, dtype=f32), (P, 1))
    same = np.kron(np.eye(2), np.tril(np.ones((64, 64)))) > 0
    out["L0f_causal"] = np.where(same, 0, NEG).astype(f32)
    own = np.zeros((2, 64, 4, 3, 8), f32)
    for p in range(4):
        for h in range(2):
            own[h, :, p, :, 2 * p + h] = 1
    out["L0f_own"] = own.reshape(P, 4, 3, 8)
    up = i["L1_ffn_W_up"]
    F = up.shape[2]
    out["L1f_wu"] = np.pad(up, ((0, 0), (0, 0), (0, 3 * P - F))).transpose(1, 0, 2)
    down = np.zeros((8, 3 * P, D), f32)
    down[:, :F] = i["L1_ffn_W_down"]
    down[:, 2 * P + 96] = i["L1_ffn_b_down"]
    out["L1f_wd"] = down.reshape(4, 2, 3, P, D).transpose(3, 0, 2, 1, 4).reshape(P, 4, 3, 2 * D)
    out["L1f_bu"] = np.pad(i["L1_ffn_b_up"], ((0, 0), (0, 3 * P - F))).reshape(4, 3, P).transpose(2, 0, 1)
    out["L1f_wr"] = i["L1_ffn_Wr"]
    out["L1f_br"] = i["L1_ffn_br"]
    out["L1f_tri"] = np.triu(np.ones((P, P), f32))
    past = np.arange(P)[:, None] >= np.arange(P)[None]
    out["mask"] = np.where(np.concatenate([np.ones((P, 3 * P), bool), past], 1), 0, NEG).astype(f32)
    out["maskT"] = np.where(past.T, 0, NEG).astype(bf16)
    d_major = lambda w: w.reshape(w.shape[:-1] + (16, 8)).swapaxes(-1, -2).reshape(w.shape)
    q, k, v, o = (i["L2_attn_W" + c] for c in "qkvm")
    bq, bk, bv, bo = (i["L2_attn_b" + c] for c in "qkvm")
    out["L2a_w"] = np.stack([d_major(q), d_major(k), v, o], 1)
    out["L2a_qkb"] = np.stack([d_major(bq), d_major(bk)], 1)
    out["L2a_vob"] = np.stack([bv, bo])
    (q, k, v), (bq, bk, bv) = i["L3_attn_c_attn_kernel"].T.reshape(D, 3, D).swapaxes(0, 1), i["L3_attn_c_attn_bias"].reshape(3, D)
    out["L3a_w"] = np.stack([d_major(q), d_major(k), v, i["L3_attn_c_proj_kernel"].T], 1)
    out["L3a_qkb"] = np.stack([d_major(bq), d_major(bk)], 1)
    out["L3a_vob"] = np.stack([bv, i["L3_attn_c_proj_bias"]])
    return {k: np.ascontiguousarray(v) for k, v in out.items()}


def build(nc, arrays, stages=tuple(range(8))):
    dram = {k: nc.dram_tensor("in_" + k, v.shape, mybir.dt.from_np(v.dtype), kind="ExternalInput").ap()
            for k, v in arrays.items()}
    dram["out"] = nc.dram_tensor("out_0", (NB, T, D), F32, kind="ExternalOutput").ap()
    program(nc, dram, stages)


def kernel(**inputs):
    import concourse.bacc as bacc
    from concourse.bass_utils import run_bass_kernel_spmd

    nc = bacc.Bacc("TRN2", target_bir_lowering=False, num_devices=1)
    arrays = layouts({k: np.asarray(v) for k, v in inputs.items()})
    build(nc, arrays)
    launch = run_bass_kernel_spmd(nc, [{"in_" + k: v for k, v in arrays.items()}], core_ids=[0])
    return launch.results[0]["out_0"]
```

```python
from contextlib import ExitStack

import numpy as np

import concourse.bass as bass
from concourse import mybir

F32 = mybir.dt.float32
BF16 = mybir.dt.bfloat16
I32 = mybir.dt.int32
U32 = mybir.dt.uint32
ALU = mybir.AluOpType
ACT = mybir.ActivationFunctionType
AX = mybir.AxisListType

P = 128
NB = 8
T = 512
NI = T // P
NT = NB * NI
D = 128
LN_EPS = 1e-5
NEG = -1e30


def wait_alone(eng, sem, value):
    eng.wait_ge(sem, value)
    eng.sem_inc(State.passed[eng.engine], 1)


class Chain:

    def __init__(self, eng, sem, turn=0, per=0, before=0):
        self.eng, self.sem, self.base, self.per, self.n = eng, sem, turn * per + before, per, 0

    def then(self, ins):
        self.n += 1
        ins.then_inc(self.sem, 1)

    def wait(self, alone=False):
        if self.per and alone:
            wait_alone(self.eng, self.sem, self.base + self.n)
        else:
            self.eng.wait_ge(self.sem, self.base + self.n)

    def link(self, ins, alone=False):
        self.then(ins)
        self.wait(alone)

    def end(self):
        assert self.per in (0, self.n), f"{self.n} steps a turn"


def rsqrt(dve, c, out, v, t, scale, eps):
    rsqrt_guess(dve, c, out, v, scale, eps)
    for _ in range(3):
        rsqrt_newton(dve, c, out, v, t)


def rsqrt_guess(dve, c, out, v, scale, eps):
    c.link(dve.tensor_scalar(v, v, scale, eps, ALU.mult, ALU.add))
    c.link(dve.tensor_scalar(out.bitcast(I32), v.bitcast(I32), -0.5, float(0x5F3759DF), ALU.mult, ALU.add))


def rsqrt_newton(dve, c, out, v, t):
    c.link(dve.tensor_tensor(t, out, out, ALU.mult))
    c.link(dve.tensor_tensor(t, t, v, ALU.mult))
    c.link(dve.tensor_scalar(t, t, -0.5, 1.5, ALU.mult, ALU.add))
    c.link(dve.tensor_tensor(out, out, t, ALU.mult))


RSQRT_STEPS = 14


class State:
    passed = {}


    def sem(self, name):
        self.sems.append(self.nc.alloc_semaphore(name))
        return self.sems[-1]


def bcast(ap, axis, n):
    v = ap.unsqueeze(axis)
    return v.broadcast_to([n if k == axis else s for k, s in enumerate(v.shape)])


def setup_stage(S):
    n = "mod_"
    nc = S.nc
    loaded, mod_loaded, silu_done, modT_done, chain, gates_ready, gatesT_done, gatesT_ready = map(S.sem, (
        "x_loaded", "mod_loaded", "silu", "modT_done", "setup", "gates", "gatesT", "gatesTs"))
    with ExitStack() as ctx:
        wmod = ctx.enter_context(nc.sbuf_tensor(n + "w", [P, 4, 6 * D], F32))
        cT = ctx.enter_context(nc.sbuf_tensor(n + "cT", [P, 4, NB], F32))
        sT = ctx.enter_context(nc.sbuf_tensor(n + "sT", [P, 4, NB], F32))
        clip = ctx.enter_context(nc.sbuf_tensor(n + "clip", [P, 2, 4, 2, NB], F32))
        gates = ctx.enter_context(nc.sbuf_tensor(n + "gates", [P, 4, 2, NB], F32))
        ps = ctx.enter_context(nc.psum_tensor(n + "ps", [P, 4, 6, NB], F32))
        psG = ctx.enter_context(nc.psum_tensor(n + "psG", [4 * 2 * NB, P], F32))
        block = ctx.enter_context(nc.Block())

        @block.sync
        def _(sp):
            for l in range(4):
                sp.dma_start(cT[:, l], S.dram[f"L{l}_cT"]).then_inc(mod_loaded, 16)
                sp.dma_start(wmod[:, l], S.dram[f"L{l}_wmod"]).then_inc(mod_loaded, 16)
            for b in range(NB):
                sp.dma_start(S.x[:, b * NI:(b + 1) * NI], S.dram["x"][b].rearrange("(i p) f -> p i f", p=P)).then_inc(loaded, 16)
            sp.dma_start(S.ident[:], S.dram["ident"]).then_inc(loaded, 16)
            sp.dma_start(S.identb[:], S.dram["identb"]).then_inc(loaded, 16)
            sp.wait_ge(gatesT_ready, 1)
            sp.dma_start(S.gates_dram.rearrange("l k b f -> (l k b) f"), S.gatesT[:]).then_inc(S.gates_stored, 16)

        @block.scalar
        def _(act):
            act.wait_ge(mod_loaded, 8 * 16)
            act.activation(sT[:], cT[:], ACT.Silu).then_inc(silu_done, 1)

        @block.tensor
        def _(pe):
            pe.wait_ge(silu_done, 1)
            for l in range(4):
                for k in range(6):
                    ins = pe.matmul(ps[:, l, k], wmod[:, l, k * D:(k + 1) * D], sT[:, l], start=True, stop=True)
            ins.then_inc(modT_done, 1)
            pe.wait_ge(loaded, (NB + 2) * 16)
            pe.wait_ge(gates_ready, 1)
            pe.transpose(psG[:], gates[:].rearrange("p l k b -> p (l k b)"), S.ident[:]).then_inc(gatesT_done, 1)

        @block.vector
        def _(dve):
            c = Chain(dve, chain)
            dve.memset(S.ones[:], 1.0)
            dve.wait_ge(loaded, (NB + 2) * 16)
            for b in range(NB):
                for i in range(NI):
                    ins = dve.bn_stats(S.bn[:, b, i], S.x[:, b * NI + i])
            c.link(ins)
            for t in range(NT):
                ins = dve.bn_aggr(S.mv[:, t], S.bn[:, t // NI, t % NI])
            c.then(ins)
            dve.wait_ge(modT_done, 1)
            c.link(dve.tensor_copy(S.modTs[:], ps[:]))
            for l in range(4):
                scales = S.modTs[:, l, 1::3]
                ins = dve.tensor_scalar(scales, scales, 1.0, None, ALU.add)
            c.link(ins)
            raw = [S.modTs[:, l, 2::3] for l in range(4)]
            for l, g in enumerate(raw):
                dve.tensor_scalar(clip[:, 0, l], g, 0.25, None, ALU.max)
                ins = dve.tensor_scalar(clip[:, 1, l], g, -0.25, None, ALU.min)
            c.link(ins)
            for l, g in enumerate(raw):
                dve.scalar_tensor_tensor(clip[:, 0, l], g, 0.0, clip[:, 0, l], ALU.is_ge, ALU.mult)
                ins = dve.scalar_tensor_tensor(clip[:, 1, l], g, 0.0, clip[:, 1, l], ALU.is_lt, ALU.mult)
            c.link(ins)
            dve.tensor_tensor(gates[:], clip[:, 0], clip[:, 1], ALU.add).then_inc(gates_ready, 1)
            dve.wait_ge(gatesT_done, 1)
            dve.tensor_copy(S.gatesT[:], psG[:]).then_inc(gatesT_ready, 1)


def load_gates(S, sp, l):
    if S.gate_loads == 0:
        sp.wait_ge(S.gates_stored, 16)
    S.gate_loads += 1
    row = S.gates_dram[l].rearrange("k b f -> (k b f)")
    sp.dma_start(S.gate[:].rearrange("p k b f -> p (k b f)"), row.partition_broadcast(P)).then_inc(S.gates_loaded, 16)


def wait_gates(S, dve):
    dve.wait_ge(S.gates_loaded, 16 * S.gate_loads)


def rstd_step(S, dve, c):
    c.link(dve.tensor_copy(S.var[:], S.mv[:, :, 1]))
    rsqrt(dve, c, S.rstd[:], S.var[:], S.nwt[:], 1.0, LN_EPS)


def normalise(S, dve, b, z):
    for i in range(NI):
        t = b * NI + i
        ins = dve.tensor_scalar(z[:, i], S.x[:, bass.ds(t, 1)].squeeze(1), S.mv[:, bass.ds(t, 1), 0],
                                S.rstd[:, bass.ds(t, 1)], ALU.subtract, ALU.mult)
    return ins


def add_and_stats(S, dve, c, b, kind, result, was_read=None):
    add_result(S, dve, c, b, kind, result, was_read)
    new_stats(S, dve, c, b)


def add_result(S, dve, c, b, kind, result, was_read=None):
    xb = S.x[:, bass.ds(b * NI, NI)]
    g = bcast(S.gate[:, kind, bass.ds(b, 1)].squeeze(1), 1, NI)
    ins = dve.tensor_tensor(S.upd[:], result, g, ALU.mult)
    if was_read is None:
        c.link(ins)
    else:
        ins.then_inc(was_read, 1)
        dve.wait_ge(was_read, b + 1)
    c.link(dve.tensor_tensor(xb, xb, S.upd[:], ALU.add), alone=True)


def new_stats(S, dve, c, b):
    for i in range(NI):
        ins = dve.bn_stats(S.bn[:, 0, i], S.x[:, bass.ds(b * NI + i, 1)].squeeze(1))
    c.link(ins, alone=True)
    for i in range(NI):
        ins = dve.bn_aggr(S.mv4[:, i], S.bn[:, 0, i])
    c.link(ins, alone=True)
    c.then(dve.tensor_copy(S.mv[:, bass.ds(b * NI, NI)], S.mv4[:]))


ADD_STEPS = 5


def l0_attn_stage(S):
    nc = S.nc
    H, HD = 8, 8
    LAMBDA_INIT = 0.8 - 0.6 * float(np.exp(-0.3 * 12))
    n = "L0a_"
    sem = lambda s: S.sem(n + s)
    loaded, chain, z_ready, zT_done, hT_ready, qkv_done, qk_used, v_ready, rope_done, prod1, prod2 = map(
        sem, ("loaded", "dve", "z", "zT", "hT", "qkv", "qk_used", "v", "rope", "prod1", "prod2"))
    soft_ready, exp_done, pm_ready, red1, red2, a_ready, aT_done, aT_ready, o_done, added = map(
        sem, ("soft", "exp", "pm", "red1", "red2", "a", "aT", "aTs", "o", "added"))
    with ExitStack() as ctx:
        sb = lambda name, shape, dt=F32: ctx.enter_context(nc.sbuf_tensor(n + name, shape, dt))
        pt = lambda name, shape, dt=F32: ctx.enter_context(nc.psum_tensor(n + name, shape, dt))
        w = sb("w", [P, 6, D])
        rope = sb("rope", [P, NI, 2, D])
        lam4 = sb("lam4", [P, 4, HD])
        lnT = sb("lnT", [P, 2])
        lam = sb("lam", [P, 4])
        z = sb("z", [P, NI, D])
        hT = sb("hT", [P, T])
        vs = sb("v", [P, 2, NI, D])
        r1 = sb("r1", [P, NI, 2, D])
        r2 = sb("r2", [P, NI, 2, D])
        pr1 = sb("pr1", [P, NI, 2, 512])
        pr2 = sb("pr2", [P, NI, 1024])
        s = sb("s", [P, NI, 2, 8, 8])
        e = sb("e", [P, NI, 2, 8, 8])
        mx = sb("mx", [P, NI * 16])
        sm = sb("sm", [P, NI, 2, 8])
        pm = sb("pm", [P, NI, 8, 8])
        a = sb("a", [P, NI, D])
        a2 = sb("a2", [P, NI, D])
        ss = sb("ss", [P, 3, NI * 8])
        aT = sb("aT", [P, T])
        psT = pt("psT", [P, T])
        psQ = pt("psQ", [P, 2, 2, 2, D])
        psV = pt("psV", [P, NI, D])
        psA = pt("psA", [P, T])
        psO = pt("psO", [P, NI, D])
        block = ctx.enter_context(nc.Block())

        @block.sync
        def _(sp):
            sp.dma_start(w[:], S.dram["L0a_w"]).then_inc(loaded, 16)
            load_gates(S, sp, 0)
            sp.dma_start(rope[:], S.dram["L0a_rope"]).then_inc(loaded, 16)
            sp.dma_start(lam4[:], S.dram["L0a_lam"].partition_broadcast(P)).then_inc(loaded, 16)
            for h in range(H):
                sp.dma_start(lnT[h * 16:(h + 1) * 16], S.dram["L0a_ln"]).then_inc(loaded, 16)

        def turns(eng, body):
            for t in range(3):
                body(t, t % 2, True, t > 0, True, t > 1)
            with eng.Fori(1, NB // 2 - 1) as two:
                for u in range(2):
                    body(two * 2 + (u + 1), 1 - u, True, True, True, True)
            body(NB - 1, 1, True, True, False, True)
            body(NB, 0, False, True, False, True)

        @block.tensor
        def _(pe):
            pe.wait_ge(loaded, (3 + H) * 16)

            def project(b, later):
                pe.wait_ge(z_ready, b + 1)
                if later:
                    pe.wait_ge(hT_ready, b)
                for i in range(NI):
                    ins = pe.transpose(psT[:, i * P:(i + 1) * P], z[:, i], S.ident[:])
                ins.then_inc(zT_done, 1)
                pe.wait_ge(hT_ready, b + 1)
                for i in range(NI):
                    if i == 0 and later:
                        pe.wait_ge(v_ready, b)
                    if i >= 2 or later:
                        pe.wait_ge(qk_used, NI * b + i - 1)
                    h = hT[:, i * P:(i + 1) * P]
                    pe.matmul(psQ[:, i % 2].rearrange("p a b f -> p (a b f)"), h,
                              w[:, 0:4].rearrange("p a f -> p (a f)"), start=True, stop=True)
                    pe.matmul(psV[:, i], h, w[:, 4], start=True, stop=True).then_inc(qkv_done, 1)

            project(0, False)

            def turn(t, par, front, back, ahead, end):
                if ahead:
                    project(t + 1, True)
                if back:
                    pe.wait_ge(a_ready, t)
                    for i in range(NI):
                        ins = pe.transpose(psA[:, i * P:(i + 1) * P], a[:, i], S.ident[:])
                    ins.then_inc(aT_done, 1)
                    pe.wait_ge(aT_ready, t)
                    for i in range(NI):
                        ins = pe.matmul(psO[:, i], aT[:, i * P:(i + 1) * P], w[:, 5], start=True, stop=True)
                    ins.then_inc(o_done, 1)

            turns(pe, turn)

        @block.scalar
        def _(act):
            act.wait_ge(chain, 1 + RSQRT_STEPS + 2)
            act.activation(lam[:, 2:4], lam[:, 0:2], ACT.Exp).then_inc(exp_done, 1)

            def modulate(b):
                act.wait_ge(zT_done, b + 1)
                act.activation(hT[:], psT[:], ACT.Identity, bias=S.modT[:, 0, bass.ds(b, 1)],
                               scale=S.modT[:, 1, bass.ds(b, 1)]).then_inc(hT_ready, 1)

            def values(b, par, used):
                act.wait_ge(qkv_done, NI * (b + 1))
                if used:
                    act.wait_ge(prod2, NI * (b - 1))
                act.activation(vs[:, par], psV[:], ACT.Copy).then_inc(v_ready, 1)

            def turn(t, par, front, back, ahead, end):
                if ahead:
                    act.wait_ge(qkv_done, NI * (t + 1))
                    modulate(t + 1)
                if front:
                    act.wait_ge(soft_ready, t + 1)
                    act.activation(e[:], s[:], ACT.Exp, scale=float(HD) ** -0.25).then_inc(exp_done, 1)
                if ahead:
                    values(t + 1, 1 - par, back)
                if back:
                    act.wait_ge(aT_done, t)
                    act.activation(aT[:], psA[:], ACT.Identity, bias=lnT[:, 1:2], scale=lnT[:, 0:1]).then_inc(aT_ready, 1)

            modulate(0)
            values(0, 0, False)
            turns(act, turn)

        @block.gpsimd
        def _(pool):
            def turn(t, par, front, back, ahead, end):
                if front:
                    for i in range(NI):
                        pool.wait_ge(qk_used, NI * t + i + 1)
                        pool.tensor_tensor(r1[:, i], r1[:, i], r2[:, i], ALU.add).then_inc(rope_done, 1)
                        wait_alone(pool, rope_done, NI * t + i + 1)
                        if back:
                            pool.wait_ge(red1, NI * (t - 1) + i + 1)
                        for g in range(2):
                            q = r1[:, i, 0].rearrange("p (n g d) -> p n g d", g=2, d=HD)[:, :, g]
                            k = r1[:, i, 1].rearrange("p (n g d) -> p n g d", g=2, d=HD)[:, :, g]
                            ins = pool.tensor_tensor(pr1[:, i, g].rearrange("p (n m d) -> p n m d", n=H, m=H),
                                                     bcast(q, 2, H), bcast(k, 1, H), ALU.mult)
                        ins.then_inc(prod1, 1)
                if back:
                    row = t - 1
                    pool.wait_ge(pm_ready, t)
                    pool.wait_ge(v_ready, t)
                    for i in range(NI):
                        if end:
                            pool.wait_ge(red2, NI * (row - 1) + i + 1)
                        v = vs[:, 1 - par, i].rearrange("p (m e) -> p e m", m=H)
                        pool.tensor_tensor(pr2[:, i].rearrange("p (n e m) -> p n e m", n=H, m=H),
                                           bcast(pm[:, i], 2, 2 * HD), bcast(v, 1, H), ALU.mult).then_inc(prod2, 1)

            turns(pool, turn)

        @block.vector
        def _(dve):
            c = Chain(dve, chain)
            rstd_step(S, dve, c)
            normalise(S, dve, 0, z).then_inc(z_ready, 1)
            dve.wait_ge(loaded, (3 + H) * 16)
            c.link(dve.tensor_tensor(lam4[:, 0:4:2], lam4[:, 0:4:2], lam4[:, 1:4:2], ALU.mult))
            c.link(dve.tensor_reduce(lam[:, 0:2], lam4[:, 0:4:2], AX.X, ALU.add))
            c.then(dve.tensor_scalar(lnT[:], lnT[:], 1.0 - LAMBDA_INIT, None, ALU.mult))
            dve.wait_ge(exp_done, 1)
            c.link(dve.tensor_tensor(lam[:, 0:1], lam[:, 3:4], lam[:, 2:3], ALU.subtract))
            c.link(dve.tensor_scalar(lam[:, 0:1], lam[:, 0:1], -LAMBDA_INIT, None, ALU.add))
            n0 = c.n
            FRONT, BACK = 1, 6 + RSQRT_STEPS
            sr = s[:].rearrange("p i g n m -> p (i g n) m")
            er = e[:].rearrange("p i g n m -> p (i g n) m")
            smr = sm[:].rearrange("p i g n -> p (i g n)")
            ar = a[:].rearrange("p i (n e) -> p (i n) e", e=16)

            def rotate(b, i):
                dve.wait_ge(qkv_done, NI * b + i + 1)
                dve.tensor_tensor(r1[:, i], psQ[:, i % 2, :, 0], bcast(rope[:, i, 0], 1, 2), ALU.mult)
                ins = dve.tensor_tensor(r2[:, i], psQ[:, i % 2, :, 1], bcast(rope[:, i, 1], 1, 2), ALU.mult)
                ins.then_inc(qk_used, 1)

            def add(row):
                dve.wait_ge(o_done, row + 1)
                ac = Chain(dve, added, row, ADD_STEPS)
                add_and_stats(S, dve, ac, row, 0, psO[:])
                ac.end()

            for i in range(NI):
                rotate(0, i)
            n0 = c.n

            def turn(t, par, front, back, ahead, end):
                c = Chain(dve, chain, 0, front and back and ahead)
                c.base = n0 + (t if front else NB) * FRONT + ((t - 1) * BACK if back else 0)
                row = t - 1
                if ahead:
                    dve.wait_ge(zT_done, t + 1)
                    normalise(S, dve, t + 1, z).then_inc(z_ready, 1)
                if back:
                    dve.wait_ge(exp_done, t + 1)
                    c.link(dve.tensor_reduce(smr, er, AX.X, ALU.add))
                    c.link(dve.reciprocal(smr, smr))
                    c.link(dve.tensor_scalar(sm[:, :, 1], sm[:, :, 1], lam[:, 0:1], None, ALU.mult))
                    c.link(dve.tensor_tensor(er, er, bcast(smr, 2, 8), ALU.mult))
                    dve.tensor_tensor(pm[:].rearrange("p i n m -> p i (n m)"),
                                      e[:, :, 0].rearrange("p i n m -> p i (n m)"),
                                      e[:, :, 1].rearrange("p i n m -> p i (n m)"), ALU.add).then_inc(pm_ready, 1)
                if end:
                    if isinstance(t, int) and t == 2:
                        wait_gates(S, dve)
                    add(t - 2)
                if front:
                    for i in range(NI):
                        dve.wait_ge(prod1, NI * t + i + 1)
                        dve.tensor_reduce(s[:, i].rearrange("p g n m -> p (g n m)"), pr1[:, i].rearrange(
                            "p g (x d) -> p (g x) d", d=HD), AX.X, ALU.add).then_inc(red1, 1)
                        if ahead:
                            rotate(t + 1, i)
                    dve.wait_ge(red1, NI * (t + 1))
                    c.link(dve.tensor_reduce(mx[:], sr, AX.X, ALU.max))
                    dve.tensor_tensor(sr, sr, bcast(mx[:], 2, 8), ALU.subtract).then_inc(soft_ready, 1)
                if back:
                    for i in range(NI):
                        dve.wait_ge(prod2, NI * row + i + 1)
                        dve.tensor_reduce(a[:, i], pr2[:, i].rearrange("p (x m) -> p x m", m=H),
                                          AX.X, ALU.add).then_inc(red2, 1)
                    dve.wait_ge(red2, NI * (row + 1))
                    c.link(dve.tensor_tensor(a2[:], a[:], a[:], ALU.mult))
                    c.link(dve.tensor_reduce(ss[:, 0], a2[:].rearrange("p i (n e) -> p (i n) e", e=16), AX.X, ALU.add))
                    rsqrt(dve, c, ss[:, 1], ss[:, 0], ss[:, 2], 1.0 / 16, 1e-8)
                    dve.tensor_tensor(ar, ar, bcast(ss[:, 1], 2, 16), ALU.mult).then_inc(a_ready, 1)
                assert c.n == FRONT * front + BACK * back, c.n

            turns(dve, turn)
            add(NB - 1)


def token_choice_stage(S):
    nc = S.nc
    n = "L0f_"
    E, R = 8, T // 8
    with ExitStack() as ctx:
        sb = lambda name, shape, dt=F32: ctx.enter_context(nc.sbuf_tensor(n + name, shape, dt))
        z = sb("z", [P, NT, D])
        gates = sb("gates", [P, NI, NB * E])
        rank = sb("rank", [P, NI, NB * E])
        w = dict(q=sb("wq", [P, E, D]), k=sb("wk", [P, E, D]), s=sb("wsw", [P, E, D]), v=sb("wv", [P, E, D]),
                 o=sb("wo", [P, E, D]))
        tables = sb("tables", [P, NI, 3, D], BF16)
        masks = dict(iota=sb("iota", [P, R]), causal=sb("causal", [P, P]), own=sb("own", [P, E // 2, 3, E]))
        zp = sb("zp", [P, 2, 3, NI, D], BF16)
        with ExitStack() as inner:
            token_choice_ranks(S, n, inner, z, gates, rank, w, tables, masks, zp, R)
        with ExitStack() as inner:
            token_choice_experts(S, n, inner, z, gates, rank, w, tables, masks, zp, R)


def token_choice_ranks(S, n, ctx, z, gates, rank, w, tables, masks, zp, R):
    nc = S.nc
    E = 8
    BE = NB * E
    small, loaded, chain, z_ready, zT_done, hT_ready, logits_done, gates_ready, pairs_done, top_chain, ranks_done = map(
        lambda s: S.sem(n + s), ("small", "loaded", "dve", "z", "zT", "hT", "logits", "gates", "pairs", "top", "ranks"))
    sb = lambda name, shape, dt=F32: ctx.enter_context(nc.sbuf_tensor(n + name, shape, dt))
    pt = lambda name, shape, dt=F32: ctx.enter_context(nc.psum_tensor(n + name, shape, dt))
    wr = sb("wr", [P, E])
    hT = sb("hT", [P, 2, T])
    first_parts = S.sem(n + "first_parts")
    zr = sb("zr_", [P, NI, D])
    work = sb("work", [BE, 2, T])
    top = sb("top", [BE, R // 8, 8])
    tri = sb("tri", [P, P])
    chosen = sb("chosen", [P, NI, BE])
    psT = pt("psT", [P, 2, T])
    psL = pt("psL", [P, 2, T])
    psP = pt("psP", [BE, T])
    psR = pt("psR", [P, NI * BE])
    psC = pt("psC", [P, 1, 512])
    with nc.Block() as block:
        @block.sync
        def _(sp):
            sp.dma_start(wr[:], S.dram[n + "wr"]).then_inc(small, 16)
            sp.dma_start(tri[:], S.dram["tri"]).then_inc(small, 16)
            sp.dma_start(tables[:], S.dram[n + "tables"]).then_inc(loaded, 16)
            for k in "qksvo":
                sp.dma_start(w[k][:], S.dram[n + "w" + k]).then_inc(loaded, 16)
            for k, tile in masks.items():
                sp.dma_start(tile[:], S.dram[n + k]).then_inc(loaded, 16)
            sp.wait_ge(loaded, 9 * 16)

        @block.gpsimd
        def _(pool):
            for b in range(2):
                pool.wait_ge(z_ready, b + 1)
                z_parts_of(Chain(pool, first_parts, 0, 0, 5 * b), z[:, b * NI:(b + 1) * NI], zp[:, b], zr)

        @block.tensor
        def _(pe):
            pe.wait_ge(small, 32)

            def logits(b):
                pe.wait_ge(hT_ready, b + 1)
                if b >= 2:
                    pe.wait_ge(gates_ready, b - 1)
                for i in range(NI):
                    ins = pe.matmul(psL[:, b % 2, i * E:(i + 1) * E], hT[:, b % 2, i * P:(i + 1) * P], wr[:],
                                    start=True, stop=True)
                ins.then_inc(logits_done, 1)

            for b in range(NB):
                pe.wait_ge(z_ready, b + 1)
                if b >= 2:
                    pe.wait_ge(hT_ready, b - 1)
                for i in range(NI):
                    ins = pe.transpose(psT[:, b % 2, i * P:(i + 1) * P], z[:, b * NI + i], S.ident[:])
                ins.then_inc(zT_done, 1)
                if b > 0:
                    logits(b - 1)
            logits(NB - 1)
            pe.wait_ge(gates_ready, NB)
            for i in range(NI):
                ins = pe.transpose(psP[:, i * P:(i + 1) * P], gates[:, i], S.ident[:])
            ins.then_inc(pairs_done, 1)
            pe.wait_ge(ranks_done, 1)
            for i in range(NI):
                ins = pe.transpose(psC[:, 0, i * BE:(i + 1) * BE], work[:, 1, i * P:(i + 1) * P], S.ident[0:BE, 0:BE])
            ins.then_inc(pairs_done, 1)
            pe.wait_ge(ranks_done, 2)
            for i in range(NI):
                for k in range(i + 1):
                    ins = pe.matmul(psR[:, i * BE:(i + 1) * BE], tri[:] if k == i else S.ones[:], chosen[:, k],
                                    start=(k == 0), stop=(k == i))
            ins.then_inc(pairs_done, 1)

        @block.scalar
        def _(act):
            def take_gates(b):
                act.wait_ge(logits_done, b + 1)
                act.activation(gates[:, :, b * E:(b + 1) * E], psL[:, b % 2, 0:NI * E].rearrange("p (i e) -> p i e", i=NI),
                               ACT.Sigmoid).then_inc(gates_ready, 1)

            for b in range(NB):
                act.wait_ge(zT_done, b + 1)
                if b >= 2:
                    act.wait_ge(logits_done, b - 1)
                act.activation(hT[:, b % 2], psT[:, b % 2], ACT.Identity, bias=S.modT[:, 3, b:b + 1],
                               scale=S.modT[:, 4, b:b + 1]).then_inc(hT_ready, 1)
                if b >= 1:
                    take_gates(b - 1)
            take_gates(NB - 1)

        @block.vector
        def _(dve):
            c = Chain(dve, chain)
            rstd_step(S, dve, c)
            for b in range(NB):
                normalise(S, dve, b, z[:, b * NI:(b + 1) * NI]).then_inc(z_ready, 1)
            c = Chain(dve, top_chain)
            dve.wait_ge(pairs_done, 1)
            c.link(dve.tensor_copy(work[:, 0], psP[:]))
            for r in range(R // 8):
                c.link(dve.max(top[:, r], work[:, r % 2]))
                c.link(dve.match_replace(work[:, (r + 1) % 2], top[:, r], work[:, r % 2], -1.0))
            dve.tensor_scalar(work[:, 1], work[:, 0], -1.0, None, ALU.is_equal).then_inc(ranks_done, 1)
            dve.wait_ge(pairs_done, 2)
            dve.tensor_copy(chosen[:].rearrange("p i x -> p (i x)"), psC[:, 0, 0:NI * BE]).then_inc(ranks_done, 1)
            dve.wait_ge(pairs_done, 3)
            dve.wait_ge(ranks_done, 2)
            flat = rank[:].rearrange("p i x -> p (i x)")
            c.link(dve.tensor_tensor(flat, psR[:], chosen[:].rearrange("p i x -> p (i x)"), ALU.mult))
            c.then(dve.tensor_scalar(flat, flat, -1.0, None, ALU.add))


def z_parts_of(c, zrow, p3, zr):
    pool = c.eng
    c.link(pool.tensor_copy(p3[:, 0], zrow), alone=True)
    c.link(pool.tensor_tensor(zr[:], zrow, p3[:, 0], ALU.subtract), alone=True)
    c.link(pool.tensor_copy(p3[:, 1], zr[:]), alone=True)
    c.link(pool.tensor_tensor(zr[:], zr[:], p3[:, 1], ALU.subtract), alone=True)
    c.link(pool.tensor_copy(p3[:, 2], zr[:]))


def token_choice_experts(S, n, ctx, z, gates, rank, w, tables, masks, zp, R):
    nc = S.nc
    E, NP, H2 = 8, 4, D // 2
    ER = E * R
    SCALE = float(D) ** -0.5
    (hot_ready, z_chain, g_parts, x_done, x_ready, tab_done, tab_ready, q_done, rot_q, rot_k, high,
     sw_done, v_done, v_ready, hotT_done, hotT_ready, gg_done, gg_ready, gg_sum, rotated) = map(lambda s: S.sem(n + s), (
         "hot", "pool", "g_parts", "x", "xs", "tab", "tabs", "q", "rot_q", "rot_k", "high",
         "sw", "v", "vs", "hotT", "hotTs", "gg", "ggs", "gg_sum", "rotated"))
    chain, s_done, s_ready, exp_done, aT_done, aT_ready, av_done, av_ready, o_done, o_parts, y_done, added, op1, op2 = map(
        lambda s: S.sem(n + s), ("chain", "s", "ss", "exp_", "aT", "aTs", "av", "avs", "o", "os", "y", "added", "op1", "op2"))
    sb = lambda name, shape, dt=F32: ctx.enter_context(nc.sbuf_tensor(n + name, shape, dt))
    pt = lambda name, shape, dt=F32: ctx.enter_context(nc.psum_tensor(n + name, shape, dt))
    iota, causal, own = masks["iota"], masks["causal"], masks["own"]
    hot = sb("hot", [P, 2, NI, ER], BF16)
    zr = sb("zr", [P, NI, D])
    gp = sb("gp", [P, 2, NI, 3, E], BF16)
    gr = sb("gr", [P, NI, E])
    xT = sb("xT", [P, ER])
    tab = sb("tab", [P, ER])
    tab_low = sb("tab_low", [H2, ER])
    rot = sb("rot", [H2, 2, 2, ER])
    qk = sb("qk", [P, 2, 2, ER])
    v = sb("v", [P, 2, NP, D])
    hotT = sb("hotT", [P, 2, NP, T], BF16)
    gg = sb("gg", [P, 2, NP])
    ggm = sb("ggm", [P, NP, 3 * E])
    s = sb("s", [P, NP, P])
    mx = sb("mx", [P, NP])
    sm = sb("sm", [P, NP])
    e = sb("e", [P, NP, P])
    aT = sb("aT", [P, NP, P])
    avT = sb("avT", [P, NP, P])
    o = sb("o", [P, NP, D])
    op = sb("op", [P, 3, NP, D], BF16)
    bx, bt, bq, bk, bh, bs, ba, by = (pt("bank_" + k, [P, T]) for k in ("x", "t", "q", "k", "h", "s", "a", "y"))
    LOOP0 = 2

    class Turn:
        def __init__(self, t, parity, steady):
            self.t, self.par, self.steady = t, parity, steady
            self.front, self.back, self.end = (steady or 0 <= t - lag < NB for lag in range(3))
            self.ahead = steady or t + 1 < NB
            self.later = steady or t > 0

    def turns(eng, body):
        for t in range(LOOP0):
            body(Turn(t, t % 2, False))
        with eng.Fori(LOOP0 // 2, NB // 2 - 1) as two:
            for u in range(2):
                body(Turn(two * 2 + u, u, True))
        for t in range(NB - 2, NB + 1):
            body(Turn(t, t % 2, False))

    with nc.Block() as block:
        @block.gpsimd
        def _(pool):
            def parts(b, par, before):
                c = Chain(pool, z_chain, 0, before)
                if before:
                    c.base = (b - 2) * 9 + 8
                    wait_alone(pool, gg_done, b - 1)
                    z_parts_of(c, z[:, bass.ds(b * NI, NI)], zp[:, par], zr)
                else:
                    c.base = b * 4
                g = gates[:, :, bass.ds(b * E, E)]
                g3 = gp[:, par]
                c.link(pool.tensor_copy(g3[:, :, 0], g), alone=True)
                c.link(pool.tensor_tensor(gr[:], g, g3[:, :, 0], ALU.subtract), alone=True)
                c.link(pool.tensor_copy(g3[:, :, 1], gr[:]), alone=True)
                c.link(pool.tensor_tensor(gr[:], gr[:], g3[:, :, 1], ALU.subtract), alone=True)
                pool.tensor_copy(g3[:, :, 2], gr[:]).then_inc(g_parts, 1)

            parts(0, 0, False)
            parts(1, 1, False)
            with pool.Fori(1, NB // 2) as two:
                for par in range(2):
                    parts(two * 2 + par, par, True)

        @block.tensor
        def _(pe):
            def pair(e):
                return slice(e // 2 * P, e // 2 * P + P), slice(e % 2 * R, e % 2 * R + R)

            def turn_hot(u, half):
                t, f = u.t, u.par
                if half == 0 and u.later:
                    pe.wait_ge(gg_ready, t)
                if half == 1:
                    pe.wait_ge(hotT_ready, 2 * t + 1)
                for p in range(2):
                    cols = slice((2 * half + p) * P, (2 * half + p + 1) * P)
                    for i in range(NI):
                        ins = pe.transpose(bh[:, p * 256 + i * 64:p * 256 + (i + 1) * 64].bitcast(BF16),
                                           hot[:, f, i, cols], S.identb[:])
                ins.then_inc(hotT_done, 1)

            def turn(u):
                t, row = u.t, u.t - 1
                f, r = u.par, 1 - u.par
                if u.back:
                    pe.wait_ge(rot_k, row + 1)
                    pe.wait_ge(rot_q, row + 1)
                    pe.wait_ge(high, 2 * row + 2)
                    for p in range(NP):
                        ins = pe.matmul(bs[:, p * P:(p + 1) * P], qk[:, r, 0, p * P:(p + 1) * P],
                                        qk[:, r, 1, p * P:(p + 1) * P], start=True, stop=True)
                    ins.then_inc(s_done, 1)
                if u.front:
                    if u.steady or t >= 2:
                        pe.wait_ge(z_chain, (t - 1) * 9 + 4)
                    pe.wait_ge(hot_ready, t + 1)
                    if u.later:
                        pe.wait_ge(rot_k, t)
                    for i in range(NI):
                        for a in range(3):
                            ins = pe.matmul(bx[:], zp[:, f, a, i], hot[:, f, i], start=(i == a == 0), stop=(i == NI - 1 and a == 2))
                    ins.then_inc(x_done, 1)
                    if u.later:
                        pe.wait_ge(v_ready, t)
                    for i in range(NI):
                        for a in range(3):
                            ins = pe.matmul(bt[:], tables[:, i, a], hot[:, f, i], start=(i == a == 0), stop=(i == NI - 1 and a == 2))
                    ins.then_inc(tab_done, 1)
                    turn_hot(u, 0)
                if u.back:
                    pe.wait_ge(exp_done, row + 1)
                    for p in range(NP):
                        ins = pe.transpose(bs[:, p * P:(p + 1) * P], e[:, p], S.ident[:])
                    ins.then_inc(aT_done, 1)
                if u.front:
                    pe.wait_ge(x_ready, t + 1)
                    for a, (wt, bank) in enumerate((("q", bq), ("k", bk))):
                        for x in range(E):
                            ins = pe.matmul(bank[:, x * R:(x + 1) * R], w[wt][:, x], xT[:, x * R:(x + 1) * R],
                                            start=True, stop=True)
                    ins.then_inc(q_done, 1)
                    for x in range(E):
                        ins = pe.matmul(bx[:, x * R:(x + 1) * R], w["s"][:, x], xT[:, x * R:(x + 1) * R],
                                        start=True, stop=True)
                    ins.then_inc(sw_done, 1)
                if u.back:
                    pe.wait_ge(aT_ready, row + 1)
                    for p in range(NP):
                        ins = pe.matmul(ba[:, p * P:(p + 1) * P], v[:, r, p], aT[:, p], start=True, stop=True)
                    ins.then_inc(av_done, 1)
                if u.front:
                    turn_hot(u, 1)
                if u.back:
                    pe.wait_ge(av_ready, row + 1)
                    for x in range(E):
                        cols, rows = pair(x)
                        ins = pe.matmul(ba[rows, cols], avT[:, x // 2, rows], w["o"][:, x], start=True, stop=True)
                    ins.then_inc(o_done, 1)
                if u.front:
                    pe.wait_ge(tab_ready, t + 1)
                    for x in range(E):
                        cols, rows = pair(x)
                        ins = pe.matmul(bt[rows, cols], xT[:, x * R:(x + 1) * R], w["v"][:, x], start=True, stop=True)
                    ins.then_inc(v_done, 1)
                    pe.wait_ge(hotT_ready, 2 * t + 2)
                    pe.wait_ge(g_parts, t + 1)
                    for p in range(NP):
                        for i in range(NI):
                            ins = pe.matmul(bh[:, p * 32:p * 32 + 3 * E], hot[:, f, i, p * P:(p + 1) * P],
                                            gp[:, f, i].rearrange("p a e -> p (a e)"), start=(i == 0), stop=(i == NI - 1))
                    ins.then_inc(gg_done, 1)
                if u.back:
                    pe.wait_ge(o_parts, row + 1)
                    if u.steady or row > 0:
                        pe.wait_ge(added, row * ADD_STEPS)
                    for i in range(NI):
                        for p in range(NP):
                            for a in range(3):
                                ins = pe.matmul(by[:, i * D:(i + 1) * D], hotT[:, r, p, i * P:(i + 1) * P], op[:, a, p],
                                                start=(p == a == 0), stop=(p == NP - 1 and a == 2))
                    ins.then_inc(y_done, 1)

            turns(pe, turn)

        @block.scalar
        def _(act):
            def take_hot(u, half):
                t = u.t
                act.wait_ge(hotT_done, 2 * t + half + 1)
                if half == 0 and u.later:
                    act.wait_ge(y_done, t - 1)
                act.activation(hotT[:, u.par, 2 * half:2 * half + 2], bh[:].bitcast(BF16).rearrange(
                    "p (a k) -> p a k", a=2), ACT.Copy).then_inc(hotT_ready, 1)

            def turn(u):
                t, row = u.t, u.t - 1
                f, r = u.par, 1 - u.par
                if u.back:
                    act.wait_ge(s_ready, row + 1)
                    if u.steady or row > 0:
                        act.wait_ge(aT_done, row)
                    for p in range(NP):
                        ins = act.activation(e[:, p], s[:, p], ACT.Exp, bias=mx[:, p:p + 1], scale=SCALE,
                                             accum_out=sm[:, p:p + 1])
                    ins.then_inc(exp_done, 1)
                if u.front:
                    act.wait_ge(x_done, t + 1)
                    if u.later:
                        act.wait_ge(v_done, t)
                    act.activation(xT[:], bx[:], ACT.Identity, bias=S.modT[:, 3, bass.ds(t, 1)],
                                   scale=S.modT[:, 4, bass.ds(t, 1)]).then_inc(x_ready, 1)
                    act.wait_ge(tab_done, t + 1)
                    if u.later:
                        act.wait_ge(rot_k, t)
                    act.activation(tab_low[:], bt[H2:P], ACT.Copy)
                    act.activation(tab[:], bt[:], ACT.Copy).then_inc(tab_ready, 1)
                    take_hot(u, 0)
                if u.back:
                    act.wait_ge(aT_done, row + 1)
                    if u.steady or row > 0:
                        act.wait_ge(av_done, row)
                    act.activation(aT[:], bs[:].rearrange("p (a k) -> p a k", a=NP), ACT.Copy).then_inc(aT_ready, 1)
                if u.front:
                    act.wait_ge(q_done, t + 1)
                    if u.later:
                        act.wait_ge(s_done, t - 1)
                    for a, bank in enumerate((bq, bk)):
                        act.activation(qk[H2:P, f, a], bank[H2:P], ACT.Copy).then_inc(high, 1)
                if u.back:
                    act.wait_ge(av_done, row + 1)
                    if u.steady or row > 0:
                        act.wait_ge(o_done, row)
                    act.activation(avT[:], ba[:].rearrange("p (a k) -> p a k", a=NP), ACT.Copy).then_inc(av_ready, 1)
                if u.front:
                    take_hot(u, 1)
                    act.wait_ge(v_done, t + 1)
                    act.activation(v[:, f], bt[:].rearrange("p (a k) -> p a k", a=NP), ACT.Copy).then_inc(v_ready, 1)

            turns(act, turn)

        @block.vector
        def _(dve):
            BACK = 7

            def one_hot(row, par, used):
                ranks = rank[:, :, bass.ds(row * E, E)]
                if used:
                    dve.wait_ge(gg_done, row - 1)
                for i in range(NI):
                    ins = dve.tensor_tensor(hot[:, par, i].rearrange("p (e j) -> p e j", e=E), bcast(ranks[:, i], 2, R),
                                            bcast(iota[:], 1, E), ALU.is_equal)
                ins.then_inc(hot_ready, 1)

            def add(row):
                dve.wait_ge(y_done, row + 1)
                ac = Chain(dve, added, row, ADD_STEPS)
                add_and_stats(S, dve, ac, row, 1, by[:].rearrange("p (i f) -> p i f", i=NI))

            def turn(u):
                t, row = u.t, u.t - 1
                f, r = u.par, 1 - u.par
                c = Chain(dve, chain, 0, u.steady)
                c.base = row * BACK
                if u.back:
                    dve.wait_ge(s_done, row + 1)
                    c.link(dve.tensor_tensor(s[:], bs[:].rearrange("p (a k) -> p a k", a=NP), bcast(causal[:], 1, NP), ALU.add))
                    c.link(dve.tensor_reduce(mx[:], s[:], AX.X, ALU.max))
                    dve.tensor_scalar(mx[:], mx[:], -SCALE, None, ALU.mult).then_inc(s_ready, 1)
                if u.end:
                    add(t - 2)
                if u.front:
                    dve.wait_ge(tab_ready, t + 1)
                    dve.wait_ge(q_done, t + 1)
                    dve.tensor_tensor(rot[:, 0, 0], bq[0:H2], tab[0:H2], ALU.mult)
                    dve.tensor_tensor(rot[:, 1, 0], bk[0:H2], tab[0:H2], ALU.mult)
                    dve.wait_ge(sw_done, t + 1)
                    dve.tensor_tensor(rot[:, 0, 1], bx[0:H2], tab_low[:], ALU.mult).then_inc(rotated, 1)
                    dve.tensor_tensor(rot[:, 1, 1], bx[H2:P], tab[H2:P], ALU.mult).then_inc(rotated, 1)
                    dve.wait_ge(rotated, 2 * t + 2)
                    if u.later:
                        dve.wait_ge(s_done, t - 1)
                    dve.tensor_tensor(qk[0:H2, f, 0], rot[:, 0, 0], rot[:, 0, 1], ALU.add).then_inc(rot_q, 1)
                    dve.tensor_tensor(qk[0:H2, f, 1], rot[:, 1, 0], rot[:, 1, 1], ALU.add).then_inc(rot_k, 1)
                if u.back:
                    dve.wait_ge(exp_done, row + 1)
                    c.link(dve.reciprocal(sm[:], sm[:]))
                    c.link(dve.tensor_tensor(sm[:], sm[:], gg[:, r], ALU.mult))
                    dve.wait_ge(o_done, row + 1)
                    for p in range(NP):
                        ins = dve.tensor_scalar(o[:, p], ba[:, p * P:(p + 1) * P], sm[:, p:p + 1], None, ALU.mult)
                    c.link(ins)
                    if u.steady or row > 0:
                        dve.wait_ge(y_done, row)
                    c.link(dve.tensor_copy(op[:, 0], o[:]))
                    c.link(dve.tensor_tensor(o[:], o[:], op[:, 0], ALU.subtract))
                    dve.tensor_copy(op[:, 1], o[:]).then_inc(op1, 1)
                    dve.wait_ge(op1, row + 1)
                    dve.tensor_tensor(o[:], o[:], op[:, 1], ALU.subtract).then_inc(op2, 1)
                    dve.wait_ge(op2, row + 1)
                    dve.tensor_copy(op[:, 2], o[:]).then_inc(o_parts, 1)
                if u.front:
                    dve.wait_ge(gg_done, t + 1)
                    dve.tensor_tensor(ggm[:], bh[:, 0:NP * 32].rearrange("p (a k) -> p a k", a=NP)[:, :, 0:3 * E],
                                      own[:].rearrange("p a b e -> p a (b e)"), ALU.mult).then_inc(gg_ready, 1)
                    dve.wait_ge(gg_ready, t + 1)
                    dve.tensor_reduce(gg[:, f], ggm[:], AX.X, ALU.add).then_inc(gg_sum, 1)
                if u.ahead:
                    one_hot(t + 1, r, u.later)
                assert not u.back or c.n == BACK, c.n

            one_hot(0, 0, False)
            turns(dve, turn)
            add(NB - 1)


def head_attn_stage(S, l):
    nc = S.nc
    H, HD = 16, 8
    K1, M0 = 96, 96
    K2 = M0 + 3
    GH = 4
    W = 10 * P
    COL_Q = {3: 0, 2: 512, 0: 896, 1: 1024}
    COL_K = {0: 0, 1: 512, 3: 896, 2: 1024}
    n = f"L{l}a_"
    sem = lambda s: S.sem(n + s)
    (loaded, cleared, chain, z_ready, zT_done, hT_ready, q_done, q_ready, k_done, k_ready, v_done, v_ready,
     parts_ready, parts_chain, parts_stored) = map(sem, (
         "loaded", "cleared", "dve", "z", "zT", "hT", "q", "qs", "k", "ks", "v", "vs",
         "parts", "parts_chain", "stored"))
    (sA, sB, maxA, maxB, m_ready, mT_done, mT_ready, m_stored, stA, stB, expA, expB, pv_done,
     raw_ready, rawT_done, norm_ready, nT_done, nT_ready, o_done, added) = map(sem, (
         "sA", "sB", "maxA", "maxB", "m", "mT", "mTs", "m_stored", "stA", "stB", "expA", "expB", "pv",
         "raw", "rawT", "norm", "nT", "nTs", "o", "added"))
    pool_cleared = sem("pool_cleared")
    stack_ready = [sem("stack0"), sem("stack1")]
    m_loaded = [sem("m_loaded0"), sem("m_loaded1")]
    scr = nc.dram_tensor(n + "parts_dram", (2, 2, 3, P, T), BF16, kind="Internal").ap()
    scrm = nc.dram_tensor(n + "maxima_dram", (2, 3 * 32, P), BF16, kind="Internal").ap()

    with ExitStack() as ctx:
        sb = lambda name, shape, dt=F32: ctx.enter_context(nc.sbuf_tensor(n + name, shape, dt))
        pt = lambda name, shape, dt=F32: ctx.enter_context(nc.psum_tensor(n + name, shape, dt))
        w = sb("w", [P, 4, D])
        qkb = sb("qkb", [P, 2])
        vob = sb("vob", [P, 2, D])
        mask = sb("mask", [P, T])
        maskT = sb("maskT", [P, P], BF16)
        z = sb("z", [P, NI, D])
        hT = sb("hT", [P, T])
        qk = sb("qk", [P, 2, T])
        rest = sb("rest", [P, 2, T])
        parts = sb("parts", [P, 2, 3, T], BF16)
        qst = sb("qst", [P, 2, H, T], BF16)
        kst = sb("kst", [P, 2, H, T], BF16)
        V = sb("V", [P, 2, NI, H, 32])
        mrow = sb("mrow", [P, H, NI])
        mrest = sb("mrest", [P, 32])
        mpart = sb("mpart", [P, 3, 32], BF16)
        mT = sb("mT", [3 * 32, P], BF16)
        PT = sb("PT", [P, 2, GH, W])
        raw = sb("raw", [P, T])
        rden = sb("rden", [P, NI, GH])
        norm = sb("norm", [P, 2, NI, H, HD])
        nT = sb("nT", [P, T])
        psS = pt("psS", [P, 3 * 512])
        psE = pt("psE", [P, 3 * 512])
        psO = pt("psO", [P, T])
        misc = pt("misc", [P, T])
        block = ctx.enter_context(nc.Block())
        SC = float(HD) ** -0.5

        USES = [(0, "m1", 2, (mT_ready, 2, 2)), (1, "raw2", 3, (norm_ready, 4, 3)), (4, "v", 1, (v_ready, 1, 1)),
                (5, "z", 0, (hT_ready, 1, 1)), (6, "raw3", 3, (norm_ready, 4, 4)), (7, "q", 0, (q_ready, 1, 1)),
                (8, "k", 0, (k_ready, 1, 1)), (9, "norm", 3, (nT_ready, 1, 1)), (10, "out", 3, (added, 1, 1)),
                (11, "raw0", 2, (norm_ready, 4, 1)), (12, "m0", 1, (mT_ready, 2, 1)),
                (13, "raw1", 2, (norm_ready, 4, 2))]
        LOOP0 = 3
        live = lambda t, lag: 0 <= t - lag < NB

        class Turn:

            def __init__(self, t, parity, steady):
                self.t, self.par, self.steady = t, parity, steady
                self.A, self.B, self.C, self.D = (steady or live(t, k) for k in range(4))

            def runs(self, back, lag):
                return self.steady or live(self.t - back, lag)

            def misc_copied_out(self, eng, k):
                for back in (0, 1):
                    for _, _, lag, (sem_, per, at) in reversed(USES[:k] if back == 0 else USES):
                        if self.runs(back, lag):
                            eng.wait_ge(sem_, (self.t - back - lag) * per + at)
                            return

        def turns(eng, body):
            for t in range(LOOP0):
                body(Turn(t, t % 2, False))
            last = LOOP0 + (NB - LOOP0) // 2 * 2
            with eng.Fori(LOOP0, last, 2) as t:
                for u in range(2):
                    body(Turn(t + u, (LOOP0 + u) % 2, True))
            for t in range(last, NB + 3):
                body(Turn(t, t % 2, False))

        @block.sync
        def _(sp):
            for dst, src in ((w, n + "w"), (qkb, n + "qkb"), (mask, "mask"), (maskT, "maskT")):
                sp.dma_start(dst[:], S.dram[src]).then_inc(loaded, 16)
            sp.dma_start(vob[:], S.dram[n + "vob"].partition_broadcast(P)).then_inc(loaded, 16)
            load_gates(S, sp, l)

            sp.wait_ge(pool_cleared, 1)

            def maxima_rows(row, par, half):
                wait_alone(sp, mT_ready, 2 * row + half + 1)
                wait_alone(sp, m_loaded[half], row * 16)
                sp.dma_start(scrm[half], mT[:]).then_inc(m_stored, 16)
                wait_alone(sp, m_stored, (2 * row + half + 1) * 16)
                sp.dma_start(qst[M0:K2, par, 8 * half:8 * half + 8, :].rearrange("c h t -> c (h t)"),
                             scrm[half].rearrange("(c x) p -> c (x p)", c=3)).then_inc(m_loaded[half], 16)

            def stack_rows(row, par, half):
                h = slice(8 * half, 8 * half + 8)
                src = scr[par].rearrange("a c (d h) t -> a c d h t", d=HD)
                for side, st in ((0, qst), (1, kst)):
                    r = 0
                    for c0, c1, rep in (((0, 1, 3), (1, 2, 2), (2, 3, 1)), ((0, 3, 1), (0, 2, 1), (0, 1, 1)))[side]:
                        for c in range(c0, c1):
                            for _ in range(rep):
                                sp.dma_start(st[r:r + HD, par, h, :], src[side, c, :, h, :]).then_inc(stack_ready[half], 16)
                                r += HD
                    assert r == 6 * HD

            def turn(u):
                t = u.t
                if u.C:
                    maxima_rows(t - 2, u.par, 1)
                if u.A:
                    wait_alone(sp, parts_ready, 2 * (t + 1))
                    if u.C:
                        for half in range(2):
                            wait_alone(sp, stack_ready[half], (t - 1) * 12 * 16)
                    for side in range(2):
                        sp.dma_start(scr[u.par, side].rearrange("c p t -> p c t"), parts[:, side]).then_inc(parts_stored, 16)
                    wait_alone(sp, parts_stored, 32 * (t + 1))
                    if u.C:
                        wait_alone(sp, stB, 16 * (t - 2) + 8)
                    stack_rows(t, u.par, 0)
                if u.B:
                    maxima_rows(t - 1, 1 - u.par, 0)
                if u.A:
                    if u.C:
                        wait_alone(sp, stB, 16 * (t - 2) + 16)
                    stack_rows(t, u.par, 1)

            turns(sp, turn)

        @block.tensor
        def _(pe):
            pe.wait_ge(loaded, 80)

            def max_scores(row, par, h):
                if h % 8 == 0:
                    pe.wait_ge(stack_ready[h // 8], (row + 1) * 12 * 16)
                for i in (3, 2, 0, 1):
                    if i == 3:
                        pe.wait_ge(maxA, 16 * row + h)
                    if i == 2:
                        pe.wait_ge(maxB, 16 * row + h)
                    ins = pe.matmul(psS[:, COL_Q[i]:COL_Q[i] + (i + 1) * P], qst[0:K1, par, h, i * P:(i + 1) * P],
                                    kst[0:K1, par, h, 0:(i + 1) * P], start=True, stop=True)
                    if i in (3, 1):
                        ins.then_inc(sA if i == 3 else sB, 1)

            def exp_scores(row, par, h):
                if h % 8 == 0:
                    pe.wait_ge(m_loaded[h // 8], (row + 1) * 16)
                for i in (0, 1, 3, 2):
                    if i == 0:
                        pe.wait_ge(expA, 16 * row + h)
                    if i == 1:
                        pe.wait_ge(expB, 16 * row + h)
                    c0 = COL_K[i]
                    pe.matmul(psE[:, c0:c0 + (4 - i) * P], kst[0:K2, par, h, i * P:(i + 1) * P],
                              qst[0:K2, par, h, i * P:T], start=True, stop=False, skip_group_check=True)
                    ins = pe.matmul(psE[:, c0:c0 + P], S.identb[:], maskT[:], start=False, stop=True,
                                    skip_group_check=True)
                    if i in (0, 2):
                        ins.then_inc(stA if i == 0 else stB, 1)

            def value_sums(row, par, g, tiles):
                if 0 in tiles:
                    pe.wait_ge(expB, 16 * row + 4 * g + 4)
                    if g == 0:
                        pe.wait_ge(v_ready, row + 1)
                    pe.wait_ge(raw_ready, 4 * row + g)
                for i in tiles:
                    for j in range(GH):
                        ins = pe.matmul(psO[32 * j:32 * j + 32, i * P:T], V[:, par, i, GH * g + j],
                                        PT[:, g % 2, j, COL_K[i]:COL_K[i] + (4 - i) * P],
                                        start=(i == 0), stop=(i == NI - 1), skip_group_check=True)
                if NI - 1 in tiles:
                    ins.then_inc(pv_done, 1)

            TILES = {1: (0,), 2: (1,), 3: (2, 3)}

            def turn(u):
                t = u.t
                if not u.steady and t == 1:
                    pe.wait_ge(cleared, 3)
                    pe.wait_ge(pool_cleared, 2)
                for s in range(16):
                    if s % 4 and s < 4 and u.D:
                        value_sums(t - 3, 1 - u.par, 3, TILES[s % 4])
                    if s % 4 and s > 4 and u.C:
                        value_sums(t - 2, u.par, s // 4 - 1, TILES[s % 4])
                    if u.B:
                        max_scores(t - 1, 1 - u.par, s)
                    if u.C:
                        exp_scores(t - 2, u.par, s)
                    for k, (slot, name, lag, _) in enumerate(USES):
                        if slot != s or not u.runs(0, lag):
                            continue
                        u.misc_copied_out(pe, k)
                        row = t - lag
                        if name in ("m0", "m1"):
                            pe.wait_ge(m_ready, 2 * row + int(name[1]) + 1)
                            pe.transpose(misc[0:96, 0:64].bitcast(BF16), mpart[:].rearrange("p c x -> p (c x)"),
                                         S.identb[:]).then_inc(mT_done, 1)
                        elif name == "v":
                            pe.wait_ge(hT_ready, row + 1)
                            for i in range(NI):
                                ins = pe.matmul(misc[:, i * P:(i + 1) * P], hT[:, i * P:(i + 1) * P], w[:, 2],
                                                start=True, stop=True)
                            ins.then_inc(v_done, 1)
                        elif name == "z":
                            pe.wait_ge(z_ready, row + 1)
                            for i in range(NI):
                                ins = pe.transpose(misc[:, i * P:(i + 1) * P], z[:, i], S.ident[:])
                            ins.then_inc(zT_done, 1)
                        elif name in ("q", "k"):
                            pe.wait_ge(hT_ready, row + 1)
                            pe.matmul(misc[:], w[:, "qk".index(name)], hT[:], start=True, stop=True).then_inc(
                                q_done if name == "q" else k_done, 1)
                        elif name[:3] == "raw":
                            pe.wait_ge(raw_ready, 4 * row + int(name[3]) + 1)
                            for i in range(NI):
                                ins = pe.transpose(misc[:, i * P:(i + 1) * P], raw[:, i * P:(i + 1) * P], S.ident[:])
                            ins.then_inc(rawT_done, 1)
                        elif name == "norm":
                            pe.wait_ge(norm_ready, 4 * row + 4)
                            for i in range(NI):
                                ins = pe.transpose(misc[:, i * P:(i + 1) * P],
                                                   norm[:, 1 - u.par, i].rearrange("p h d -> p (h d)"), S.ident[:])
                            ins.then_inc(nT_done, 1)
                        else:
                            pe.wait_ge(nT_ready, row + 1)
                            for i in range(NI):
                                ins = pe.matmul(misc[:, i * P:(i + 1) * P], nT[:, i * P:(i + 1) * P], w[:, 3],
                                                start=True, stop=True)
                            ins.then_inc(o_done, 1)

            turns(pe, turn)

        @block.scalar
        def _(act):
            act.wait_ge(loaded, 80)

            def turn(u):
                t = u.t
                for s in range(16):
                    if s in (0, 4) and u.D or s in (8, 12) and u.C:
                        x = 4 * (t - 3) + 2 + s // 4 if s < 8 else 4 * (t - 2) + s // 4 - 2
                        act.wait_ge(pv_done, x + 1)
                        act.wait_ge(rawT_done, x)
                        act.activation(raw[:], psO[:], ACT.Copy).then_inc(raw_ready, 1)
                    if u.C:
                        row, g, j = t - 2, s // 4, s % 4
                        if j == 0 and (g >= 2 or u.D):
                            act.wait_ge(pv_done, 4 * row + g - 1)
                        act.wait_ge(stA, 16 * row + s + 1)
                        act.activation(PT[:, g % 2, j, 0:512], psE[:, 0:512], ACT.Exp).then_inc(expA, 1)
                        act.wait_ge(stB, 16 * row + s + 1)
                        act.activation(PT[:, g % 2, j, 512:W], psE[:, 512:W], ACT.Exp).then_inc(expB, 1)
                    if s in (0, 12) and (u.C if s == 0 else u.B):
                        row, half = (t - 2, 1) if s == 0 else (t - 1, 0)
                        act.wait_ge(mT_done, 2 * row + half + 1)
                        act.wait_ge(m_stored, (2 * row + half) * 16)
                        act.activation(mT[:], misc[0:96, 0:64].bitcast(BF16), ACT.Copy).then_inc(mT_ready, 1)
                    if s == 5 and u.A:
                        act.wait_ge(zT_done, t + 1)
                        if u.B:
                            act.wait_ge(k_done, t)
                            act.wait_ge(v_done, t)
                        act.activation(hT[:], misc[:], ACT.Identity, bias=S.modT[:, 0, bass.ds(t, 1)],
                                       scale=S.modT[:, 1, bass.ds(t, 1)]).then_inc(hT_ready, 1)
                    if s in (7, 8) and u.A:
                        side = s - 7
                        act.wait_ge((q_done, k_done)[side], t + 1)
                        act.wait_ge(parts_ready, 2 * t)
                        act.activation(qk[:, side], misc[:], ACT.Identity, bias=qkb[:, side:side + 1],
                                       scale=(SC, 1.0)[side]).then_inc((q_ready, k_ready)[side], 1)
                    if s == 9 and u.D:
                        row = t - 3
                        act.wait_ge(nT_done, row + 1)
                        act.activation(nT[:], misc[:], ACT.Copy).then_inc(nT_ready, 1)

            turns(act, turn)

        @block.gpsimd
        def _(pool):
            pool.memset(qst[32:64].bitcast(U32), 0)
            pool.memset(kst[32:64].bitcast(U32), 0).then_inc(pool_cleared, 1)
            pool.wait_ge(pool_cleared, 1)

            def turn(u):
                if not u.A:
                    return
                t = u.t
                c = Chain(pool, parts_chain, t, 6)
                for side in range(2):
                    f, r, p3 = qk[:, side], rest[:, side], parts[:, side]
                    if u.B and side == 0:
                        pool.wait_ge(parts_stored, 32 * t)
                    wait_alone(pool, (q_ready, k_ready)[side], t + 1)
                    c.link(pool.tensor_scalar(p3[:, 0], f, 1.0, 0.0, ALU.mult, ALU.add))
                    c.link(pool.tensor_tensor(r, f, p3[:, 0], ALU.subtract), alone=True)
                    c.link(pool.tensor_scalar(p3[:, 1], r, 1.0, 0.0, ALU.mult, ALU.add))
                    pool.tensor_tensor(p3[:, 2], r, p3[:, 1], ALU.subtract).then_inc(parts_ready, 1)
                c.end()
                if not u.steady and t == 0:
                    pool.wait_ge(parts_ready, 2)
                    pool.memset(qst[64:M0].bitcast(U32), 0).then_inc(pool_cleared, 1)
                    pool.wait_ge(pool_cleared, 2)
            turns(pool, turn)

        @block.vector
        def _(dve):
            c = Chain(dve, chain)
            rstd_step(S, dve, c)
            dve.wait_ge(loaded, 80)
            c.then(dve.tensor_scalar(qkb[:, 0:1], qkb[:, 0:1], SC, None, ALU.mult))
            n0 = c.n
            STEPS = {"A": 0, "B": 6, "C": 2, "D": 2 + ADD_STEPS}

            def chain_before(t):
                return sum(STEPS[x] for k in range(t) for x, lag in zip("ABCD", range(4)) if live(k, lag))

            def turn(u):
                t = u.t
                c = Chain(dve, chain, 0, u.steady)
                c.base = n0 + (chain_before(t) if not u.steady else
                               (t - LOOP0) * sum(STEPS.values()) + chain_before(LOOP0))

                def split_max(row, half):
                    dve.wait_ge(maxB, 16 * row + 8 * half + 8)
                    dve.wait_ge(maxA, 16 * row + 8 * half + 8)
                    if half or u.steady or t > 1:
                        dve.wait_ge(mT_done, 2 * row + half)
                    m = mrow[:, 8 * half:8 * half + 8].rearrange("p h i -> p (h i)")
                    c.link(dve.tensor_scalar(mpart[:, 0], m, -1.0, None, ALU.mult))
                    c.link(dve.scalar_tensor_tensor(mrest[:], m, -1.0, mpart[:, 0], ALU.mult, ALU.subtract))
                    c.link(dve.tensor_copy(mpart[:, 1], mrest[:]))
                    dve.tensor_tensor(mpart[:, 2], mrest[:], mpart[:, 1], ALU.subtract).then_inc(m_ready, 1)

                def divide(row, par, g):
                    dve.wait_ge(rawT_done, 4 * row + g + 1)
                    tok = misc[:].rearrange("p (i j x) -> p i j x", i=NI, j=GH)
                    c.link(dve.reciprocal(rden[:], tok[:, :, :, HD]))
                    for i in range(NI):
                        ins = dve.tensor_tensor(norm[:, par, i, GH * g:GH * g + GH], tok[:, i, :, 0:HD],
                                                bcast(rden[:, i], 2, HD), ALU.mult)
                    ins.then_inc(norm_ready, 1)

                for s in range(16):
                    if u.B:
                        row = t - 1
                        for i in (3, 2, 0, 1):
                            if i == 3:
                                wait_alone(dve, sA, 16 * row + s + 1)
                            if i == 2:
                                wait_alone(dve, sB, 16 * row + s + 1)
                            ps = psS[:, COL_Q[i]:COL_Q[i] + (i + 1) * P]
                            ins = dve.tensor_tensor_reduce(ps, ps, mask[:, (3 - i) * P:T], 1.0, -3e38, ALU.add,
                                                           ALU.max, mrow[:, s, i:i + 1])
                            if i in (3, 1):
                                ins.then_inc(maxA if i == 3 else maxB, 1)
                        if s in (7, 15):
                            split_max(row, s // 8)
                    if s == 0 and u.A:
                        if u.B:
                            dve.wait_ge(zT_done, t)
                        normalise(S, dve, t, z).then_inc(z_ready, 1)
                    if s == 4 and u.B:
                        row = t - 1
                        dve.wait_ge(v_done, row + 1)
                        if u.D:
                            dve.wait_ge(pv_done, 4 * (t - 3) + 4)
                        c_v = V[:, 1 - u.par, :, :, 0:HD]
                        for i in range(NI):
                            ins = dve.tensor_tensor(c_v[:, i], misc[:, i * P:(i + 1) * P].rearrange(
                                "p (h d) -> p h d", h=H), vob[:, 0].rearrange("p (h d) -> p h d", h=H), ALU.add)
                        ins.then_inc(v_ready, 1)
                    if s in (1, 6) and u.D:
                        divide(t - 3, 1 - u.par, 2 if s == 1 else 3)
                    if s in (11, 13) and u.C:
                        divide(t - 2, u.par, 0 if s == 11 else 1)
                    if s == 10 and u.D:
                        row = t - 3
                        dve.wait_ge(o_done, row + 1)
                        dve.tensor_tensor(S.upd[:], misc[:].rearrange("p (i f) -> p i f", i=NI),
                                          bcast(vob[:, 1], 1, NI), ALU.add).then_inc(added, 1)
                        dve.wait_ge(added, row + 1)
                        add_result(S, dve, c, row, 0, S.upd[:])
                    if s == 12 and u.D:
                        new_stats(S, dve, c, t - 3)
                assert c.n == sum(k for k, on in zip(STEPS.values(), (u.A, u.B, u.C, u.D)) if on)
                if not u.steady and t == LOOP0 - 1:
                    wait_gates(S, dve)
                if not u.steady and t == 0:
                    dve.memset(V[:], 0.0).then_inc(cleared, 1)
                    dve.wait_ge(cleared, 1)
                    dve.memset(kst[M0:K2].bitcast(U32), 0x3F803F80)
                    dve.memset(V[:, :, :, :, HD:HD + 1], 1.0).then_inc(cleared, 1)
                    dve.memset(kst[64:M0].bitcast(U32), 0).then_inc(cleared, 1)

            turns(dve, turn)


def gqa_attn_stage(S):
    nc = S.nc
    H, HD, KV = 16, 64, 4
    PAIRS = H // 2
    W = 10 * P
    COL_Q = {3: 0, 2: 512, 0: 896, 1: 1024}
    COL_K = {0: 0, 1: 512, 3: 896, 2: 1024}
    SC = float(HD) ** -0.5
    n = "L1a_"
    sem = lambda s: S.sem(n + s)
    (loaded, cleared, setup, setup_act, chain, z_ready, zT_done, hT_ready, proj_done, v_ready, kA_ready,
     kB_ready, qA_ready, qD_ready, bias_ready, bias_chain, sA, sB, maxA, maxB, m_ready) = map(sem, (
         "loaded", "cleared", "setup", "setup_act", "dve", "z", "zT", "hT", "proj", "v", "kA",
         "kB", "qA", "qD", "bias", "bias_chain", "sA", "sB", "maxA", "maxB", "m"))
    (exp_done, rsum_ready, p_ready, tA, tB, ptA, ptB, pv_done, outT_ready, o_done) = map(sem, (
        "exp", "rsum", "p", "tA", "tB", "ptA", "ptB", "pv", "outT", "o"))
    with ExitStack() as ctx:
        sb = lambda name, shape, dt=F32: ctx.enter_context(nc.sbuf_tensor(n + name, shape, dt))
        pt = lambda name, shape, dt=F32: ctx.enter_context(nc.psum_tensor(n + name, shape, dt))
        wq = sb("wq", [P, H, HD // 2, 2])
        wr = sb("wr", [P, H, HD // 2, 2])
        wt = sb("wt", [P, H, HD // 2])
        wk = sb("wk", [P, KV, 2, HD])
        wv = sb("wv", [P, KV * HD])
        wo = sb("wo", [P, PAIRS, D])
        ang = sb("ang", [P, 2, H])
        turns_ = sb("angle_turns", [P, 2, H])
        slope = sb("slope", [P, H])
        cneg = sb("cneg", [P, T])
        mask = sb("mask", [P, P])
        z = sb("z", [P, NI, D])
        hT = sb("hT", [P, T])
        q = sb("q", [P, 2, PAIRS, T])
        k = sb("k", [P, 2, 2, KV, T])
        V = sb("V", [P, 2, NI, KV * HD])
        bias = sb("bias", [P, 2, T])
        Pm = sb("Pm", [P, 4, W])
        mrow = sb("mrow", [P, 4, NI])
        mneg = sb("mneg", [P, 4, NI])
        sums = sb("sums", [P, 4, NI])
        rsum = sb("rsum", [P, 4, NI])
        PT = sb("PT", [P, 4, W])
        outT = sb("outT", [P, PAIRS, T])
        psS = pt("psS", [P, 3 * 512])
        psT = pt("psT", [P, 3 * 512])
        psO = pt("psO", [P, T])
        misc = pt("misc", [P, T])
        block = ctx.enter_context(nc.Block())

        USES = [(3, "out", 0, 2, (chain, None, None)), (4, "z", 0, 0, (hT_ready, 1, 1)),
                (5, "v", 0, 0, (v_ready, 2, 1)), (5, "v", 1, 0, (v_ready, 2, 2))]
        USES += [(6 + g, "k", g, 0, (kB_ready, KV, g + 1)) for g in range(KV)]
        USES += [(s, "q", p, 0, ((qA_ready, qD_ready)[p % 2], PAIRS // 2, p // 2 + 1))
                 for p, s in enumerate((10, 11, 12, 12, 13, 13, 14, 15))]
        Z_USE, V_USE, K_USE, Q_USE = 1, 2, 4, 8
        A_PROJ = 14
        LOOP0 = 2
        live = lambda t, lag: 0 <= t - lag < NB

        class Turn:

            def __init__(self, t, parity, steady):
                self.t, self.par, self.steady = t, parity, steady
                self.A, self.C, self.D = (steady or live(t, lag) for lag in range(3))

            def runs(self, back, lag):
                return self.steady or live(self.t - back, lag)

            def bank(self, at):
                return psS[:, 0:T] if not self.steady and self.t == 0 and at % 2 else misc[:]

            def misc_copied_out(self, eng, at):
                for back in (0, 1):
                    in_turn_0 = not self.steady and self.t == back
                    for k_, (_, name, _, lag, (sem_, per, value)) in reversed(list(enumerate(USES[:at] if back == 0 else USES))):
                        if in_turn_0 and k_ % 2 != (at % 2 if back == 0 else 0):
                            continue
                        if self.runs(back, lag):
                            if name == "out":
                                eng.wait_ge(outs_read, self.t - back - lag + 1)
                            else:
                                eng.wait_ge(sem_, (self.t - back - lag) * per + value)
                                if name == "k":
                                    eng.wait_ge(kA_ready, (self.t - back - lag) * per + value)
                            return

        outs_read = sem("outs_read")

        def turns(eng, body):
            for t in range(LOOP0):
                body(Turn(t, t % 2, False))
            with eng.Fori(LOOP0 // 2, NB // 2) as pair:
                for u in range(2):
                    body(Turn(pair * 2 + u, u, True))
            for t in range(NB, NB + 2):
                body(Turn(t, t % 2, False))

        @block.sync
        def _(sp):
            for dst, src in ((wq, "wq"), (wk, "wk"), (wv, "wv"), (wo, "wo")):
                sp.dma_start(dst[:], S.dram[n + src]).then_inc(loaded, 16)
            sp.dma_start(cneg[:], S.dram["cneg"]).then_inc(loaded, 16)
            sp.dma_start(mask[:], S.dram["mask"][:, 3 * P:]).then_inc(loaded, 16)
            sp.dma_start(ang[:, 1], S.dram[n + "angle"].partition_broadcast(P)).then_inc(loaded, 16)
            sp.dma_start(slope[:], S.dram[n + "slopes"].partition_broadcast(P)).then_inc(loaded, 16)
            load_gates(S, sp, 1)

        @block.tensor
        def _(pe):
            def scores(t, row, par, h):
                g, pair, odd = h // 4, h // 2, h % 2
                if h % 2 == 0:
                    pe.wait_ge((qA_ready, qD_ready)[pair % 2], PAIRS // 2 * row + pair // 2 + 1)
                if h % 4 == 0:
                    pe.wait_ge(kA_ready, KV * row + g + 1)
                    pe.wait_ge(kB_ready, KV * row + g + 1)
                for i in (3, 2, 0, 1):
                    if i == 3:
                        pe.wait_ge(maxA, 16 * row + h)
                    if i == 2:
                        pe.wait_ge(maxB, 16 * row + h)
                    ins = pe.matmul(psS[:, COL_Q[i]:COL_Q[i] + (i + 1) * P], q[:, par, pair, i * P:(i + 1) * P],
                                    k[:, par, odd, g, 0:(i + 1) * P], start=True, stop=True)
                    if i in (3, 1):
                        ins.then_inc(sA if i == 3 else sB, 1)

            def transposes(G, h):
                pe.wait_ge(p_ready, G + 1)
                for part, tiles in enumerate(((0,), (1, 3, 2))):
                    pe.wait_ge((ptA, ptB)[part], G)
                    for kt in tiles:
                        for i in range(kt, NI):
                            c = COL_K[kt] + (i - kt) * P
                            ins = pe.transpose(psT[:, c:c + P], Pm[:, h % 4, COL_Q[i] + kt * P:COL_Q[i] + (kt + 1) * P],
                                               S.ident[:])
                    ins.then_inc((tA, tB)[part], 1)

            def values(pair_count, row, vpar, pair):
                pe.wait_ge(ptA, 2 * pair_count + 2)
                pe.wait_ge(ptB, 2 * pair_count + 2)
                if pair == 0:
                    pe.wait_ge(v_ready, 2 * row + 2)
                pe.wait_ge(outT_ready, pair_count)
                g = pair // 2
                for kt in range(NI):
                    for j in range(2):
                        ins = pe.matmul(psO[64 * j:64 * j + 64, kt * P:T], V[:, vpar, kt, g * HD:(g + 1) * HD],
                                        PT[:, (2 * pair + j) % 4, COL_K[kt]:COL_K[kt] + (4 - kt) * P],
                                        start=(kt == 0), stop=(kt == NI - 1), skip_group_check=True)
                ins.then_inc(pv_done, 1)

            def use(u, at):
                _, name, x, lag, _ = USES[at]
                if not u.runs(0, lag):
                    return
                u.misc_copied_out(pe, at)
                row = u.t - lag
                bank = u.bank(at)
                if name == "out":
                    pe.wait_ge(outT_ready, PAIRS * (row + 1))
                    for i in range(NI):
                        for p in range(PAIRS):
                            ins = pe.matmul(bank[:, i * P:(i + 1) * P], outT[:, p, i * P:(i + 1) * P], wo[:, p],
                                            start=(p == 0), stop=(p == PAIRS - 1))
                    ins.then_inc(o_done, 1)
                elif name == "z":
                    pe.wait_ge(z_ready, row + 1)
                    for i in range(NI):
                        ins = pe.transpose(bank[:, i * P:(i + 1) * P], z[:, i], S.ident[:])
                    ins.then_inc(zT_done, 1)
                else:
                    if not u.steady and row == 0 and name == "v":
                        pe.wait_ge(loaded, 8 * 16)
                    if not u.steady and row == 0 and name == "q":
                        pe.wait_ge(setup, 12)
                    pe.wait_ge(hT_ready, row + 1)
                    if name == "v":
                        for i in range(2):
                            t_ = 2 * x + i
                            ins = pe.matmul(bank[:, i * 256:(i + 1) * 256], hT[:, t_ * P:(t_ + 1) * P], wv[:],
                                            start=True, stop=True)
                    elif name == "k":
                        ins = pe.matmul(bank, wk[:, x].rearrange("p a d -> p (a d)"), hT[:], start=True, stop=True)
                    else:
                        ins = pe.matmul(bank, wr[:, 2 * x:2 * x + 2].rearrange("p h a b -> p (h a b)"), hT[:],
                                        start=True, stop=True)
                    ins.then_inc(proj_done, 1)

            def turn(u):
                if not u.steady and u.t == 1:
                    pe.wait_ge(cleared, 1)
                    pe.wait_ge(qD_ready, PAIRS // 2)
                for s in range(H):
                    at = [k_ for k_, x in enumerate(USES) if x[0] == s]
                    G = 16 * (u.t - 1) + s
                    if u.C:
                        scores(u.t, u.t - 1, 1 - u.par, s)
                    if len(at) > 1:
                        use(u, at[0])
                    if (u.D if s < 2 else u.C):
                        transposes(G - 2, (s - 2) % H)
                    if s % 2 == 0 and (u.D if s < 4 else u.C):
                        pair = (s // 2 - 2) % PAIRS
                        row = u.t - (2 if s < 4 else 1)
                        values(PAIRS * (u.t - 1) + s // 2 - 2, row, u.par if s < 4 else 1 - u.par, pair)
                    if at:
                        use(u, at[-1])

            turns(pe, turn)

        @block.scalar
        def _(act):
            def take_q(u, p):
                act.wait_ge(proj_done, A_PROJ * u.t + 2 + KV + p + 1)
                act.activation(q[:, u.par, p], u.bank(Q_USE + p), ACT.Copy).then_inc(qA_ready, 1)

            def turn(u):
                t = u.t
                row = t - 1
                for s in range(H):
                    G = 16 * row + s
                    if s in (12, 13) and u.A:
                        take_q(u, 2 * s - 22)
                    if (u.D if s < 2 else u.C):
                        h = (s - 2) % H
                        act.wait_ge(tA, G - 1)
                        if u.D or s >= 6:
                            act.wait_ge(pv_done, PAIRS * row + s // 2 - 3)
                        act.activation(PT[:, h % 4, 0:512], psT[:, 0:512], ACT.Copy).then_inc(ptA, 1)
                    if u.C:
                        act.wait_ge(m_ready, G + 1)
                        for i in (3, 2, 0, 1):
                            part = Pm[:, s % 4, COL_Q[i]:COL_Q[i] + (i + 1) * P]
                            ins = act.activation(part, part, ACT.Exp, bias=mneg[:, s % 4, i:i + 1],
                                                 accum_out=sums[:, s % 4, i:i + 1])
                        ins.then_inc(exp_done, 1)
                    if not u.A:
                        continue
                    if s == 4:
                        act.wait_ge(zT_done, t + 1)
                        act.wait_ge(proj_done, A_PROJ * t)
                        act.activation(hT[:], u.bank(Z_USE), ACT.Identity, bias=S.modT[:, 0, bass.ds(t, 1)],
                                       scale=S.modT[:, 1, bass.ds(t, 1)]).then_inc(hT_ready, 1)
                        if not u.steady and t == 0:
                            act.wait_ge(setup, 5)
                            act.activation(ang[:], ang[:], ACT.Sin).then_inc(setup_act, 1)
                            act.activation(slope[:], slope[:], ACT.Exp).then_inc(setup_act, 1)
                    if 6 <= s < 10:
                        act.wait_ge(proj_done, A_PROJ * t + 2 + s - 5)
                        act.activation(k[0:64, u.par, 0, s - 6], u.bank(K_USE + s - 6)[0:64], ACT.Copy).then_inc(kA_ready, 1)
                    for slot, name, p, _, _ in USES:
                        if slot == s and name == "q" and p % 2 == 0 and p not in (2, 4):
                            take_q(u, p)

            turns(act, turn)

        @block.gpsimd
        def _(pool):
            pool.memset(k[64:128, :, 0], 0.0)
            pool.memset(k[0:64, :, 1], 0.0).then_inc(cleared, 1)
            pool.wait_ge(cleared, 1)
            pool.wait_ge(loaded, 8 * 16)
            pool.wait_ge(setup_act, 2)

            def turn(u):
                row = u.t - 1
                for s in range(H):
                    G = 16 * row + s
                    if u.C:
                        if u.D or s >= 2:
                            wait_alone(pool, maxB, G - 1)
                        pool.tensor_scalar(bias[:, s % 2], cneg[:], slope[:, s:s + 1], 0.0, ALU.mult,
                                           ALU.add).then_inc(bias_chain, 1)
                        pool.wait_ge(bias_chain, G + 1)
                        pool.tensor_tensor(bias[:, s % 2, 3 * P:], bias[:, s % 2, 3 * P:], mask[:],
                                           ALU.add).then_inc(bias_ready, 1)
                    if (u.D if s < 1 else u.C):
                        h = (s - 1) % H
                        wait_alone(pool, rsum_ready, G)
                        for i in range(NI):
                            part = Pm[:, h % 4, COL_Q[i]:COL_Q[i] + (i + 1) * P]
                            ins = pool.tensor_scalar(part, part, rsum[:, h % 4, i:i + 1], 1.0, ALU.mult, ALU.mult)
                        ins.then_inc(p_ready, 1)

            turns(pool, turn)

        @block.vector
        def _(dve):
            def rotate_weights():
                dve.wait_ge(loaded, 8 * 16)
                c = Chain(dve, setup)
                ROUND = 1.5 * 2.0 ** 23
                TWO_PI_HI = 6.28125
                TWO_PI_LO = 2 * np.pi - 6.28125
                PI = float(np.nextafter(np.float32(np.pi), np.float32(0)))
                c.link(dve.tensor_scalar(ang[:, 0], ang[:, 1], float(np.pi / 2), None, ALU.add))
                c.link(dve.tensor_scalar(turns_[:], ang[:], 1.0 / (2 * np.pi), ROUND, ALU.mult, ALU.add))
                c.link(dve.tensor_scalar(turns_[:], turns_[:], -ROUND, None, ALU.add))
                c.link(dve.scalar_tensor_tensor(ang[:], turns_[:], -TWO_PI_HI, ang[:], ALU.mult, ALU.add))
                c.link(dve.scalar_tensor_tensor(ang[:], turns_[:], -TWO_PI_LO, ang[:], ALU.mult, ALU.add))
                assert c.n == 5
                dve.wait_ge(setup_act, 1)
                c.link(dve.tensor_scalar(ang[:], ang[:], SC, None, ALU.mult))
                cos, sin = (bcast(ang[:, a], 2, HD // 2) for a in range(2))
                c.link(dve.tensor_tensor(wt[:], wq[:, :, :, 1], sin, ALU.mult))
                c.link(dve.tensor_tensor(wr[:, :, :, 0], wq[:, :, :, 0], cos, ALU.mult))
                c.link(dve.tensor_tensor(wr[:, :, :, 0], wr[:, :, :, 0], wt[:], ALU.subtract))
                c.link(dve.tensor_tensor(wt[:], wq[:, :, :, 0], sin, ALU.mult))
                c.link(dve.tensor_tensor(wr[:, :, :, 1], wq[:, :, :, 1], cos, ALU.mult))
                c.link(dve.tensor_tensor(wr[:, :, :, 1], wr[:, :, :, 1], wt[:], ALU.add))
                assert c.n == 12

            c = Chain(dve, chain)
            rstd_step(S, dve, c)
            n0 = c.n

            def take_v(u, x):
                dve.wait_ge(proj_done, A_PROJ * u.t + x + 1)
                if u.D and x == 0:
                    dve.wait_ge(pv_done, PAIRS * (u.t - 1))
                dve.tensor_copy(V[:, u.par, 2 * x:2 * x + 2].rearrange("p i f -> p (i f)"),
                                u.bank(V_USE + x)).then_inc(v_ready, 1)

            def turn(u):
                t = u.t
                row = t - 1
                c = Chain(dve, chain, 0, u.steady)
                for s in range(H):
                    G = 16 * row + s
                    if (u.D if s < 1 else u.C):
                        h = (s - 1) % H
                        dve.wait_ge(exp_done, G)
                        dve.reciprocal(rsum[:, h % 4], sums[:, h % 4]).then_inc(rsum_ready, 1)
                    if u.C:
                        dve.wait_ge(bias_ready, G + 1)
                        if u.D or s >= 4:
                            dve.wait_ge(tB, G - 3)
                        for i in (3, 2, 0, 1):
                            if i in (3, 2):
                                wait_alone(dve, sA if i == 3 else sB, G + 1)
                            ins = dve.tensor_tensor_reduce(
                                Pm[:, s % 4, COL_Q[i]:COL_Q[i] + (i + 1) * P], psS[:, COL_Q[i]:COL_Q[i] + (i + 1) * P],
                                bias[:, s % 2, (3 - i) * P:T], 1.0, -3e38, ALU.add, ALU.max, mrow[:, s % 4, i:i + 1])
                            if i in (3, 1):
                                ins.then_inc(maxA if i == 3 else maxB, 1)
                        dve.wait_ge(maxB, G + 1)
                        dve.wait_ge(maxA, G + 1)
                        dve.tensor_scalar(mneg[:, s % 4], mrow[:, s % 4], -1.0, None, ALU.mult).then_inc(m_ready, 1)
                    if s == 5 and u.A:
                        take_v(u, 0)
                    if (u.D if s < 2 else u.C):
                        h = (s - 2) % H
                        dve.wait_ge(tB, G - 1)
                        if u.D or s >= 6:
                            dve.wait_ge(pv_done, PAIRS * row + s // 2 - 3)
                        dve.tensor_copy(PT[:, h % 4, 512:W], psT[:, 512:W]).then_inc(ptB, 1)
                    if s % 2 == 0 and (u.D if s < 4 else u.C):
                        pair = (s // 2 - 2) % PAIRS
                        dve.wait_ge(pv_done, PAIRS * row + s // 2 - 1)
                        if s == 4 and u.D:
                            dve.wait_ge(o_done, row)
                        dve.tensor_copy(outT[:, pair], psO[:]).then_inc(outT_ready, 1)
                    if s == 3 and u.A:
                        if not (not u.steady and t == 0):
                            dve.wait_ge(zT_done, t)
                        normalise(S, dve, t, z).then_inc(z_ready, 1)
                        if not u.steady and t == 0:
                            rotate_weights()
                    if s == 3 and u.D:
                        r = t - 2
                        c.base = n0 + r * (ADD_STEPS - 1)
                        dve.wait_ge(o_done, r + 1)
                        add_result(S, dve, c, r, 0, misc[:].rearrange("p (i f) -> p i f", i=NI), outs_read)
                    if s == 4 and u.D:
                        new_stats(S, dve, c, t - 2)
                    if s == 5 and u.A:
                        take_v(u, 1)
                    if 6 <= s < 10 and u.A:
                        dve.wait_ge(proj_done, A_PROJ * t + 2 + s - 5)
                        dve.tensor_copy(k[64:128, u.par, 1, s - 6], u.bank(K_USE + s - 6)[64:128]).then_inc(kB_ready, 1)
                    for slot, name, p, _, _ in USES:
                        if u.A and slot == s and name == "q" and p % 2:
                            dve.wait_ge(proj_done, A_PROJ * t + 2 + KV + p + 1)
                            dve.tensor_copy(q[:, u.par, p], u.bank(Q_USE + p)).then_inc(qD_ready, 1)
                if not u.steady and t == LOOP0 - 1:
                    wait_gates(S, dve)

            turns(dve, turn)


def expert_choice_stage(S):
    nc = S.nc
    E, NG, K = 8, 4, NB * T // 8
    F = int(D * 4 * (2.0 / 3.0))
    NC = 3
    LAST = 96
    n = "L1f_"
    with ExitStack() as ctx:
        sb = lambda name, shape, dt=F32: ctx.enter_context(nc.sbuf_tensor(n + name, shape, dt))
        hT = sb("hT", [P, NB, T])
        prob = sb("prob", [P, E, NT])
        ws = sb("ws", [P, E, NT])
        wu = sb("wu", [P, NG, NC * P])
        wd = sb("wd", [P, NG, NC, 2 * D])
        bu = sb("bu", [P, NG, NC])
        with ExitStack() as inner:
            expert_choice_weights(S, n, inner, hT, prob, wu, wd, bu)
        S.nc.all_engine_barrier()
        with ExitStack() as inner:
            expert_choice_experts(S, n, inner, hT, prob, ws, wu, wd, bu, K, LAST)


def expert_choice_weights(S, n, ctx, hT, prob, wu, wd, bu):
    nc = S.nc
    E = prob.shape[1]
    small, loaded, chain, z_ready, zT_done, hT_ready, logits_done, logits_read, shifted, exp_done = map(
        lambda s: S.sem(n + s), ("small", "loaded", "dve", "z", "zT", "hT", "logits", "logits_read", "shifted", "exp"))
    sb = lambda name, shape, dt=F32: ctx.enter_context(nc.sbuf_tensor(n + name, shape, dt))
    pt = lambda name, shape, dt=F32: ctx.enter_context(nc.psum_tensor(n + name, shape, dt))
    wr, br = sb("wr", [P, E]), sb("br", [P, E])
    z = sb("z", [P, 2, NI, D])
    mx, sm = sb("mx", [P, NT]), sb("sm", [P, NT])
    psT = pt("psT", [P, 2, T])
    psL = pt("psL", [P, 2, T])
    with nc.Block() as block:
        @block.sync
        def _(sp):
            sp.dma_start(wr[:], S.dram[n + "wr"]).then_inc(small, 16)
            sp.dma_start(br[:], S.dram[n + "br"].partition_broadcast(P)).then_inc(small, 16)
            sp.dma_start(bu[:], S.dram[n + "bu"]).then_inc(loaded, 16)
            for g in range(4):
                sp.dma_start(wu[:, g], S.dram[n + "wu"][:, g]).then_inc(loaded, 16)
                sp.dma_start(wd[:, g], S.dram[n + "wd"][:, g]).then_inc(loaded, 16)
            sp.wait_ge(loaded, 9 * 16)

        @block.tensor
        def _(pe):
            pe.wait_ge(small, 32)

            def transposes(row, par):
                pe.wait_ge(z_ready, row + 1)
                for i in range(NI):
                    ins = pe.transpose(psT[:, par, i * P:(i + 1) * P], z[:, par, i], S.ident[:])
                ins.then_inc(zT_done, 1)

            def logits(row, par):
                pe.wait_ge(hT_ready, row + 1)
                for i in range(NI):
                    ins = pe.matmul(psL[:, par, i * E:(i + 1) * E], hT[:, row, i * P:(i + 1) * P],
                                    wr[:], start=True, stop=True)
                ins.then_inc(logits_done, 1)

            for b in range(NB):
                if b >= 2:
                    pe.wait_ge(hT_ready, b - 1)
                transposes(b, b % 2)
                if b > 0:
                    if b > 2:
                        pe.wait_ge(logits_read, b - 2)
                    logits(b - 1, (b - 1) % 2)
            pe.wait_ge(logits_read, NB - 2)
            logits(NB - 1, (NB - 1) % 2)

        @block.scalar
        def _(act):
            for b in range(NB):
                act.wait_ge(zT_done, b + 1)
                act.activation(hT[:, b], psT[:, b % 2], ACT.Identity, bias=S.modT[:, 3, b:b + 1],
                               scale=S.modT[:, 4, b:b + 1]).then_inc(hT_ready, 1)
            act.wait_ge(shifted, 1)
            act.activation(prob[:], prob[:], ACT.Exp).then_inc(exp_done, 1)

        @block.vector
        def _(dve):
            c = Chain(dve, chain)
            rstd_step(S, dve, c)
            dve.wait_ge(small, 32)

            def take_logits(b):
                dve.wait_ge(logits_done, b + 1)
                dve.tensor_tensor(prob[:, :, b * NI:(b + 1) * NI], psL[:, b % 2, 0:NI * E].rearrange("p (i e) -> p e i", e=E),
                                  bcast(br[:], 2, NI), ALU.add).then_inc(logits_read, 1)

            for b in range(NB):
                if b >= 2:
                    dve.wait_ge(zT_done, b - 1)
                normalise(S, dve, b, z[:, b % 2]).then_inc(z_ready, 1)
                if b >= 2:
                    take_logits(b - 2)
            take_logits(NB - 2)
            take_logits(NB - 1)
            dve.wait_ge(logits_read, NB)
            by_token = prob[:].rearrange("p e t -> p t e")
            c.link(dve.tensor_reduce(mx[:], by_token, AX.X, ALU.max))
            dve.tensor_tensor(prob[:], prob[:], bcast(mx[:], 1, E), ALU.subtract).then_inc(shifted, 1)
            dve.wait_ge(exp_done, 1)
            c.link(dve.tensor_reduce(sm[:], by_token, AX.X, ALU.add))
            c.link(dve.reciprocal(sm[:], sm[:]))
            c.then(dve.tensor_tensor(prob[:], prob[:], bcast(sm[:], 1, E), ALU.mult))


def expert_choice_experts(S, n, ctx, hT, prob, ws, wu, wd, bu, K, LAST):
    nc = S.nc
    E = prob.shape[1]
    NG, NC = wd.shape[1], wd.shape[2]
    AHEAD = 16
    HALF = E // 2
    loaded, chain, turned, turned_out, part_ready, total_done, v_done, eq_ready, ws_ready = map(
        lambda s: S.sem(n + s), ("tri_loaded", "top", "turned", "turned_out", "part", "total", "v", "eq", "ws"))
    ones_ready, sum_chain, up_done, mid_ready, down_done, used, added = map(
        lambda s: S.sem(n + s), ("ones", "sum", "up", "mid", "down", "used", "added"))
    sb = lambda name, shape, dt=F32: ctx.enter_context(nc.sbuf_tensor(n + name, shape, dt))
    pt = lambda name, shape, dt=F32: ctx.enter_context(nc.psum_tensor(n + name, shape, dt))
    tri = sb("tri", [P, P])
    blocks = sb("blocks", [P, P])
    first = sb("first", [P, HALF])
    pT = sb("pT", [P, 2, P])
    found = sb("found", [P, 2, 3, P])
    cand = sb("cand", [P, 2, 3])
    v = sb("v", [P, 2])
    best = sb("best", [P, 2])
    step = sb("step", [P, 2, 3])
    cnt = sb("cnt", [P, 2, 3])
    vrow = sb("vrow", [P, 2, HALF])
    vall = sb("vall", [P, E])
    hit = sb("hit", [P, E, NT])
    eq = sb("eq", [P, E, NT])
    pre = sb("pre", [P, 2, E, NT])
    more = sb("more", [P, E])
    need = sb("need", [P, E])
    mid = sb("mid", [P, AHEAD, NC, T])
    y = sb("y", [P, NI, D])
    psU = pt("psU", [P, NC, T])
    psN = pt("psN", [P, T])
    psO = pt("psO", [P, 2, NI, 2 * D])
    psP = psO[:, 0, 0:2].rearrange("p i x -> p (i x)")
    psV = psO[:, 0, 2:4].rearrange("p i x -> p (i x)")
    psE = psO[:, 1, 0:2].rearrange("p i (e t) -> p i e t", e=E)
    LEAST = 2.0 ** -126
    EXPONENT = [(2.0 ** unit, 2.0 ** (2 * unit), 2.0 ** (3 * unit)) for unit in (16, 4, 1)]
    PAIRS_OF_BITS = 11
    ROUNDS = 1 + len(EXPONENT) + 1 + PAIRS_OF_BITS
    with nc.Block() as block:
        @block.sync
        def _(sp):
            sp.dma_start(blocks[:], S.dram["blocks"]).then_inc(loaded, 16)
            sp.dma_start(first[:], S.dram["first"]).then_inc(loaded, 16)
            sp.dma_start(tri[:], S.dram["tri"]).then_inc(loaded, 16)

        @block.gpsimd
        def _(pool):
            pool.memset(mid[LAST:P, :, NC - 1], 1.0).then_inc(ones_ready, 1)

        @block.tensor
        def _(pe):
            def up(s, c):
                if s > 0:
                    pe.wait_ge(mid_ready, NC * (s - 1) + c + 1)
                m = P if c < NC - 1 else LAST
                pe.matmul(psU[0:m, c], wu[:, s % NG, c * P:c * P + m], hT[:, s // NG], start=True, stop=True).then_inc(up_done, 1)

            def down(s):
                if s >= 2:
                    pe.wait_ge(used, s - 1)
                for i in range(NI):
                    for c in range(NC):
                        ins = pe.matmul(psO[:, s % 2, i], mid[:, s % AHEAD, c, i * P:(i + 1) * P], wd[:, s % NG, c],
                                        start=(c == 0), stop=(c == NC - 1))
                ins.then_inc(down_done, 1)

            for h in range(2):
                ins = pe.transpose(psP[:, h * P:(h + 1) * P], prob[:, h * HALF:(h + 1) * HALF].rearrange("p e t -> p (e t)"),
                                   S.ident[:])
            ins.then_inc(turned, 1)
            pe.wait_ge(loaded, 3 * 16)
            early = AHEAD * NC // ROUNDS
            for k in range(ROUNDS):
                pe.wait_ge(part_ready, k + 1)
                pe.matmul(psN[:, 0:6], blocks[:], cnt[:].rearrange("p h k -> p (h k)"), start=True, stop=True).then_inc(total_done, 1)
                for x in range(k * early, (k + 1) * early):
                    up(x // NC, x % NC)
            for x in range(ROUNDS * early, AHEAD * NC):
                up(x // NC, x % NC)
            pe.wait_ge(v_done, 1)
            pe.matmul(psV[:, 0:E], S.ones[:], vrow[:].rearrange("p h e -> p (h e)"), start=True, stop=True).then_inc(total_done, 1)
            pe.wait_ge(eq_ready, 1)
            flat = eq[:].rearrange("p e t -> p (e t)")
            pe.matmul(psE[:, 0].rearrange("p e t -> p (e t)"), tri[:], flat, start=True, stop=True)
            pe.matmul(psE[:, 1].rearrange("p e t -> p (e t)"), S.ones[:], flat, start=True, stop=True)
            pe.wait_ge(eq_ready, 2)
            pe.matmul(psN[:, 0:E], S.ones[:], more[:], start=True, stop=True).then_inc(total_done, 1)
            pe.wait_ge(ones_ready, 1)
            pe.wait_ge(ws_ready, 1)
            pe.wait_ge(mid_ready, NC * AHEAD)
            for s in range(NB * NG):
                if s >= AHEAD:
                    pe.wait_ge(mid_ready, NC * s + NC)
                down(s)
                if s + AHEAD < NB * NG:
                    for c in range(NC):
                        up(s + AHEAD, c)

        @block.scalar
        def _(act):
            def row(b, first):
                for g in range(NG):
                    for c in range(NC):
                        act.wait_ge(up_done, NC * (b * NG + g) + c + 1)
                        m = P if c < NC - 1 else LAST
                        act.activation(mid[0:m, bass.ds(first + g, 1), c].squeeze(1), psU[0:m, c], ACT.Silu,
                                       bias=bu[0:m, g, c:c + 1]).then_inc(mid_ready, 1)

            with act.Fori(0, AHEAD // NG) as b:
                row(b, b * NG)
            with act.Fori(0, NB - AHEAD // NG) as b:
                row(b + AHEAD // NG, b * NG)

        @block.vector
        def _(dve):
            c = Chain(dve, chain)
            dve.wait_ge(turned, 1)
            dve.tensor_copy(pT[:].rearrange("p h k -> p (h k)"), psP[:, 0:2 * P]).then_inc(turned_out, 1)
            dve.wait_ge(turned_out, 1)
            three = cand[:]
            rounds = 0

            def take_best():
                nonlocal rounds
                for h in range(2):
                    for k in range(3):
                        ins = dve.tensor_scalar(found[:, h, k], pT[:, h], cand[:, h, k:k + 1], 0.0, ALU.is_ge, ALU.add,
                                                accum_out=cnt[:, h, k:k + 1])
                ins.then_inc(part_ready, 1)
                rounds += 1
                dve.wait_ge(total_done, rounds)
                totals = psN[:, 0:6].rearrange("p (h k) -> p h k", h=2)
                c.link(dve.scalar_tensor_tensor(three, totals, K - 0.5, three, ALU.is_ge, ALU.mult))
                c.link(dve.tensor_reduce(best[:], three, AX.X, ALU.max))
                c.link(dve.tensor_tensor(v[:], v[:], best[:], ALU.max))

            c.then(dve.memset(cand[:, :, 0], LEAST))
            c.then(dve.memset(cand[:, :, 1:3], LEAST * 2.0 ** 64))
            c.link(dve.memset(v[:], 0.0))
            take_best()
            for factors in EXPONENT:
                for k, m in enumerate(factors):
                    ins = dve.tensor_scalar(cand[:, :, k], v[:], m, None, ALU.mult)
                c.link(ins)
                take_best()
            for k in range(3):
                ins = dve.tensor_scalar(step[:, :, k], v[:], 0.5, None, ALU.mult)
            c.link(ins)
            c.link(dve.tensor_tensor(three, step[:], bcast(v[:], 2, 3), ALU.add))
            for k in range(3):
                ins = dve.tensor_scalar(step[:, :, k], step[:, :, k], (k + 1) / 4, None, ALU.mult)
            c.then(ins)
            take_best()
            for _ in range(PAIRS_OF_BITS):
                c.link(dve.tensor_tensor(three, step[:], bcast(v[:], 2, 3), ALU.add))
                c.then(dve.tensor_scalar(step[:], step[:], 0.25, None, ALU.mult))
                take_best()
            assert rounds == ROUNDS
            for h in range(2):
                ins = dve.tensor_scalar(vrow[:, h], first[:], v[:, h:h + 1], None, ALU.mult)
            ins.then_inc(v_done, 1)
            dve.wait_ge(total_done, ROUNDS + 1)
            c.link(dve.tensor_copy(vall[:], psV[:, 0:E]))
            dve.tensor_tensor(eq[:], prob[:], bcast(vall[:], 2, NT), ALU.is_equal).then_inc(eq_ready, 1)
            c.link(dve.tensor_tensor(hit[:], prob[:], bcast(vall[:], 2, NT), ALU.is_gt))
            dve.tensor_reduce(more[:], hit[:], AX.X, ALU.add).then_inc(eq_ready, 1)
            dve.wait_ge(total_done, ROUNDS + 2)
            c.link(dve.tensor_scalar(need[:], psN[:, 0:E], -1.0, float(K), ALU.mult, ALU.add))
            c.link(dve.tensor_copy(pre[:, 0], psE[:, 1]))
            a, s = 0, 1
            while s < NT:
                c.then(dve.tensor_tensor(pre[:, 1 - a, :, s:], pre[:, a, :, s:], pre[:, a, :, :NT - s], ALU.add))
                c.link(dve.tensor_copy(pre[:, 1 - a, :, :s], pre[:, a, :, :s]))
                a, s = 1 - a, 2 * s
            c.link(dve.tensor_tensor(pre[:, a], pre[:, a], psE[:, 1], ALU.subtract))
            c.link(dve.tensor_tensor(pre[:, a], pre[:, a], psE[:, 0], ALU.add))
            c.link(dve.tensor_tensor(pre[:, a], pre[:, a], bcast(need[:], 2, NT), ALU.is_le))
            c.link(dve.tensor_tensor(pre[:, a], pre[:, a], eq[:], ALU.mult))
            c.link(dve.tensor_tensor(hit[:], hit[:], pre[:, a], ALU.add))
            dve.tensor_tensor(ws[:], hit[:], prob[:], ALU.mult).then_inc(ws_ready, 1)
            dve.wait_ge(ws_ready, 1)
            with dve.Fori(0, NB) as b:
                c = Chain(dve, sum_chain, b, NG)
                for g in range(NG):
                    dve.wait_ge(down_done, b * NG + g + 1)
                    for k in range(2):
                        for i in range(NI):
                            w = ws[:, 2 * g + k, bass.ds(b * NI + i, 1)]
                            out = psO[:, g % 2, i, k * D:(k + 1) * D]
                            if g == k == 0:
                                ins = dve.tensor_scalar(y[:, i], out, w, None, ALU.mult)
                            else:
                                ins = dve.scalar_tensor_tensor(y[:, i], out, w, y[:, i], ALU.mult, ALU.add)
                        if k == 0:
                            c.link(ins)
                        else:
                            ins.then_inc(used, 1)
                            dve.wait_ge(used, b * NG + g + 1)
                c.end()
                ac = Chain(dve, added, b, ADD_STEPS)
                add_and_stats(S, dve, ac, b, 1, y[:])
                ac.end()


def moe_stage(S, l):
    nc = S.nc
    gated = l == 3
    E = 16 if gated else 8
    NC = 9 if gated else 32
    PER = 1 if gated else 4
    SCALED = 8 if gated else 32
    NH = 3 if gated else 4
    NU = 2
    SLOT = dict(y=3, z=4, logits=5, c=8) if gated else dict(y=3, z=5, logits=7, c=15, c2=17)
    ROUTE = (5, 5, 6, 6, 7, 7) if gated else (7, 8, 9, 10, 11, 12)
    FINISH = () if gated else (3, 18, 19, 20, 21, 22, 23, 24, 25, 26)
    n = f"L{l}f_"
    sem = lambda s: S.sem(n + s)
    loaded = [sem(f"loaded{p}") for p in range(1 if gated else 8)]
    (bias_loaded, chain, z_ready, zT_done, hT_ready, logits_done, logits_read, pair_ready, pair_exp,
     c_ready, cT_done, cT_ready, cb_done, up_done, g_ready, h_ready, down_done, yS_ready, yT_done, y_read,
     c2_done, c2_ready, hstep) = map(sem, (
         "bias_loaded", "dve", "z", "zT", "hT", "logits", "logits_read", "pair", "pair_exp",
         "c", "cT", "cTs", "cb", "up", "g", "h", "down", "yS", "yT", "y_read", "c2", "c2s", "hstep"))

    def dist(k, bufs):
        return bufs if k >= bufs else k + NC - max(j for j in range(NC) if j % bufs == k % bufs)

    with ExitStack() as ctx:
        sb = lambda name, shape, dt=F32: ctx.enter_context(nc.sbuf_tensor(n + name, shape, dt))
        pt = lambda name, shape, dt=F32: ctx.enter_context(nc.psum_tensor(n + name, shape, dt))
        wu = sb("wu", [P, 2 if gated else 1, NC, P])
        wd = sb("wd", [P, NC, D])
        wr = sb("wr", [P, E])
        rb = sb("rb", [P, E])
        iota = sb("iota", [P, E])
        sel = sb("sel", [3 * E, SCALED // PER, P], BF16)
        z = sb("z", [P, NI, D])
        hT = sb("hT", [P, 2, T])
        logit = sb("logit", [P, NI, E])
        top = sb("top", [P, NI, 8])
        idx = sb("idx", [P, NI, 8], U32)
        idxf = sb("idxf", [P, NI, 2])
        pair = sb("pair", [P, NI, 2])
        den = sb("den", [P, NI])
        hot = sb("hot", [P, 2, NI, E])
        cw = sb("cw", [P, NI, E])
        crest = sb("crest", [P, NI, E])
        c3 = sb("c3", [P, NI, 3, E], BF16)
        c3T = sb("c3T", [3 * E, 2, T], BF16)
        g = sb("g", [P, 3, T])
        h = sb("h", [P, NH, T])
        yS = sb("yS", [P, T])
        psU = pt("psU", [P, NU, T])
        psG = pt("psG", [P, NU, T]) if gated else None
        psC = pt("psC", [P, 2, T])
        psY = pt("psY", [P, T])
        misc = pt("misc", [P, T])
        if not gated:
            b1 = sb("b1", [P, NC])
            b2 = sb("b2", [E, D])
            cT = sb("cT", [E, 2, T])
            lnp = sb("lnp", [P, 2, D])
            y = sb("y", [P, NI, D])
            ymv = sb("ymv", [P, NI, 2])
            yr = sb("yr", [P, 3, NI])
        block = ctx.enter_context(nc.Block())

        USES = [("y", 2, y_read), ("z", 0, hT_ready), ("logits", 0, logits_read), ("c", 0, cT_ready)]
        if not gated:
            USES.append(("c2", 0, c2_ready))
        LOOP0 = 2
        live = lambda t, lag: 0 <= t - lag < NB

        class Turn:

            def __init__(self, t, parity, steady):
                self.t, self.par, self.steady = t, parity, steady
                self.A, self.C, self.D = (steady or live(t, lag) for lag in range(3))

            def runs(self, back, lag):
                return self.steady or live(self.t - back, lag)

            def misc_copied_out(self, eng, at):
                for back in (0, 1):
                    for _, lag, sem_ in reversed(USES[:at] if back == 0 else USES):
                        if self.runs(back, lag):
                            eng.wait_ge(sem_, self.t - back - lag + 1)
                            return

        def turns(eng, body):
            for t in range(LOOP0):
                body(Turn(t, t % 2, False))
            with eng.Fori(LOOP0 // 2, NB // 2) as two:
                for u in range(2):
                    body(Turn(two * 2 + u, u, True))
            for t in range(NB, NB + 2):
                body(Turn(t, t % 2, False))

        @block.sync
        def _(sp):
            for dst, src in ((wr[:], n + "wr"), (rb[:], n + "rb"), (iota[:], n + "iota"), (sel[:], n + "sel")):
                s = S.dram[src]
                sp.dma_start(dst, s.partition_broadcast(P) if src == n + "rb" else s).then_inc(bias_loaded, 16)
            if not gated:
                sp.dma_start(b1[:], S.dram[n + "b1"]).then_inc(bias_loaded, 16)
                sp.dma_start(b2[:], S.dram[n + "b2"]).then_inc(bias_loaded, 16)
                sp.dma_start(lnp[:], S.dram[n + "lnp"].partition_broadcast(P)).then_inc(bias_loaded, 16)
            for p, sem_ in enumerate(loaded):
                ks = slice(p * NC // len(loaded), (p + 1) * NC // len(loaded))
                sp.dma_start(wu[:, :, ks], S.dram[n + "wu"][:, :, ks]).then_inc(sem_, 16)
                sp.dma_start(wd[:, ks], S.dram[n + "wd"][:, ks]).then_inc(sem_, 16)
        SMALL = 4 * 16 if gated else 7 * 16

        @block.tensor
        def _(pe):
            pe.wait_ge(bias_loaded, SMALL)

            def weights_to_all(row, rpar, x):
                if x == 0:
                    pe.wait_ge(cT_ready, row + 1)
                last = PER * (x - 2) + PER
                if x >= 2:
                    pe.wait_ge(h_ready, NC * row + last)
                else:
                    pe.wait_ge(h_ready, NC * row)
                pe.matmul(psC[:, x % 2], sel[:, x], c3T[:, rpar], start=True, stop=True).then_inc(cb_done, 1)

            def up(row, rpar, k):
                d = dist(k, NU)
                sem_ = h_ready if gated else g_ready
                if not (isinstance(row, int) and NC * row + k - d + 1 < 0):
                    pe.wait_ge(sem_, NC * row + k - d + 1)
                if gated:
                    pe.matmul(psG[:, k % NU], wu[:, 0, k], hT[:, rpar], start=True, stop=True)
                pe.matmul(psU[:, k % NU], wu[:, 1 if gated else 0, k], hT[:, rpar], start=True, stop=True).then_inc(up_done, 1)

            def down(row, rpar, k):
                if k == 0:
                    pe.wait_ge(yS_ready, row)
                    if not gated:
                        pe.wait_ge(c2_ready, row + 1)
                        pe.matmul(psY[:], b2[:], cT[:, rpar], start=True, stop=False, skip_group_check=True)
                pe.wait_ge(h_ready, NC * row + k + 1)
                pe.matmul(psY[:], wd[:, k], h[:, k % NH], start=(gated and k == 0), stop=(k == NC - 1),
                          skip_group_check=True).then_inc(down_done, 1)

            def use(u, at):
                name, lag, _ = USES[at]
                if not u.runs(0, lag):
                    return
                u.misc_copied_out(pe, at)
                row = u.t - lag
                if name == "y":
                    pe.wait_ge(yS_ready, row + 1)
                    for i in range(NI):
                        ins = pe.transpose(misc[:, i * P:(i + 1) * P], yS[:, i * P:(i + 1) * P], S.ident[:])
                    ins.then_inc(yT_done, 1)
                elif name == "z":
                    pe.wait_ge(z_ready, row + 1)
                    for i in range(NI):
                        ins = pe.transpose(misc[:, i * P:(i + 1) * P], z[:, i], S.ident[:])
                    ins.then_inc(zT_done, 1)
                elif name == "logits":
                    pe.wait_ge(hT_ready, row + 1)
                    for i in range(NI):
                        ins = pe.matmul(misc[:, i * E:(i + 1) * E], hT[:, u.par, i * P:(i + 1) * P], wr[:],
                                        start=True, stop=True)
                    ins.then_inc(logits_done, 1)
                elif name == "c":
                    wait_alone(pe, c_ready, row + 1)
                    for i in range(NI):
                        ins = pe.transpose(misc[0:3 * E, i * 64:(i + 1) * 64].bitcast(BF16),
                                           c3[:, i].rearrange("p a e -> p (a e)"), S.identb[:])
                    ins.then_inc(cT_done, 1)
                else:
                    for i in range(NI):
                        ins = pe.transpose(misc[0:E, i * P:(i + 1) * P], cw[:, i], S.ident[:])
                    ins.then_inc(c2_done, 1)

            def turn(u):
                for k in range(NC):
                    if k < 2 and u.D:
                        down(u.t - 2, u.par, NC - 2 + k)
                    if u.C:
                        for p in range(len(loaded)):
                            if not u.steady and u.t == 1 and k == p * NC // len(loaded):
                                pe.wait_ge(loaded[p], 32)
                        if k % PER == 0 and k < SCALED:
                            weights_to_all(u.t - 1, 1 - u.par, k // PER)
                        up(u.t - 1, 1 - u.par, k)
                        if k >= 2:
                            down(u.t - 1, 1 - u.par, k - 2)
                    for at, (name, _, _) in enumerate(USES):
                        if SLOT[name] == k:
                            use(u, at)

            turns(pe, turn)

        @block.scalar
        def _(act):
            def turn(u):
                t = u.t
                for k in range(NC):
                    if u.C:
                        G = NC * (t - 1) + k
                        act.wait_ge(up_done, G + 1)
                        if u.D or k >= 3:
                            act.wait_ge(h_ready, G - dist(k, 3) + 1)
                        if gated:
                            act.activation(g[:, k % 3], psG[:, k % NU], ACT.Silu).then_inc(g_ready, 1)
                        else:
                            act.activation(g[:, k % 3], psU[:, k % NU], ACT.Gelu, bias=b1[:, k:k + 1]).then_inc(g_ready, 1)
                    if k == 2 and u.D and gated:
                        act.wait_ge(down_done, NC * (t - 1))
                        act.activation(yS[:], psY[:], ACT.Copy).then_inc(yS_ready, 1)
                    if not u.A:
                        continue
                    if k == SLOT["z"]:
                        act.wait_ge(zT_done, t + 1)
                        if u.D:
                            act.wait_ge(up_done, NC * (t - 1))
                            act.wait_ge(yS_ready, t - 1)
                        act.activation(hT[:, u.par], misc[:], ACT.Identity, bias=S.modT[:, 3, bass.ds(t, 1)],
                                       scale=S.modT[:, 4, bass.ds(t, 1)]).then_inc(hT_ready, 1)
                    if k == SLOT["logits"] + 1:
                        act.wait_ge(pair_ready, t + 1)
                        act.activation(pair[:, :, 1], pair[:, :, 1], ACT.Exp).then_inc(pair_exp, 1)
                    if k == SLOT["c"]:
                        act.wait_ge(cT_done, t + 1)
                        if u.D:
                            act.wait_ge(cb_done, SCALED // PER * (t - 1))
                        act.activation(c3T[:, u.par], misc[0:3 * E, 0:256].bitcast(BF16), ACT.Copy).then_inc(cT_ready, 1)
                    if not gated and k == SLOT["c2"]:
                        act.wait_ge(c2_done, t + 1)
                        if u.D:
                            act.wait_ge(down_done, NC * (t - 2) + 1)
                        act.activation(cT[:, u.par], misc[0:E], ACT.Copy).then_inc(c2_ready, 1)

            turns(act, turn)

        @block.vector
        def _(dve):
            c = Chain(dve, chain)
            rstd_step(S, dve, c)
            n0 = c.n
            A_STEPS = 13
            D_STEPS = ADD_STEPS - 1 if gated else ADD_STEPS + RSQRT_STEPS + 6

            def finish(u, c, piece):
                row = u.t - 2
                if piece == 0:
                    dve.wait_ge(yT_done, row + 1)
                    dve.tensor_copy(y[:], misc[:].rearrange("p (i f) -> p i f", i=NI)).then_inc(y_read, 1)
                    wait_alone(dve, y_read, row + 1)
                elif piece == 1:
                    for i in range(NI):
                        ins = dve.bn_stats(S.bn[:, 1, i], y[:, i])
                    c.link(ins, alone=True)
                elif piece == 2:
                    for i in range(NI):
                        ins = dve.bn_aggr(ymv[:, i], S.bn[:, 1, i])
                    c.link(ins)
                    c.link(dve.tensor_copy(yr[:, 0], ymv[:, :, 1]))
                    rsqrt_guess(dve, c, yr[:, 1], yr[:, 0], 1.0, LN_EPS)
                elif piece <= 5:
                    rsqrt_newton(dve, c, yr[:, 1], yr[:, 0], yr[:, 2])
                elif piece == 6:
                    for i in range(NI):
                        ins = dve.tensor_scalar(y[:, i], y[:, i], ymv[:, i, 0:1], yr[:, 1, i:i + 1],
                                                ALU.subtract, ALU.mult)
                    c.link(ins)
                elif piece == 7:
                    c.link(dve.tensor_tensor(y[:], y[:], bcast(lnp[:, 0], 1, NI), ALU.mult))
                elif piece == 8:
                    c.link(dve.tensor_tensor(y[:], y[:], bcast(lnp[:, 1], 1, NI), ALU.add))
                else:
                    add_and_stats(S, dve, c, row, 1, y[:])

            def route(u, c, piece):
                t = u.t
                former = u.steady or t > 0
                if piece == 0:
                    if not former:
                        dve.wait_ge(bias_loaded, SMALL)
                    dve.wait_ge(logits_done, t + 1)
                    if former:
                        dve.wait_ge(c_ready, t)
                    dve.tensor_tensor(logit[:], misc[:, 0:NI * E].rearrange("p (i e) -> p i e", i=NI),
                                      bcast(rb[:], 1, NI), ALU.add).then_inc(logits_read, 1)
                    wait_alone(dve, logits_read, t + 1)
                    for i in range(NI):
                        ins = dve.max(top[:, i], logit[:, i])
                    c.link(ins, alone=True)
                elif piece == 1:
                    for i in range(NI):
                        ins = dve.max_index(idx[:, i], top[:, i], logit[:, i])
                    c.link(ins)
                    dve.tensor_tensor(pair[:, :, 1], top[:, :, 1], top[:, :, 0], ALU.subtract).then_inc(pair_ready, 1)
                elif piece == 2:
                    c.link(dve.tensor_copy(idxf[:], idx[:, :, 0:2]))
                    for a in range(2):
                        ins = dve.tensor_tensor(hot[:, a], bcast(iota[:], 1, NI), bcast(idxf[:, :, a], 2, E),
                                                ALU.is_equal)
                    c.link(ins)
                elif piece == 3:
                    dve.wait_ge(pair_exp, t + 1)
                    c.link(dve.tensor_scalar(den[:], pair[:, :, 1], 1.0, None, ALU.add))
                    c.link(dve.reciprocal(pair[:, :, 0], den[:]))
                    c.link(dve.tensor_tensor(pair[:, :, 1], pair[:, :, 1], pair[:, :, 0], ALU.mult))
                elif piece == 4:
                    if former:
                        dve.wait_ge(cT_done if gated else c2_done, t)
                    for a in range(2):
                        ins = dve.tensor_tensor(hot[:, a], hot[:, a], bcast(pair[:, :, a], 2, E), ALU.mult)
                    c.link(ins)
                    c.link(dve.tensor_tensor(cw[:], hot[:, 0], hot[:, 1], ALU.add))
                    c.link(dve.tensor_copy(c3[:, :, 0], cw[:]))
                else:
                    c.link(dve.tensor_tensor(crest[:], cw[:], c3[:, :, 0], ALU.subtract))
                    c.link(dve.tensor_copy(c3[:, :, 1], crest[:]))
                    c.link(dve.tensor_tensor(crest[:], crest[:], c3[:, :, 1], ALU.subtract))
                    dve.tensor_copy(c3[:, :, 2], crest[:]).then_inc(c_ready, 1)

            def turn(u):
                t = u.t
                c = Chain(dve, chain, 0, u.steady)
                c.base = n0 + (t * A_STEPS if u.A else NB * A_STEPS) + ((t - 2) * D_STEPS if u.D else 0)
                steps = (A_STEPS if u.A else 0) + (D_STEPS if u.D else 0)

                for k in range(NC):
                    if u.C:
                        G = NC * (t - 1) + k
                        dve.wait_ge(g_ready, G + 1)
                        if u.D or k >= NH:
                            dve.wait_ge(down_done, G - dist(k, NH) + 1)
                        hk = h[:, k % NH]
                        if gated:
                            ins = dve.tensor_tensor(hk, g[:, k % 3], psU[:, k % NU], ALU.mult)
                            if k < SCALED:
                                ins.then_inc(hstep, 1)
                                dve.wait_ge(hstep, SCALED * (t - 1) + k + 1)
                        if k < SCALED:
                            if k % PER == 0:
                                dve.wait_ge(cb_done, SCALED // PER * (t - 1) + k // PER + 1)
                            ins = dve.tensor_tensor(hk, hk if gated else g[:, k % 3], psC[:, k // PER % 2], ALU.mult)
                        ins.then_inc(h_ready, 1)
                    if k == 0 and u.A:
                        if u.steady or t > 0:
                            dve.wait_ge(zT_done, t)
                        normalise(S, dve, t, z).then_inc(z_ready, 1)
                    if k == 2 and u.D and not gated:
                        dve.wait_ge(down_done, NC * (t - 1))
                        dve.tensor_tensor(yS[:], psY[:], hT[:, u.par], ALU.add).then_inc(yS_ready, 1)
                    if u.A:
                        for piece, slot in enumerate(ROUTE):
                            if k == slot:
                                route(u, c, piece)
                    if u.D:
                        if gated and k == SLOT["y"]:
                            dve.wait_ge(yT_done, t - 1)
                            add_and_stats(S, dve, c, t - 2, 1, misc[:].rearrange("p (i f) -> p i f", i=NI), y_read)
                        for piece, slot in enumerate(FINISH):
                            if k == slot:
                                finish(u, c, piece)
                assert c.n == steps, (c.n, steps)

            turns(dve, turn)


def store_stage(S):
    nc = S.nc
    stored = nc.alloc_semaphore("stored")
    with nc.Block() as block:
        @block.sync
        def _(sp):
            for b in range(NB):
                sp.dma_start(S.dram["out"][b].rearrange("(i p) f -> p i f", p=P), S.x[:, b * NI:(b + 1) * NI]).then_inc(stored, 16)
            sp.wait_ge(stored, NB * 16)


def run_stage(S, stage, *args):
    nc = S.nc
    S.sems = []
    stage(S, *args)
    nc.clear_and_free_semaphores(S.sems)
    nc.all_engine_barrier()


def program(nc, dram, stages):
    S = State()
    S.nc, S.dram = nc, dram
    for eng in (nc.vector, nc.gpsimd, nc.tensor, nc.sync):
        State.passed[eng.engine] = nc.alloc_semaphore(f"waits_passed_{eng.engine.name}")
    al = nc.alloc_sbuf_tensor
    S.x = al("x", [P, NT, D], F32)
    S.ident = al("ident", [P, P], F32)
    S.identb = al("identb", [P, P], BF16)
    S.ones = al("ones", [P, P], F32)
    S.bn = al("bn", [P, NB, NI, 6], F32)
    S.mv = al("mv", [P, NT, 2], F32)
    S.mv4 = al("mv4", [P, NI, 2], F32)
    S.var = al("var", [P, NT], F32)
    S.rstd = al("rstd", [P, NT], F32)
    S.nwt = al("nwt", [P, NT], F32)
    S.modTs = al("modT", [P, 4, 6, NB], F32)
    S.gate = al("gate", [P, 2, NB, D], F32)
    S.upd = al("upd", [P, NI, D], F32)
    S.gatesT = al("gatesT", [4 * 2 * NB, D], F32)
    S.gates_dram = nc.dram_tensor("gates_dram", (4, 2, NB, D), F32, kind="Internal").ap()
    S.gates_stored, S.gates_loaded = nc.alloc_semaphore("gates_stored"), nc.alloc_semaphore("gates_loaded")
    S.gate_loads = 0
    run_stage(S, setup_stage)
    parts = [l0_attn_stage, token_choice_stage, gqa_attn_stage, expert_choice_stage, lambda S: head_attn_stage(S, 2),
             lambda S: moe_stage(S, 2), lambda S: head_attn_stage(S, 3), lambda S: moe_stage(S, 3)]
    for k, part in enumerate(parts):
        if k in stages:
            if k % 2 == 0 or k == stages[0]:
                S.modT = S.modTs[:, k // 2]
            run_stage(S, part)
    store_stage(S)


def swap_pairs(w):
    return w.reshape(w.shape[0], -1, 2)[:, :, ::-1].reshape(w.shape)


def layouts(i):
    bf16 = np.dtype("bfloat16")
    f32 = np.float32
    out = {"x": i["L0_attn_x"], "ident": np.eye(P, dtype=f32), "identb": np.eye(P, dtype=bf16)}
    for l in range(4):
        out[f"L{l}_wmod"] = i[f"L{l}_wmod"]
        out[f"L{l}_cT"] = i[f"L{l}_c"].T
    q, k, v, o = (i["L0_attn_W" + c] for c in "qkvo")
    out["L0a_w"] = np.stack([q, swap_pairs(q), k, swap_pairs(k), v, o], 1)
    inv = (1.0 / 10000.0 ** (np.arange(0, 8, 2, dtype=f32) / f32(8))).astype(f32)
    fr = np.repeat(np.arange(T, dtype=f32)[:, None] * inv[None], 2, 1)
    sign = np.tile(np.array([-1, 1], f32), 4)
    cs = np.stack([np.tile(np.cos(fr), (1, 16)), np.tile(np.sin(fr) * sign, (1, 16))], 1)
    out["L0a_rope"] = cs.reshape(NI, P, 2, D).transpose(1, 0, 2, 3)
    out["L0a_lam"] = np.stack([i["L0_attn_lambda_" + c] for c in ("q1", "k1", "q2", "k2")])
    out["L0a_ln"] = np.stack([i["L0_attn_ln_w"], i["L0_attn_ln_b"]], 1)
    in_pos = lambda w: np.concatenate([np.zeros_like(w), w], 0)
    out["L1a_wq"] = in_pos(i["L1_attn_Wq"].T).reshape(P, 16, 32, 2)
    out["L1a_wk"] = np.repeat(in_pos(i["L1_attn_Wk"].T).reshape(P, 4, 1, 64), 2, 2)
    out["L1a_wv"] = np.concatenate([i["L1_attn_Wv"].T, np.zeros((64, 256), f32)], 0)
    out["L1a_wo"] = i["L1_attn_Wo"].T.reshape(8, P, D).transpose(1, 0, 2)
    out["L1a_angle"] = i["L1_attn_q_phase_angle"]
    out["L1a_slopes"] = i["L1_attn_alibi_log_slopes"]
    out["cneg"] = np.tile(-np.arange(T, dtype=f32), (P, 1))
    def part_rows(E, sets, experts):
        s = np.zeros((3, E, sets, P), bf16)
        for x in range(sets):
            for j in range(experts):
                s[:, x * experts + j, x, j * P // experts:(j + 1) * P // experts] = 1
        return s.reshape(3 * E, sets, P)
    out["iota"] = np.tile(np.arange(16, dtype=f32), (P, 1))
    out["L2f_iota"] = out["iota"][:, :8]
    out["L3f_iota"] = out.pop("iota")
    out["L2f_wu"] = i["L2_ffn_W1"].transpose(1, 0, 2).reshape(P, 1, 32, P)
    out["L2f_wd"] = i["L2_ffn_W2"].reshape(32, P, D).transpose(1, 0, 2)
    out["L2f_wr"] = i["L2_ffn_Wg"]
    out["L2f_rb"] = i["L2_ffn_bg"]
    out["L2f_sel"] = part_rows(8, 8, 1)
    out["L2f_b1"] = i["L2_ffn_b1"].reshape(32, P).T
    out["L2f_b2"] = i["L2_ffn_b2"]
    out["L2f_lnp"] = np.stack([i["L2_ffn_gamma"], i["L2_ffn_beta"]])
    two = lambda w: w.transpose(1, 0, 2).reshape(P, 8, P)
    gate = np.concatenate([two(i["L3_ffn_gate_proj"]), i["L3_ffn_sh_gate"].T[:, None]], 1)
    up = np.concatenate([two(i["L3_ffn_up_proj"]), i["L3_ffn_sh_up"].T[:, None]], 1)
    out["L3f_wu"] = np.stack([gate, up], 1)
    out["L3f_wd"] = np.concatenate([i["L3_ffn_down_proj"].reshape(8, P, D).transpose(1, 0, 2),
                                    i["L3_ffn_sh_down"].T[:, None]], 1)
    out["L3f_wr"] = i["L3_ffn_router_w"].T
    out["L3f_rb"] = i["L3_ffn_router_bias"]
    out["L3f_sel"] = part_rows(16, 8, 2)
    out["L0f_wr"] = i["L0_ffn_Wr"].T
    q, k, v = np.split(i["L0_ffn_Wqkv"].transpose(1, 0, 2), 3, axis=2)
    half_swapped = lambda w: np.concatenate([w[..., 32:64], w[..., :32]], -1)
    out["L0f_wq"], out["L0f_wk"], out["L0f_wv"] = q, k, v
    out["L0f_ws"] = np.concatenate([half_swapped(q), half_swapped(k)], -1)
    out["L0f_wo"] = i["L0_ffn_Wo"].transpose(1, 0, 2)
    inv = (1.0 / f32(10000.0) ** (np.arange(32, dtype=f32) * f32(2.0) / f32(64))).astype(f32)
    ang = np.arange(T, dtype=f32)[:, None] * inv
    sin, cos = np.sin(ang), np.cos(ang)
    rest = np.concatenate([cos, cos, -sin, sin], 1)
    parts = []
    for _ in range(3):
        parts.append(rest.astype(bf16))
        rest = rest - parts[-1].astype(f32)
    out["L0f_tables"] = np.stack(parts, 1).reshape(NI, P, 3, P).transpose(1, 0, 2, 3)
    out["L0f_iota"] = np.tile(np.arange(64, dtype=f32), (P, 1))
    same = np.kron(np.eye(2), np.tril(np.ones((64, 64)))) > 0
    out["L0f_causal"] = np.where(same, 0, NEG).astype(f32)
    own = np.zeros((2, 64, 4, 3, 8), f32)
    for p in range(4):
        for h in range(2):
            own[h, :, p, :, 2 * p + h] = 1
    out["L0f_own"] = own.reshape(P, 4, 3, 8)
    up = i["L1_ffn_W_up"]
    F = up.shape[2]
    out["L1f_wu"] = np.pad(up, ((0, 0), (0, 0), (0, 3 * P - F))).transpose(1, 0, 2)
    down = np.zeros((8, 3 * P, D), f32)
    down[:, :F] = i["L1_ffn_W_down"]
    down[:, 2 * P + 96] = i["L1_ffn_b_down"]
    out["L1f_wd"] = down.reshape(4, 2, 3, P, D).transpose(3, 0, 2, 1, 4).reshape(P, 4, 3, 2 * D)
    out["L1f_bu"] = np.pad(i["L1_ffn_b_up"], ((0, 0), (0, 3 * P - F))).reshape(4, 3, P).transpose(2, 0, 1)
    out["L1f_wr"] = i["L1_ffn_Wr"]
    out["L1f_br"] = i["L1_ffn_br"]
    out["blocks"] = np.kron(np.eye(4, dtype=f32), np.ones((32, 32), f32))
    out["first"] = np.kron(np.eye(4, dtype=f32), np.eye(32, dtype=f32)[:, :1])
    out["tri"] = np.triu(np.ones((P, P), f32))
    past = np.arange(P)[:, None] >= np.arange(P)[None]
    out["mask"] = np.where(np.concatenate([np.ones((P, 3 * P), bool), past], 1), 0, NEG).astype(f32)
    out["maskT"] = np.where(past.T, 0, NEG).astype(bf16)
    d_major = lambda w: w.reshape(w.shape[:-1] + (16, 8)).swapaxes(-1, -2).reshape(w.shape)
    q, k, v, o = (i["L2_attn_W" + c] for c in "qkvm")
    bq, bk, bv, bo = (i["L2_attn_b" + c] for c in "qkvm")
    out["L2a_w"] = np.stack([d_major(q), d_major(k), v, o], 1)
    out["L2a_qkb"] = np.stack([d_major(bq), d_major(bk)], 1)
    out["L2a_vob"] = np.stack([bv, bo])
    (q, k, v), (bq, bk, bv) = i["L3_attn_c_attn_kernel"].T.reshape(D, 3, D).swapaxes(0, 1), i["L3_attn_c_attn_bias"].reshape(3, D)
    out["L3a_w"] = np.stack([d_major(q), d_major(k), v, i["L3_attn_c_proj_kernel"].T], 1)
    out["L3a_qkb"] = np.stack([d_major(bq), d_major(bk)], 1)
    out["L3a_vob"] = np.stack([bv, i["L3_attn_c_proj_bias"]])
    return {k: np.ascontiguousarray(v) for k, v in out.items()}


def build(nc, arrays, stages=tuple(range(8))):
    dram = {k: nc.dram_tensor("in_" + k, v.shape, mybir.dt.from_np(v.dtype), kind="ExternalInput").ap()
            for k, v in arrays.items()}
    dram["out"] = nc.dram_tensor("out_0", (NB, T, D), F32, kind="ExternalOutput").ap()
    program(nc, dram, stages)


def kernel(**inputs):
    import concourse.bacc as bacc
    from concourse.bass_utils import run_bass_kernel_spmd

    nc = bacc.Bacc("TRN2", target_bir_lowering=False, num_devices=1)
    arrays = layouts({k: np.asarray(v) for k, v in inputs.items()})
    build(nc, arrays)
    launch = run_bass_kernel_spmd(nc, [{"in_" + k: v for k, v in arrays.items()}], core_ids=[0])
    return launch.results[0]["out_0"]
```
